# Optimizing a Trainium2 kernel written in Bass

```python
import numpy as np
import jax
import jax.numpy as jnp

def _softmax(x, axis=-1):
    return jax.nn.softmax(x, axis=axis)

def _gelu(x):
    return jax.nn.gelu(x, approximate=True)

def _silu(x):
    return jax.nn.silu(x)

def _sigmoid(x):
    return jax.nn.sigmoid(x)

def _layernorm(x, axis=-1, eps=1e-05):
    m = jnp.mean(x, axis=axis, keepdims=True)
    v = jnp.var(x, axis=axis, keepdims=True)
    return (x - m) / jnp.sqrt(v + eps)

def _scatter_add(tgt, idx, src, axis=0):
    return tgt.at[idx].add(src)

def _segment_sum(src, seg, n):
    return jax.ops.segment_sum(src, seg, n)
kernel_name = 'mk_macaron_d1_jaxref_r8_0c277a'

def setup_inputs(seed: int=0):
    np.random.seed(seed)
    _w = jnp.asarray

    def _L0_attn_setup():
        import jax, jax.numpy as jnp
        import numpy as np
        DIM_HEAD = 128
        HEADS = 16
        SCALE = DIM_HEAD ** (-0.5)

        def rotate_half(t):
            x1, x2 = jnp.split(t, 2, axis=-1)
            return jnp.concatenate((-x2, x1), axis=-1)

        def apply_rope(pos, t):
            return t * jnp.cos(pos) + rotate_half(t) * jnp.sin(pos)
        key = jax.random.key(seed)
        k0, k1, k2, k3 = jax.random.split(key, 4)
        b, n, dim = (2, 256, 256)
        inner = HEADS * DIM_HEAD
        return {'x': jax.random.normal(k0, (b, n, dim), jnp.float32), 'Wq': jax.random.normal(k1, (dim, inner), jnp.float32) * 0.02, 'Wkv': jax.random.normal(k2, (dim, 2 * DIM_HEAD), jnp.float32) * 0.02, 'Wout': jax.random.normal(k3, (inner, dim), jnp.float32) * 0.02}
    _L0_attn_in = _L0_attn_setup()

    def _L0_ffn_setup():
        import jax, jax.numpy as jnp
        import numpy as np
        B, S, H = (2, 256, 256)
        E, K, F = (32, 4, 176)
        FS = 704
        EPS = 1e-06
        CAP = 128
        key = jax.random.key(seed)
        ks = jax.random.split(key, 10)
        s = 0.02
        return {'hidden_states': jax.random.normal(ks[0], (B, S, H), jnp.float32), 'w_norm': 1.0 + 0.02 * jax.random.normal(ks[1], (H,), jnp.float32), 'w_router': s * jax.random.normal(ks[2], (H, E), jnp.float32), 'w_gate': s * jax.random.normal(ks[3], (E, H, F), jnp.float32), 'w_up': s * jax.random.normal(ks[4], (E, H, F), jnp.float32), 'w_down': s * jax.random.normal(ks[5], (E, F, H), jnp.float32), 'sw_gate': s * jax.random.normal(ks[6], (H, FS), jnp.float32), 'sw_up': s * jax.random.normal(ks[7], (H, FS), jnp.float32), 'sw_down': s * jax.random.normal(ks[8], (FS, H), jnp.float32), 'w_shared_gate': s * jax.random.normal(ks[9], (H, 1), jnp.float32)}
    _L0_ffn_in = _L0_ffn_setup()
    _d = {'L0_attn_x': _L0_attn_in['x'], 'L0_attn_Wq': _L0_attn_in['Wq'], 'L0_attn_Wkv': _L0_attn_in['Wkv'], 'L0_attn_Wout': _L0_attn_in['Wout'], 'L0_ffn_w_norm': _L0_ffn_in['w_norm'], 'L0_ffn_w_router': _L0_ffn_in['w_router'], 'L0_ffn_w_gate': _L0_ffn_in['w_gate'], 'L0_ffn_w_up': _L0_ffn_in['w_up'], 'L0_ffn_w_down': _L0_ffn_in['w_down'], 'L0_ffn_sw_gate': _L0_ffn_in['sw_gate'], 'L0_ffn_sw_up': _L0_ffn_in['sw_up'], 'L0_ffn_sw_down': _L0_ffn_in['sw_down'], 'L0_ffn_w_shared_gate': _L0_ffn_in['w_shared_gate']}
    _x0 = _d['L0_attn_x']
    _d['L0_attn_x'] = jax.random.normal(jax.random.fold_in(jax.random.key(seed), 1), (2, 1024, 256), dtype=_x0.dtype)
    del _x0
    return _d

def reference(L0_attn_x, L0_attn_Wq, L0_attn_Wkv, L0_attn_Wout, L0_ffn_w_norm, L0_ffn_w_router, L0_ffn_w_gate, L0_ffn_w_up, L0_ffn_w_down, L0_ffn_sw_gate, L0_ffn_sw_up, L0_ffn_sw_down, L0_ffn_w_shared_gate):

    def _L0_attn_ref(x, Wq, Wkv, Wout):
        import jax, jax.numpy as jnp
        import numpy as np
        DIM_HEAD = 128
        HEADS = 16
        SCALE = DIM_HEAD ** (-0.5)

        def rotate_half(t):
            x1, x2 = jnp.split(t, 2, axis=-1)
            return jnp.concatenate((-x2, x1), axis=-1)

        def apply_rope(pos, t):
            return t * jnp.cos(pos) + rotate_half(t) * jnp.sin(pos)
        b, n, dim = x.shape
        q = x @ Wq
        kv = x @ Wkv
        k, v = jnp.split(kv, 2, axis=-1)
        q = q.reshape(b, n, HEADS, DIM_HEAD).transpose(0, 2, 1, 3)
        inv_freq = 1.0 / 10000.0 ** (jnp.arange(0, DIM_HEAD, 2, dtype=jnp.float32) / DIM_HEAD)
        freqs = jnp.arange(n, dtype=jnp.float32)[:, None] * inv_freq[None, :]
        pos = jnp.concatenate((freqs, freqs), axis=-1)
        q = apply_rope(pos, q) * SCALE
        k = apply_rope(pos, k)
        sim = jnp.einsum('bhid,bjd->bhij', q, k)
        causal_mask = jnp.triu(jnp.ones((n, n), dtype=bool), 1)
        neg = -jnp.finfo(sim.dtype).max
        sim = jnp.where(causal_mask, neg, sim)
        sim = sim - jax.lax.stop_gradient(jnp.max(sim, axis=-1, keepdims=True))
        attn = jax.nn.softmax(sim, axis=-1)
        out = jnp.einsum('bhij,bjd->bhid', attn, v)
        out = out.transpose(0, 2, 1, 3).reshape(b, n, HEADS * DIM_HEAD)
        return out @ Wout

    def _L0_ffn_ref(hidden_states, w_norm, w_router, w_gate, w_up, w_down, sw_gate, sw_up, sw_down, w_shared_gate):
        import jax, jax.numpy as jnp
        import numpy as np
        B, S, H = (2, 256, 256)
        E, K, F = (32, 4, 176)
        FS = 704
        EPS = 1e-06
        CAP = 128
        inp = hidden_states
        xf = inp.astype(jnp.float32)
        var = jnp.mean(xf * xf, axis=-1, keepdims=True)
        x = (w_norm * (xf * jax.lax.rsqrt(var + EPS))).astype(inp.dtype)
        Bq, Sq, Hq = x.shape
        x = x.reshape(-1, Hq)
        T = Bq * Sq
        logits = x @ w_router
        probs = jax.nn.softmax(logits.astype(jnp.float32), axis=-1)
        w_topk, sel = jax.lax.top_k(probs, K)
        w_topk = w_topk.astype(x.dtype)
        flat_e = sel.reshape(-1)
        order = jnp.argsort(flat_e)
        sorted_e = flat_e[order]
        counts = jnp.zeros((E,), jnp.int32).at[flat_e].add(1)
        starts = jnp.cumsum(counts) - counts
        pos = jnp.arange(T * K) - starts[sorted_e]
        tok = order // K
        valid = pos < CAP
        dest = jnp.where(valid, pos, CAP)
        buf = jnp.zeros((E, CAP + 1, Hq), x.dtype).at[sorted_e, dest].set(x[tok])
        buf = buf[:, :CAP]
        g = jnp.einsum('ech,ehf->ecf', buf, w_gate)
        u = jnp.einsum('ech,ehf->ecf', buf, w_up)
        y = jnp.einsum('ecf,efh->ech', jax.nn.silu(g) * u, w_down)
        wv = w_topk.reshape(-1)[order] * valid.astype(x.dtype)
        gath = y[sorted_e, jnp.minimum(pos, CAP - 1)]
        out = jnp.zeros((T, Hq), x.dtype).at[tok].add(gath * wv[:, None])
        sh = jax.nn.silu(x @ sw_gate) * (x @ sw_up) @ sw_down
        sh = jax.nn.sigmoid(x @ w_shared_gate) * sh
        out = out + sh
        return inp + out.reshape(Bq, Sq, Hq)
    x = L0_attn_x
    x = x + 0.5 * _L0_ffn_ref(_layernorm(x, axis=-1), L0_ffn_w_norm, L0_ffn_w_router, L0_ffn_w_gate, L0_ffn_w_up, L0_ffn_w_down, L0_ffn_sw_gate, L0_ffn_sw_up, L0_ffn_sw_down, L0_ffn_w_shared_gate)
    x = x + _L0_attn_ref(_layernorm(x, axis=-1), L0_attn_Wq, L0_attn_Wkv, L0_attn_Wout)
    x = x + 0.5 * _L0_ffn_ref(_layernorm(x, axis=-1), L0_ffn_w_norm, L0_ffn_w_router, L0_ffn_w_gate, L0_ffn_w_up, L0_ffn_w_down, L0_ffn_sw_gate, L0_ffn_sw_up, L0_ffn_sw_down, L0_ffn_w_shared_gate)
    return x

_drawn_inputs = setup_inputs


def setup_inputs(seed=0):
    import zlib

    import numpy as np

    out = dict(_drawn_inputs(seed))
    spreads = {}
    factors = {'L0_attn_Wq': 8.0,
     'L0_attn_Wkv': 3.587,
     'L0_attn_Wout': 3.387,
     'L0_ffn_w_norm': 8.0,
     'L0_ffn_w_router': 8.0,
     'L0_ffn_w_gate': 8.0,
     'L0_ffn_w_up': 8.0,
     'L0_ffn_w_down': 8.0,
     'L0_ffn_sw_gate': 6.951,
     'L0_ffn_sw_up': 6.852,
     'L0_ffn_sw_down': 6.84,
     'L0_ffn_w_shared_gate': 8.0}
    for name, (base, spread) in spreads.items():
        noise = np.random.default_rng([zlib.crc32(name.encode()), seed]).standard_normal(out[name].shape)
        drawn = base * np.exp(spread * noise) if base else spread * noise
        out[name] = jnp.asarray(drawn.astype(out[name].dtype))
    for name, factor in factors.items():
        out[name] = (out[name] * factor).astype(out[name].dtype)
    return out
```

```python
from contextlib import ExitStack

import numpy as np
import concourse.bass as bass
from concourse import mybir

F32 = mybir.dt.float32
F16 = mybir.dt.float16
BF16 = mybir.dt.bfloat16
I32 = mybir.dt.int32
U32 = mybir.dt.uint32
ALU = mybir.AluOpType
ACT = mybir.ActivationFunctionType
AX = mybir.AxisListType.X

P = 128
BATCH, SEQ, D = 2, 1024, 256
NT = BATCH * SEQ // P
DC = D // P
BLK = 4
NB = NT // BLK
E, TOPK, FE, CAP = 32, 4, 176, 128
FH = FE // 2
FS = 704
FT = -(-FS // P)
HEADS, DH = 16, 128
HG = 4
SCALE = DH ** -0.5
QT = SEQ // P
UNITS = QT * HEADS // HG
HALF = DH // 2
LN_EPS, RMS_EPS = 1e-5, 1e-6
MASKED = -3e38
EXP_ZERO = -87.3
FAR = 65536.0
MAGIC = 12582912.0
EG, AS, BS = 16, 8, 16

CONST = {}
_at = 0
for _name, _n in (("ident", P), ("mask", P), ("before", P), ("cos", QT * HALF), ("sin", QT * HALF),
                  ("own", EG), ("expert", E), ("first_slot", E), ("sixteen", BS), ("token", NT)):
    CONST[_name] = (_at, _n)
    _at += _n
CONST_COLS = _at


def constants():
    c = np.zeros((P, CONST_COLS), np.float32)

    def put(name, value):
        at, n = CONST[name]
        c[:, at:at + n] = value

    p = np.arange(P)
    put("ident", np.eye(P))
    put("mask", np.where(p[None, :] > p[:, None], MASKED, 0.0))
    put("before", p[:, None] < p[None, :])
    inv = (1.0 / np.float32(10000.0) ** (np.arange(0, DH, 2, dtype=np.float32) / np.float32(DH))).astype(np.float32)
    pos = (np.arange(SEQ, dtype=np.float32)[:, None] * inv[None, :]).astype(np.float32)
    for name, f in (("cos", np.cos), ("sin", np.sin)):
        put(name, f(pos).astype(np.float32).reshape(QT, P, HALF).transpose(1, 0, 2).reshape(P, QT * HALF))
    put("own", p[:, None] // AS == np.arange(EG)[None, :])
    put("expert", np.arange(E))
    put("first_slot", np.arange(E) * CAP)
    put("sixteen", np.arange(BS))
    put("token", p[:, None] + P * np.arange(NT)[None, :])
    return c


def one(i):
    return bass.ds(i, 1)


class Chain:

    def __init__(self, eng, sem):
        self.eng, self.sem, self.base, self.n = eng, sem, 0, 0

    def link(self, ins):
        self.n += 1
        ins.then_inc(self.sem, 1)
        self.eng.wait_ge(self.sem, self.base + self.n)

    def enter(self, i, links):
        self.start, self.links = self.base + self.n, links
        self.base, self.n = self.start + i * links, 0

    def leave(self, iterations):
        assert self.n == self.links, (self.n, self.links)
        self.base, self.n = self.start + iterations * self.links, 0


def ffn(nc, layer, env):
    ctx = ExitStack()

    def sb(name, shape, dt):
        return ctx.enter_context(nc.sbuf_tensor(f"{name}_{layer}", shape, dt))

    def sem(name):
        return ctx.enter_context(nc.semaphore(f"{name}_{layer}"))

    with ctx:
        x, const, bank = env["x"], env["const"], env["bank"]
        ident, ones_b, before_b = env["ident"], env["ones_b"], env["before_b"]
        w_norm, w_route = env["w_norm"], env["w_route"]
        ws_gate, ws_up, ws_down = env["ws_gate"], env["ws_up"], env["ws_down"]
        xr_dram, y_dram = env["xr_dram"], env["y_dram"]
        dram = env["dram"]

        h = sb("h", [P, NT, D], F32)
        xT = sb("xT", [P, DC, NT * P], F32)
        xr = [sb(f"xr{k}", [P, BLK, D], F32) for k in range(2)]
        stats = sb("stats", [P, NT, 6], F32)
        mv = sb("mv", [P, NT, 2], F32)
        half_p = sb("half_p", [P, NT], F32)
        ve = sb("ve", [P, NT], F32)
        rstd = sb("rstd", [P, NT], F32)
        shift = sb("shift", [P, NT], F32)
        msq = sb("msq", [P, NT], F32)
        rrms = sb("rrms", [P, NT], F32)
        logitsT = [sb(f"logitsT{k}", [E + 1, BLK * P], F32) for k in range(2)]
        logits = sb("logits", [P, NT, E + 1], F32)
        top = sb("top", [P, NT], F32)
        diff = sb("diff", [P, NT, E], F32)
        key = sb("key", [P, NT, E], F32)
        probs = sb("probs", [P, NT, E], F32)
        sig_e = sb("sig_e", [P, NT], F32)
        sig = sb("sig", [P, NT], F32)
        val8 = sb("val8", [P, NT, 8], F32)
        idx8 = sb("idx8", [P, NT, 8], U32)
        idxf = sb("idxf", [P, NT, TOPK], F32)
        onehot = sb("onehot", [P, NT, TOPK, E], BF16)
        chosen2 = sb("chosen2", [P, NT, 2, E], BF16)
        chosen = sb("chosen", [P, NT, E], BF16)
        den = sb("den", [P, NT], F32)
        rden = sb("rden", [P, NT], F32)
        wk = sb("wk", [P, NT, TOPK], F32)
        late = diff
        slot = sb("slot", [P, NT, E], F32)
        slotk = sb("slotk", [P, NT, TOPK], F32)
        slotu = sb("slotu", [P, NT * TOPK], U32)
        row_a = probs
        row_ah = sb("row_ah", [P, NT, E], F16)
        row_bh = sb("row_bh", [P, NT, E], F16)
        hot_a = sb("hot_a", [P, NT, EG, AS], F16)
        hot_b = sb("hot_b", [P, NT, EG, BS], F16)
        picked = hot_b[:, :, :, :].rearrange("p t e b -> p (t e b)").bitcast(F32)\
            .rearrange("p (t k e) -> p t k e", t=NT, k=TOPK)
        sixteen_h = sb("sixteen_h", [P, BS], F16)
        token_h = sb("token_h", [P, NT], F16)
        table_own = sb("table_own", [P, 2, EG, BS], F32)
        table = sb("table", [P, 2, BS], F32)
        tableT = sb("tableT", [BS, AS, E], U32)
        source = sb("source", [P, E], U32)
        s_gate = [sb(f"s_gate{k}", [P, BLK * P], F32) for k in range(2)]
        s_hid = sb("s_hid", [P, FT, BLK * P], F32)
        we_gate = [sb(f"we_gate{k}", [P, 2, DC, FE], F32) for k in range(2)]
        we_up = [sb(f"we_up{k}", [P, 2, DC, FE], F32) for k in range(2)]
        we_down = [sb(f"we_down{k}", [FH, 2, 2, D], F32) for k in range(2)]
        xe = [sb(f"xe{k}", [P, D], F32) for k in range(4)]
        xeT = [sb(f"xeT{k}", [P, DC, P], F32) for k in range(2)]
        e_gate = [s_gate[k][0:FH, 0:2 * P].rearrange("p (c t) -> p c t", c=2) for k in range(2)]
        e_hid = [s_gate[k][0:FH, 2 * P:4 * P].rearrange("p (c t) -> p c t", c=2) for k in range(2)]
        ye = [hot_a[:, 4 * k:4 * k + 4, :, :].rearrange("p t e a -> p (t e a)").bitcast(F32) for k in range(4)]
        back = xr + [sb(f"back{k}", [P, TOPK, D], F32) for k in (2, 3)]

        def col(name):
            at, n = CONST[name]
            return const[:, at:at + n]

        names = ("moments ve_ready rstd_ready msq_ready rrms_ready pool_own xr_ready xr_turned xT_ready "
                 "rT_done rT_copied r_done r_copied diff_ready val_ready exps_ready chosen_ready pos_done "
                 "hots_ready table_done table_ready tableT_done tableT_ready source_ready slots_ready "
                 "sg_done sg_act sg_used s_hid_ready so_done so_used back_clear back_used out_ready "
                 "xeT_turned xeT_ready gu_done e_act e_hid_ready y_done ye_ready sum_ready dve_own out_done").split()
        s = {n: sem(n) for n in names}
        xr_saved = [sem(f"xr_saved{k}") for k in range(2)]
        we_in = [sem(f"we_in{k}") for k in range(2)]
        xe_in = [sem(f"xe_in{k}") for k in range(4)]
        ye_out = [sem(f"ye_out{k}") for k in range(4)]
        back_in = [sem(f"back_in{k}") for k in range(4)]

        def load_pair(sp, pair, k):
            g = dram["w_gate"].rearrange("(n e) (c p) f -> n p e c f", e=2, p=P)
            u = dram["w_up"].rearrange("(n e) (c p) f -> n p e c f", e=2, p=P)
            d = dram["w_down"].rearrange("(n e) (c p) f -> n p e c f", e=2, p=FH)
            for q in range(2):
                sp.dma_start(we_gate[k][:, q], g[one(pair), :, q].rearrange("n p c f -> (n p) c f")).then_inc(we_in[k], 16)
                sp.dma_start(we_up[k][:, q], u[one(pair), :, q].rearrange("n p c f -> (n p) c f")).then_inc(we_in[k], 16)
                sp.dma_start(we_down[k][:, q], d[one(pair), :, q].rearrange("n p c f -> (n p) c f")).then_inc(we_in[k], 16)

        block = ctx.enter_context(nc.Block())

        @block.sync
        def _(sp):
            for k in range(4):
                sp.sem_inc(ye_out[k], 16)
            for k in range(2):
                load_pair(sp, k, k)
            xr_rows = xr_dram.rearrange("(n t p) d -> n p t d", p=P, t=BLK)
            for blk in range(NB):
                sp.wait_ge(s["xr_ready"], BLK * (blk + 1))
                sp.dma_start(xr_rows[blk], xr[blk % 2][:, :, :]).then_inc(xr_saved[blk % 2], 16)
            sp.wait_ge(s["tableT_ready"], 2)
            for a in range(AS):
                sp.dma_start(source[a * BS:(a + 1) * BS, :], tableT[:, a, :]).then_inc(s["source_ready"], 16)

            y_rows = y_dram.rearrange("(e c) d -> e c d", c=CAP)

            def store_y(e, k, n):
                sp.wait_ge(s["ye_ready"], n + 2)
                sp.dma_start(y_rows[one(e)].rearrange("e c d -> (e c) d"), ye[k]).then_inc(ye_out[k], 16)

            with sp.Fori(0, E // 4 - 1) as it:
                for q in range(4):
                    store_y(it * 4 + q, q, it * 4 + q + 1)
                    if q % 2:
                        sp.wait_ge(s["y_done"], it * 4 + q + 1)
                        load_pair(sp, it * 2 + q // 2 + 2, q // 2)
            for q in range(4):
                store_y(E - 4 + q, q, E - 4 + q + 1)
            if layer == 1:
                out_rows = dram["out"].rearrange("(n p) d -> n p d", p=P)
                with sp.Fori(0, NT) as t:
                    sp.wait_ge(s["out_ready"], t + 1)
                    sp.dma_start(out_rows[one(t)].rearrange("n p d -> (n p) d"),
                                 x[:, one(t), :].rearrange("p n d -> p (n d)")).then_inc(s["out_done"], 16)
                sp.wait_ge(s["out_done"], 16 * NT)
            for k in range(4):
                sp.wait_ge(ye_out[k], 16 * E // 4 + 16)

        @block.gpsimd
        def _(pool):
            nc.gpsimd.memset(half_p[:, :], -0.5).then_inc(s["pool_own"], 1)
            for k in (2, 3):
                nc.gpsimd.memset(back[k][:, :, :], 0.0).then_inc(s["pool_own"], 1)
            pool.wait_ge(s["pool_own"], 3)
            pool.wait_ge(s["ve_ready"], 1)
            nc.gpsimd.tensor_tensor(rstd[:, :], ve[:, :], half_p[:, :], ALU.pow).then_inc(s["rstd_ready"], 1)
            pool.wait_ge(s["msq_ready"], 1)
            nc.gpsimd.tensor_tensor(rrms[:, :], msq[:, :], half_p[:, :], ALU.pow).then_inc(s["rrms_ready"], 1)
            for k in range(2):
                pool.wait_ge(xr_saved[k], 16 * NB // 2)
            pool.wait_ge(s["source_ready"], 16 * AS)
            for e in range(E):
                k = e % 4
                if e >= 4:
                    pool.wait_ge(s["xeT_turned"], e)
                nc.gpsimd.indirect_dma_start(xe[k][:, :], None, xr_dram[:, :],
                                             bass.IndirectOffsetOnAxis(source[:, e:e + 1], 0)).then_inc(xe_in[k], 16)
            for k in range(4):
                pool.wait_ge(ye_out[k], 16 * E // 4 + 16)
            pool.wait_ge(s["slots_ready"], 1)
            for t in range(NT):
                k = t % 4
                if t >= 4:
                    pool.wait_ge(s["back_used"], t)
                for j in range(TOPK):
                    n = t * TOPK + j
                    nc.gpsimd.indirect_dma_start(back[k][:, j, :], None, y_dram[:, :],
                                                 bass.IndirectOffsetOnAxis(slotu[:, n:n + 1], 0),
                                                 bounds_check=E * CAP - 1, oob_is_err=False).then_inc(back_in[k], 16)

        @block.scalar
        def _(act):
            act.sem_inc(s["xeT_ready"], 2)
            for blk in range(NB):
                for c in range(DC):
                    act.wait_ge(s["xr_turned"], DC * blk + c + 1)
                    nc.scalar.copy(xT[:, c, blk * BLK * P:(blk + 1) * BLK * P], bank(c)).then_inc(s["xT_ready"], 1)
                act.wait_ge(s["rT_done"], blk + 1)
                nc.scalar.copy(logitsT[blk % 2][:, :], bank(6)[0:E + 1, :]).then_inc(s["rT_copied"], 1)
            act.wait_ge(s["diff_ready"], 1)
            nc.scalar.activation(probs[:, :, :], diff[:, :, :], ACT.Exp).then_inc(s["exps_ready"], 1)
            nc.scalar.activation(sig_e[:, :], logits[:, :, E], ACT.Exp, scale=-1.0).then_inc(s["exps_ready"], 1)
            act.wait_ge(s["val_ready"], 1)
            nc.scalar.activation(wk[:, :, :], val8[:, :, 0:TOPK], ACT.Exp).then_inc(s["exps_ready"], 1)

            def shared_gates(blk):
                for f in range(FT):
                    m = min(P, FS - f * P)
                    n = blk * FT + f
                    act.wait_ge(s["sg_done"], n + 1)
                    nc.scalar.activation(s_gate[f % 2][0:m, :], bank(2 + 2 * (f % 2))[0:m, :], ACT.Silu).then_inc(s["sg_act"], 1)

            shared_gates(0)
            shared_gates(1)
            with act.Fori(0, E // 4) as it:
                for q in range(4):
                    e = it * 4 + q
                    act.wait_ge(s["xeT_turned"], e + 4)
                    nc.scalar.copy(xeT[q % 2][:, :, :], bank(q % 2)[:, 0:DC * P].rearrange("p (c t) -> p c t", c=DC)).then_inc(s["xeT_ready"], 1)
                    act.wait_ge(s["gu_done"], e + 1)
                    nc.scalar.activation(e_gate[q % 2], bank(2 + q % 2)[0:FH, 0:2 * P].rearrange("p (c t) -> p c t", c=2),
                                         ACT.Silu).then_inc(s["e_act"], 1)
            shared_gates(2)
            shared_gates(3)

        @block.vector
        def _(dve):
            own = Chain(dve, s["dve_own"])
            link = own.link
            dve.sem_inc(s["e_hid_ready"], 2)
            dve.sem_inc(s["ye_ready"], 2)
            dve.sem_inc(s["back_used"], 3)
            if layer == 0:
                dve.wait_ge(env["x_in"], 16 * NB)
            with dve.Fori(0, NT) as t:
                nc.vector.bn_stats(stats[:, one(t), :].rearrange("p n d -> p (n d)"),
                                   x[:, one(t), :].rearrange("p n d -> p (n d)")).then_inc(s["moments"], 1)
            dve.wait_ge(s["moments"], NT)
            for t in range(NT):
                ins = nc.vector.bn_aggr(mv[:, t, :], stats[:, t, :])
            link(ins)
            nc.vector.tensor_scalar(ve[:, :], mv[:, :, 1], LN_EPS, None, ALU.add).then_inc(s["ve_ready"], 1)
            dve.wait_ge(s["rstd_ready"], 1)
            link(nc.vector.tensor_tensor(msq[:, :], mv[:, :, 1], rstd[:, :], ALU.mult))
            link(nc.vector.tensor_tensor(msq[:, :], msq[:, :], rstd[:, :], ALU.mult))
            nc.vector.tensor_scalar(msq[:, :], msq[:, :], RMS_EPS, None, ALU.add).then_inc(s["msq_ready"], 1)
            link(nc.vector.scalar_tensor_tensor(shift[:, :], mv[:, :, 0], -1.0, rstd[:, :], ALU.mult, ALU.mult))
            dve.wait_ge(s["rrms_ready"], 1)
            if layer == 0:
                dve.wait_ge(env["w_in"], 16 * env["w_loads"])
            for blk in range(NB):
                for q in range(BLK):
                    t = blk * BLK + q
                    link(nc.vector.tensor_scalar(h[:, t, :], x[:, t, :], rstd[:, t:t + 1], shift[:, t:t + 1], ALU.mult, ALU.add))
                    if blk >= 2 and q == 0:
                        dve.wait_ge(s["xr_turned"], DC * (blk - 1))
                        dve.wait_ge(xr_saved[blk % 2], 16 * (blk // 2))
                    nc.vector.scalar_tensor_tensor(xr[blk % 2][:, q, :], h[:, t, :], rrms[:, t:t + 1], w_norm[:, :],
                                                   ALU.mult, ALU.mult).then_inc(s["xr_ready"], 1)
                if blk:
                    dve.wait_ge(s["r_done"], blk)
                    nc.vector.tensor_copy(logits[:, (blk - 1) * BLK:blk * BLK, :],
                                          bank(7)[:, 0:BLK * (E + 1)].rearrange("p (t e) -> p t e", t=BLK)).then_inc(s["r_copied"], 1)
            dve.wait_ge(s["r_done"], NB)
            nc.vector.tensor_copy(logits[:, (NB - 1) * BLK:, :],
                                  bank(7)[:, 0:BLK * (E + 1)].rearrange("p (t e) -> p t e", t=BLK)).then_inc(s["r_copied"], 1)
            dve.wait_ge(s["r_copied"], NB)
            def shared_hidden(blk, f):
                m = min(P, FS - f * P)
                n = blk * FT + f
                if f == 0 and blk:
                    dve.wait_ge(s["so_done"], blk * BLK)
                dve.wait_ge(s["sg_act"], n + 1)
                nc.vector.tensor_tensor(s_hid[0:m, f, :], bank(3 + 2 * (f % 2))[0:m, :], s_gate[f % 2][0:m, :],
                                        ALU.mult).then_inc(s["s_hid_ready"], 1)

            def shared_out(blk, q):
                t = blk * BLK + q
                dve.wait_ge(s["so_done"], t + 1)
                ht = h[:, t, :]
                nc.vector.scalar_tensor_tensor(ht, bank(6 + q % 2)[:, 0:D], sig[:, t:t + 1], ht, ALU.mult, ALU.add).then_inc(s["so_used"], 1)

            def combine(t):
                k = t % 4
                dve.wait_ge(back_in[k], 16 * TOPK * (t // 4 + 1))
                dve.wait_ge(s["so_used"], min(NT, t // 8 * 8 + 8))
                for j in range(TOPK):
                    ins = nc.vector.scalar_tensor_tensor(h[:, t, :], back[k][:, j, :], wk[:, t, j:j + 1], h[:, t, :], ALU.mult, ALU.add)
                    if j < TOPK - 1:
                        link(ins)
                ins.then_inc(s["back_used"], 1)
                dve.wait_ge(s["back_used"], t + 4)
                nc.vector.scalar_tensor_tensor(x[:, t, :], h[:, t, :], 0.5, x[:, t, :], ALU.mult, ALU.add).then_inc(s["out_ready"], 1)

            link(nc.vector.reduce_max(top[:, :], logits[:, :, 0:E], axis=AX))
            nc.vector.tensor_tensor(diff[:, :, :], logits[:, :, 0:E], top[:, :].unsqueeze(2).to_broadcast([P, NT, E]),
                                    ALU.subtract).then_inc(s["diff_ready"], 1)
            dve.wait_ge(s["diff_ready"], 1)
            link(nc.vector.tensor_scalar(key[:, :, :], diff[:, :, :], EXP_ZERO, None, ALU.max))
            for t in range(NT):
                ins = nc.vector.max(val8[:, t, :], key[:, t, :])
            ins.then_inc(s["val_ready"], 1)
            dve.wait_ge(s["val_ready"], 1)
            for t in range(NT):
                ins = nc.vector.max_index(idx8[:, t, :], val8[:, t, :], key[:, t, :])
            link(ins)
            link(nc.vector.tensor_copy(idxf[:, :, :], idx8[:, :, 0:TOPK]))
            link(nc.vector.tensor_tensor(onehot[:, :, :, :], col("expert").unsqueeze(1).unsqueeze(1).to_broadcast([P, NT, TOPK, E]),
                                         idxf[:, :, :].unsqueeze(3).to_broadcast([P, NT, TOPK, E]), ALU.is_equal))
            link(nc.vector.tensor_tensor(chosen2[:, :, :, :], onehot[:, :, 0:2, :], onehot[:, :, 2:4, :], ALU.add))
            nc.vector.tensor_tensor(chosen[:, :, :], chosen2[:, :, 0, :], chosen2[:, :, 1, :], ALU.add).then_inc(s["chosen_ready"], 1)
            for f in range(FT):
                shared_hidden(0, f)
            dve.wait_ge(s["exps_ready"], 3)
            link(nc.vector.reduce_sum(den[:, :], probs[:, :, :], axis=AX))
            link(nc.vector.reciprocal(rden[:, :], den[:, :]))
            link(nc.vector.tensor_tensor(wk[:, :, :], wk[:, :, :], rden[:, :].unsqueeze(2).to_broadcast([P, NT, TOPK]), ALU.mult))
            link(nc.vector.tensor_scalar(sig[:, :], sig_e[:, :], 1.0, None, ALU.add))
            link(nc.vector.reciprocal(sig[:, :], sig[:, :]))
            nc.vector.tensor_copy(sixteen_h[:, :], col("sixteen"))
            link(nc.vector.tensor_copy(token_h[:, :], col("token")))
            pos = bank(0).rearrange("p (t e) -> p t e", t=NT)
            dve.wait_ge(s["chosen_ready"], 1)
            dve.wait_ge(s["pos_done"], 1)
            link(nc.vector.tensor_scalar(late[:, :, :], pos, float(CAP), FAR, ALU.is_ge, ALU.mult))
            link(nc.vector.tensor_tensor(late[:, :, :], pos, late[:, :, :], ALU.add))
            link(nc.vector.tensor_tensor(slot[:, :, :], late[:, :, :],
                                         col("first_slot").unsqueeze(1).to_broadcast([P, NT, E]), ALU.add))
            link(nc.vector.scalar_tensor_tensor(key[:, :, :], chosen[:, :, :], -FAR, late[:, :, :], ALU.mult, ALU.add))
            link(nc.vector.tensor_scalar(key[:, :, :], key[:, :, :], FAR, 1024.0, ALU.add, ALU.min))
            link(nc.vector.tensor_scalar(row_a[:, :, :], key[:, :, :], 1.0 / BS, -0.46875, ALU.mult, ALU.add))
            link(nc.vector.tensor_scalar(row_a[:, :, :], row_a[:, :, :], MAGIC, -MAGIC, ALU.add, ALU.add))
            link(nc.vector.tensor_copy(row_ah[:, :, :], row_a[:, :, :]))
            link(nc.vector.scalar_tensor_tensor(row_bh[:, :, :], row_a[:, :, :], -float(BS), key[:, :, :], ALU.mult, ALU.add))
            for q in range(BLK):
                shared_out(0, q)
            for g in range(2):
                eg = slice(g * EG, (g + 1) * EG)
                if g:
                    dve.wait_ge(s["table_done"], g)
                link(nc.vector.tensor_tensor(hot_a[:, :, :, :], row_ah[:, :, eg].unsqueeze(3).to_broadcast([P, NT, EG, AS]),
                                             sixteen_h[:, 0:AS].unsqueeze(1).unsqueeze(1).to_broadcast([P, NT, EG, AS]), ALU.is_equal))
                link(nc.vector.tensor_tensor(hot_a[:, :, :, :], hot_a[:, :, :, :],
                                             token_h[:, :].unsqueeze(2).unsqueeze(2).to_broadcast([P, NT, EG, AS]), ALU.mult))
                nc.vector.tensor_tensor(hot_b[:, :, :, :], row_bh[:, :, eg].unsqueeze(3).to_broadcast([P, NT, EG, BS]),
                                        sixteen_h[:, :].unsqueeze(1).unsqueeze(1).to_broadcast([P, NT, EG, BS]),
                                        ALU.is_equal).then_inc(s["hots_ready"], 1)
            dve.wait_ge(s["table_done"], 2)
            tab = bank(1).rearrange("p (g e b) -> p g e b", g=2, e=EG)
            link(nc.vector.tensor_tensor(table_own[:, :, :, :], tab,
                                         col("own").unsqueeze(1).unsqueeze(3).to_broadcast([P, 2, EG, BS]), ALU.mult))
            nc.vector.reduce_sum(table[:, :, :], table_own[:, :, :, :].rearrange("p g e b -> p g b e"), axis=AX).then_inc(s["table_ready"], 1)
            dve.wait_ge(s["tableT_done"], 1)
            for g in range(2):
                nc.vector.tensor_copy(tableT[:, :, g * EG:(g + 1) * EG],
                                      bank(1)[0:BS, g * P:(g + 1) * P].rearrange("b (e a) -> b a e", e=EG)).then_inc(s["tableT_ready"], 1)
            link(nc.vector.tensor_tensor(picked, onehot[:, :, :, :],
                                         slot[:, :, :].unsqueeze(2).to_broadcast([P, NT, TOPK, E]), ALU.mult))
            link(nc.vector.reduce_sum(slotk[:, :, :], picked, axis=AX))
            nc.vector.tensor_copy(slotu[:, :].rearrange("p (t k) -> p t k", k=TOPK), slotk[:, :, :]).then_inc(s["slots_ready"], 1)
            link(nc.vector.scalar_tensor_tensor(wk[:, :, :], slotk[:, :, :], float(E * CAP), wk[:, :, :], ALU.is_lt, ALU.mult))

            for f in range(FT):
                shared_hidden(1, f)
            for q in range(BLK):
                shared_out(1, q)
            with dve.Fori(0, E // 4) as it:
                for q in range(4):
                    e = it * 4 + q
                    dve.wait_ge(s["e_act"], e + 1)
                    nc.vector.tensor_tensor(e_hid[q % 2], bank(2 + q % 2)[0:FH, 2 * P:4 * P].rearrange("p (c t) -> p c t", c=2),
                                            e_gate[q % 2], ALU.mult).then_inc(s["e_hid_ready"], 1)
                    dve.wait_ge(s["y_done"], e + 1)
                    dve.wait_ge(ye_out[q], it * 16 + 16)
                    nc.vector.tensor_copy(ye[q], bank(4 + q % 2)[:, 0:D]).then_inc(s["ye_ready"], 1)
            t = 0
            for blk in (2, 3):
                for f in range(FT):
                    shared_hidden(blk, f)
                    if f % 2 and t < 2 * BLK:
                        combine(t)
                        t += 1
                for q in range(BLK):
                    shared_out(blk, q)
            while t < NT:
                combine(t)
                t += 1

        @block.tensor
        def _(pe):
            pe.sem_inc(s["xeT_turned"], 3)
            if layer == 0:
                pe.wait_ge(env["w_in"], 16 * env["w_loads"])
                pe.wait_ge(env["tables_ready"], 4)
            for blk in range(NB):
                pe.wait_ge(s["xr_ready"], BLK * (blk + 1))
                for c in range(DC):
                    if blk:
                        pe.wait_ge(s["xT_ready"], DC * (blk - 1) + c + 1)
                    for q in range(BLK):
                        ins = nc.tensor.transpose(bank(c)[:, q * P:(q + 1) * P], xr[blk % 2][:, q, c * P:(c + 1) * P], ident)
                    ins.then_inc(s["xr_turned"], 1)
                pe.wait_ge(s["xT_ready"], DC * (blk + 1))
                if blk:
                    pe.wait_ge(s["rT_copied"], blk)
                for c in range(DC):
                    ins = nc.tensor.matmul(bank(6)[0:E + 1, :], w_route[:, c, :], xT[:, c, blk * BLK * P:(blk + 1) * BLK * P],
                                           start=c == 0, stop=c == DC - 1)
                ins.then_inc(s["rT_done"], 1)
                pe.wait_ge(s["rT_copied"], blk + 1)
                if blk:
                    pe.wait_ge(s["r_copied"], blk)
                for q in range(BLK):
                    ins = nc.tensor.transpose(bank(7)[:, q * (E + 1):(q + 1) * (E + 1)], logitsT[blk % 2][:, q * P:(q + 1) * P],
                                              ident[0:E + 1, 0:E + 1])
                ins.then_inc(s["r_done"], 1)

            def shared_in(blk):
                for f in range(FT):
                    m = min(P, FS - f * P)
                    n = blk * FT + f
                    if blk == 0 and f >= 2 or blk:
                        pe.wait_ge(s["s_hid_ready"], n - 1)
                    for w, b in ((ws_gate, 2), (ws_up, 3)):
                        for c in range(DC):
                            ins = nc.tensor.matmul(bank(b + 2 * (f % 2))[0:m, :], w[:, c, f * P:f * P + m],
                                                   xT[:, c, blk * BLK * P:(blk + 1) * BLK * P], start=c == 0, stop=c == DC - 1)
                    ins.then_inc(s["sg_done"], 1)

            def shared_down(blk):
                for q in range(BLK):
                    t = blk * BLK + q
                    if q == 0:
                        pe.wait_ge(s["s_hid_ready"], FT * (blk + 1))
                    if t >= 2:
                        pe.wait_ge(s["so_used"], t - 1)
                    for f in range(FT):
                        m = min(P, FS - f * P)
                        ins = nc.tensor.matmul(bank(6 + q % 2)[:, 0:D], s_hid[0:m, f, q * P:(q + 1) * P], ws_down[0:m, f, :],
                                               start=f == 0, stop=f == FT - 1)
                    ins.then_inc(s["so_done"], 1)

            shared_in(0)
            pe.wait_ge(s["chosen_ready"], 1)
            nc.tensor.matmul(bank(0), before_b, chosen[:, :, :], start=True, stop=False)
            for t in range(NT - 1):
                ins = nc.tensor.matmul(bank(0)[:, (t + 1) * E:], ones_b, chosen[:, t:t + 1, :].to_broadcast([P, NT - 1 - t, E]),
                                       start=False, stop=t == NT - 2)
            ins.then_inc(s["pos_done"], 1)
            shared_down(0)
            for g in range(2):
                pe.wait_ge(s["hots_ready"], g + 1)
                for t in range(NT):
                    ins = nc.tensor.matmul(bank(1)[:, g * EG * BS:(g + 1) * EG * BS], hot_a[:, t, :, :], hot_b[:, t, :, :],
                                           start=t == 0, stop=t == NT - 1)
                ins.then_inc(s["table_done"], 1)
            pe.wait_ge(s["table_ready"], 1)
            for g in range(2):
                ins = nc.tensor.transpose(bank(1)[0:BS, g * P:(g + 1) * P], table[:, g, :], ident)
            ins.then_inc(s["tableT_done"], 1)
            pe.wait_ge(s["tableT_ready"], 2)
            shared_in(1)
            shared_down(1)

            with pe.Fori(0, E // 4) as it:
                def turn(q):
                    e = it * 4 + q
                    pe.wait_ge(xe_in[q], it * 16 + 16)
                    pe.wait_ge(s["xeT_ready"], e + 1)
                    for c in range(DC):
                        ins = nc.tensor.transpose(bank(q % 2)[:, c * P:(c + 1) * P], xe[q][:, c * P:(c + 1) * P], ident)
                    ins.then_inc(s["xeT_turned"], 1)

                def gate_up(q):
                    e = it * 4 + q
                    if q % 2 == 0:
                        pe.wait_ge(we_in[q // 2], it * 96 + 96)
                    pe.wait_ge(s["xeT_ready"], e + 3)
                    pe.wait_ge(s["e_hid_ready"], e + 1)
                    for w, o in ((we_gate, 0), (we_up, 2)):
                        for f in range(2):
                            for c in range(DC):
                                ins = nc.tensor.matmul(bank(2 + q % 2)[0:FH, (o + f) * P:(o + f + 1) * P],
                                                       w[q // 2][:, q % 2, c, f * FH:(f + 1) * FH], xeT[q % 2][:, c, :],
                                                       start=c == 0, stop=c == DC - 1)
                    ins.then_inc(s["gu_done"], 1)

                def down(q):
                    e = it * 4 + q
                    pe.wait_ge(s["e_hid_ready"], e + 3)
                    pe.wait_ge(s["ye_ready"], e + 1)
                    for f in range(2):
                        ins = nc.tensor.matmul(bank(4 + q % 2)[:, 0:D], e_hid[q % 2][:, f, :], we_down[q // 2][:, q % 2, f, :],
                                               start=f == 0, stop=f == 1)
                    ins.then_inc(s["y_done"], 1)

                turn(0)
                for q in range(4):
                    if q < 3:
                        turn(q + 1)
                    gate_up(q)
                    if q:
                        down(q - 1)
                down(3)
            pe.wait_ge(s["ye_ready"], E + 2)
            for blk in (2, 3):
                shared_in(blk)
                shared_down(blk)


def attention(nc, env):
    ctx = ExitStack()

    def sb(name, shape, dt):
        return ctx.enter_context(nc.sbuf_tensor(f"a_{name}", shape, dt))

    with ctx:
        x, const, bank = env["x"], env["const"], env["bank"]
        ident, ident_b, mask_b = env["ident"], env["ident_b"], env["mask_b"]
        w_q, w_kv, w_out = env["w_q"], env["w_kv"], env["w_out"]

        def table(name):
            at, n = CONST[name]
            return const[:, at:at + n].rearrange("p (t d) -> p t d", t=QT)

        cos, sin = table("cos"), table("sin")
        stats = sb("stats", [P, NT, 6], F32)
        mv = sb("mv", [P, NT, 2], F32)
        half_p = sb("half_p", [P, NT], F32)
        ve = sb("ve", [P, NT], F32)
        rstd = sb("rstd", [P, NT], F32)
        shift = sb("shift", [P, NT], F32)
        xn = [sb(f"xn{k}", [P, D], F32) for k in range(2)]
        xnT = sb("xnT", [P, DC, SEQ], F32)
        k_sin = sb("k_sin", [P, DH], F32)
        k_cos = sb("k_cos", [P, DH], F32)
        k_rot = [sb(f"k_rot{k}", [P, DH], F32) for k in range(2)]
        kT = sb("kT", [P, SEQ], F32)
        v = sb("v", [P, QT, DH], F32)
        q_cos = sb("q_cos", [P, HG, DH], F32)
        q_sin = sb("q_sin", [P, HG, DH], F32)
        q_rot = sb("q_rot", [P, HG, DH], F32)
        qT = [sb(f"qT{k}", [P, HG, P], F32) for k in range(2)]
        peak = sb("peak", [P, 2 * HG], F32)
        bias = sb("bias", [P, 2 * HG], F32)
        total = sb("total", [P, 2 * HG], F32)
        weight = sb("weight", [P, 2 * HG], F32)
        probs = [sb(f"probs{k}", [P, SEQ], F32) for k in range(2 * HG)]
        pT = sb("pT", [P, QT, HG, P], F32)
        oT = [sb(f"oT{k}", [P, HEADS, P], F32) for k in range(2)]

        names = ("moments ve_ready rstd_ready dve_own half_ready xn_ready xn_turned xnT_ready kv_done kv_read k_rot_ready "
                 "k_turned kT_ready q_done q_parts q_rotated q_turned qT_ready s_done max_ready exp_done weight_ready "
                 "probs_ready p_turned pT_ready o_done oT_ready a_done x_ready").split()
        s = {n: ctx.enter_context(nc.semaphore(f"a_{n}")) for n in names}

        def group_count(i):
            return -(-(i + 1) // 4)

        turned = np.cumsum([0] + [group_count(n // (HG * HG)) for n in range(UNITS * HG)]).tolist()
        TURNED = turned[-1]
        NH = UNITS * HG

        def score(n):
            return env["bank2"](2 * (n % 2))

        block = ctx.enter_context(nc.Block())

        @block.gpsimd
        def _(pool):
            pool.sem_inc(s["q_rotated"], 1)
            nc.gpsimd.memset(half_p[:, :], -0.5).then_inc(s["half_ready"], 1)
            pool.wait_ge(s["half_ready"], 1)
            pool.wait_ge(s["ve_ready"], 1)
            nc.gpsimd.tensor_tensor(rstd[:, :], ve[:, :], half_p[:, :], ALU.pow).then_inc(s["rstd_ready"], 1)
            for b in range(BATCH):
                def rotate(u):
                    pool.wait_ge(s["q_parts"], b * UNITS + (u + 1))
                    if b or u:
                        pool.wait_ge(s["q_turned"], b * UNITS + u)
                    nc.gpsimd.tensor_tensor(q_rot[:, :, :], q_cos[:, :, :], q_sin[:, :, :], ALU.add).then_inc(s["q_rotated"], 1)

                rotate(0)
                for u in range(UNITS):
                    keys = (u // HG + 1) * P
                    for j in range(HG):
                        n = u * HG + j
                        pool.wait_ge(s["weight_ready"], b * NH + (n + 1))
                        r = probs[n % (2 * HG)]
                        nc.gpsimd.tensor_scalar(r[:, 0:keys], r[:, 0:keys], weight[:, n % (2 * HG):n % (2 * HG) + 1], 1.0,
                                                ALU.mult, ALU.mult).then_inc(s["probs_ready"], 1)
                    if u + 1 < UNITS:
                        rotate(u + 1)

        @block.scalar
        def _(act):
            act.sem_inc(s["pT_ready"], 1)
            with act.Fori(0, BATCH) as b:
                def turned_keys(i):
                    act.wait_ge(s["k_turned"], b * QT + (i + 1))
                    nc.scalar.copy(kT[:, i * P:(i + 1) * P], bank(i % 2)[:, 0:P]).then_inc(s["kT_ready"], 1)

                for i in range(QT):
                    act.wait_ge(s["xn_turned"], b * QT + (i + 1))
                    nc.scalar.copy(xnT[:, :, i * P:(i + 1) * P], bank(4 + i % 2)[:, 0:DC * P].rearrange("p (c t) -> p c t", c=DC))\
                        .then_inc(s["xnT_ready"], 1)
                    if i >= 2:
                        turned_keys(i - 2)
                turned_keys(QT - 2)
                turned_keys(QT - 1)

                def queries(u):
                    act.wait_ge(s["q_turned"], b * UNITS + (u + 1))
                    nc.scalar.copy(qT[u % 2][:, :, :], bank(6).rearrange("p (h t) -> p h t", h=HG)).then_inc(s["qT_ready"], 1)

                queries(0)
                for u in range(UNITS + 1):
                    for j in range(HG):
                        if u < UNITS:
                            n = u * HG + j
                            k = n % (2 * HG)
                            keys = (u // HG + 1) * P
                            act.wait_ge(s["max_ready"], b * NH + (n + 1))
                            if n >= 2 * HG:
                                act.wait_ge(s["p_turned"], b * TURNED + turned[n - 2 * HG + 1])
                            nc.scalar.activation(probs[k][:, 0:keys], score(n)[:, 0:keys], ACT.Exp, bias=bias[:, k:k + 1],
                                                 scale=SCALE, accum_out=total[:, k:k + 1]).then_inc(s["exp_done"], 1)
                        if u:
                            n = (u - 1) * HG + j
                            i = (u - 1) // HG
                            for g in range(group_count(i)):
                                m = min(4, i + 1 - 4 * g)
                                at = turned[n] + g
                                act.wait_ge(s["p_turned"], b * TURNED + (at + 1))
                                nc.scalar.copy(pT[:, 4 * g:4 * g + m, j, :],
                                               bank(4 + at % 2)[:, 0:m * P].rearrange("p (m t) -> p m t", m=m)).then_inc(s["pT_ready"], 1)
                    if u + 1 < UNITS:
                        queries(u + 1)

        @block.vector
        def _(dve):
            own = Chain(dve, s["dve_own"])
            link = own.link
            dve.sem_inc(s["x_ready"], 1)
            with dve.Fori(0, NT) as t:
                nc.vector.bn_stats(stats[:, one(t), :].rearrange("p n d -> p (n d)"),
                                   x[:, one(t), :].rearrange("p n d -> p (n d)")).then_inc(s["moments"], 1)
            dve.wait_ge(s["moments"], NT)
            for t in range(NT):
                ins = nc.vector.bn_aggr(mv[:, t, :], stats[:, t, :])
            link(ins)
            nc.vector.tensor_scalar(ve[:, :], mv[:, :, 1], LN_EPS, None, ALU.add).then_inc(s["ve_ready"], 1)
            dve.wait_ge(s["rstd_ready"], 1)
            link(nc.vector.scalar_tensor_tensor(shift[:, :], mv[:, :, 0], -1.0, rstd[:, :], ALU.mult, ALU.mult))
            with dve.Fori(0, BATCH) as b:
                own.enter(b, UNITS * HG)

                def rows(i):
                    return x[:, one(b * QT + i), :].rearrange("p n d -> p (n d)")

                def parts(src, a_cos, a_sin, i, heads):
                    shape = [P, heads, 2, HALF]
                    q = src.rearrange("p (h s d) -> p h s d", h=heads, s=2)
                    c = cos[:, i:i + 1, :].unsqueeze(1).to_broadcast(shape)
                    d = sin[:, i:i + 1, :].to_broadcast([P, heads, HALF])
                    nc.vector.tensor_tensor(a_cos.rearrange("p h (s d) -> p h s d", s=2), q, c, ALU.mult)
                    nc.vector.scalar_tensor_tensor(a_sin[:, :, 0:HALF], q[:, :, 1, :], -1.0, d, ALU.mult, ALU.mult)
                    return nc.vector.tensor_tensor(a_sin[:, :, HALF:DH], q[:, :, 0, :], d, ALU.mult)

                def key_value(i):
                    dve.wait_ge(s["kv_done"], b * QT + (i + 1))
                    kv = bank(6 + i % 2)
                    nc.vector.tensor_copy(v[:, i, :], kv[:, DH:2 * DH])
                    parts(kv[:, 0:DH], k_cos[:, :].unsqueeze(1), k_sin[:, :].unsqueeze(1), i, 1).then_inc(s["kv_read"], 1)
                    dve.wait_ge(s["kv_read"], b * QT + (i + 1))
                    if i >= 2:
                        dve.wait_ge(s["k_turned"], b * QT + (i - 1))
                    nc.vector.tensor_tensor(k_rot[i % 2][:, :], k_cos[:, :], k_sin[:, :], ALU.add).then_inc(s["k_rot_ready"], 1)
                    dve.wait_ge(s["k_rot_ready"], b * QT + (i + 1))

                for i in range(QT):
                    if i >= 2:
                        dve.wait_ge(s["xn_turned"], b * QT + (i - 1))
                    nc.vector.tensor_scalar(xn[i % 2][:, :], rows(i), rstd[:, one(b * QT + i)], shift[:, one(b * QT + i)],
                                            ALU.mult, ALU.add).then_inc(s["xn_ready"], 1)
                    if i:
                        key_value(i - 1)
                key_value(QT - 1)

                def query_parts(u):
                    dve.wait_ge(s["q_done"], b * UNITS + (u + 1))
                    dve.wait_ge(s["q_rotated"], b * UNITS + (u + 1))
                    parts(bank(6), q_cos[:, :, :], q_sin[:, :, :], u // HG, HG).then_inc(s["q_parts"], 1)

                def normal(n):
                    k = n % (2 * HG)
                    dve.wait_ge(s["exp_done"], b * NH + (n + 1))
                    nc.vector.reciprocal(weight[:, k:k + 1], total[:, k:k + 1]).then_inc(s["weight_ready"], 1)

                query_parts(0)
                for u in range(UNITS + 1):
                    if u < UNITS:
                        keys = (u // HG + 1) * P
                        for j in range(HG):
                            n = u * HG + j
                            k = n % (2 * HG)
                            dve.wait_ge(s["s_done"], b * NH + (n + 1))
                            link(nc.vector.reduce_max(peak[:, k:k + 1], score(n)[:, 0:keys], axis=AX))
                            nc.vector.tensor_scalar(bias[:, k:k + 1], peak[:, k:k + 1], -SCALE, None, ALU.mult).then_inc(s["max_ready"], 1)
                            if j:
                                normal(n - 1)
                        normal(u * HG + HG - 1)
                        if u + 1 < UNITS:
                            query_parts(u + 1)
                    if u:
                        w = u - 1
                        i, g = w // HG, w % HG
                        dve.wait_ge(s["o_done"], b * UNITS + (w + 1))
                        if i >= 2:
                            dve.wait_ge(s["a_done"], b * QT + (i - 1))
                        nc.vector.tensor_copy(oT[i % 2][:, g * HG:(g + 1) * HG, :],
                                              bank(7).rearrange("p (h t) -> p h t", h=HG)).then_inc(s["oT_ready"], 1)
                        if g == HG - 1:
                            dve.wait_ge(s["a_done"], b * QT + (i + 1))
                            nc.vector.tensor_tensor(rows(i), bank(7)[:, 0:D], rows(i), ALU.add).then_inc(s["x_ready"], 1)
                own.leave(BATCH)

        @block.tensor
        def _(pe):
            with pe.Fori(0, BATCH) as b:
                pe.wait_ge(env["attn_w_in"], 16 * 3)
                pe.wait_ge(s["pT_ready"], b * TURNED + 1)
                pe.wait_ge(s["x_ready"], b * QT + 1)

                def key_value(i):
                    pe.wait_ge(s["xnT_ready"], b * QT + (i + 1))
                    if i >= 2:
                        pe.wait_ge(s["kv_read"], b * QT + (i - 1))
                    for c in range(DC):
                        ins = nc.tensor.matmul(bank(6 + i % 2)[:, 0:2 * DH], xnT[:, c, i * P:(i + 1) * P], w_kv[:, c, :],
                                               start=c == 0, stop=c == DC - 1)
                    ins.then_inc(s["kv_done"], 1)

                def turn_keys(i):
                    pe.wait_ge(s["k_rot_ready"], b * QT + (i + 1))
                    if i >= 2:
                        pe.wait_ge(s["kT_ready"], b * QT + (i - 1))
                    nc.tensor.transpose(bank(i % 2)[:, 0:P], k_rot[i % 2][:, :], ident).then_inc(s["k_turned"], 1)

                for i in range(QT):
                    pe.wait_ge(s["xn_ready"], b * QT + (i + 1))
                    if i >= 2:
                        pe.wait_ge(s["xnT_ready"], b * QT + (i - 1))
                    for c in range(DC):
                        ins = nc.tensor.transpose(bank(4 + i % 2)[:, c * P:(c + 1) * P], xn[i % 2][:, c * P:(c + 1) * P], ident)
                    ins.then_inc(s["xn_turned"], 1)
                    if i >= 1:
                        key_value(i - 1)
                    if i >= 2:
                        turn_keys(i - 2)
                key_value(QT - 1)
                turn_keys(QT - 2)
                turn_keys(QT - 1)

                def project_queries(u):
                    i, g = u // HG, u % HG
                    if u:
                        pe.wait_ge(s["qT_ready"], b * UNITS + u)
                    else:
                        pe.wait_ge(s["kv_read"], b * QT + QT)
                    for c in range(DC):
                        ins = nc.tensor.matmul(bank(6), xnT[:, c, i * P:(i + 1) * P], w_q[:, c, g * HG * DH:(g + 1) * HG * DH],
                                               start=c == 0, stop=c == DC - 1)
                    ins.then_inc(s["q_done"], 1)

                def turn_queries(u):
                    pe.wait_ge(s["q_rotated"], b * UNITS + (u + 2))
                    for j in range(HG):
                        ins = nc.tensor.transpose(bank(6)[:, j * P:(j + 1) * P], q_rot[:, j, :], ident)
                    ins.then_inc(s["q_turned"], 1)

                def scores(u, j):
                    i, n = u // HG, u * HG + j
                    if j == 0:
                        pe.wait_ge(s["qT_ready"], b * UNITS + (u + 1))
                    if n == 0:
                        pe.wait_ge(s["kT_ready"], b * QT + QT)
                    if n >= 2:
                        pe.wait_ge(s["exp_done"], b * NH + (n - 1))
                    keys = (i + 1) * P
                    for at in range(0, keys, 512):
                        end = min(keys, at + 512)
                        nc.tensor.matmul(score(n)[:, at:end], qT[u % 2][:, j, :], kT[:, at:end], start=True, stop=end < keys)
                    nc.tensor.matmul(score(n)[:, i * P:keys], ident_b, mask_b, start=False, stop=True).then_inc(s["s_done"], 1)

                def turn_probs(u, j):
                    i, n = u // HG, u * HG + j
                    pe.wait_ge(s["probs_ready"], b * NH + (n + 1))
                    for g in range(group_count(i)):
                        at = turned[n] + g
                        if at >= 2:
                            pe.wait_ge(s["pT_ready"], b * TURNED + at)
                        for m in range(4 * g, min(4 * g + 4, i + 1)):
                            ins = nc.tensor.transpose(bank(4 + at % 2)[:, (m - 4 * g) * P:(m - 4 * g + 1) * P],
                                                      probs[n % (2 * HG)][:, m * P:(m + 1) * P], ident)
                        ins.then_inc(s["p_turned"], 1)

                def values(u):
                    i = u // HG
                    pe.wait_ge(s["pT_ready"], b * TURNED + (turned[(u + 1) * HG] + 1))
                    if u:
                        pe.wait_ge(s["oT_ready"], b * UNITS + u)
                    if u and u % HG == 0:
                        pe.wait_ge(s["x_ready"], b * QT + (i + 1))
                    for m in range(i + 1):
                        ins = nc.tensor.matmul(bank(7), v[:, m, :], pT[:, m, :, :], start=m == 0, stop=m == i)
                    ins.then_inc(s["o_done"], 1)

                def project(i):
                    pe.wait_ge(s["oT_ready"], b * UNITS + (i + 1) * HG)
                    for hd in range(HEADS):
                        ins = nc.tensor.matmul(bank(7)[:, 0:D], oT[i % 2][:, hd, :], w_out[:, hd, :], start=hd == 0, stop=hd == HEADS - 1)
                    ins.then_inc(s["a_done"], 1)

                project_queries(0)
                turn_queries(0)
                for u in range(UNITS + 1):
                    for j in range(HG):
                        if u < UNITS:
                            scores(u, j)
                        if u:
                            turn_probs(u - 1, j)
                    if u + 1 < UNITS:
                        project_queries(u + 1)
                    if u:
                        values(u - 1)
                    if u + 1 < UNITS:
                        turn_queries(u + 1)
                    if u and u % HG == 0:
                        project(u // HG - 1)


def macaron(nc, dram):
    with ExitStack() as ctx:
        def sb(name, shape, dt=F32):
            return ctx.enter_context(nc.sbuf_tensor(name, shape, dt))

        const = sb("const", [P, CONST_COLS])
        ps = ctx.enter_context(nc.psum_tensor("ps", [P, 8 * 512], F32))
        env = {
            "dram": dram,
            "x": sb("x", [P, NT, D]),
            "const": const,
            "bank": lambda k: ps[:, k * 512:(k + 1) * 512],
            "bank2": lambda k: ps[:, k * 512:(k + 2) * 512],
            "ident": const[:, 0:P],
            "w_norm": sb("w_norm", [P, D]),
            "w_route": sb("w_route", [P, DC, E + 1]),
            "ws_gate": sb("ws_gate", [P, DC, FS]),
            "ws_up": sb("ws_up", [P, DC, FS]),
            "ws_down": sb("ws_down", [P, FT, D]),
            "w_q": sb("w_q", [P, DC, HEADS * DH]),
            "w_kv": sb("w_kv", [P, DC, 2 * DH]),
            "w_out": sb("w_out", [P, HEADS, D]),
            "xr_dram": nc.dram_tensor("xr_rows", [NT * P, D], F32, kind="Internal").ap(),
            "y_dram": nc.dram_tensor("expert_rows", [E * CAP, D], F32, kind="Internal").ap(),
        }
        for n in ("x_in", "w_in", "attn_w_in", "tables_ready"):
            env[n] = ctx.enter_context(nc.semaphore(n))
        for n in ("ones_b", "before_b", "ident_b", "mask_b"):
            env[n] = sb(n, [P, P], BF16)[:, :]
        loads(nc, env)
        ffn(nc, 0, env)
        attention(nc, env)
        ffn(nc, 1, env)


def loads(nc, env):
    dram = env["dram"]
    with nc.Block() as block:
        @block.sync
        def _(sp):
            rows = dram["x"].rearrange("(n t p) d -> n p t d", p=P, t=BLK)
            for blk in range(NB):
                sp.dma_start(env["x"][:, blk * BLK:(blk + 1) * BLK, :], rows[blk]).then_inc(env["x_in"], 16)
            n = 0
            for dst, src in (
                (env["const"][:, :], dram["const"]),
                (env["w_norm"][:, :], dram["w_norm"].rearrange("(o d) -> o d", o=1).to_broadcast([P, D])),
                (env["w_route"][:, :, 0:E], dram["w_router"].rearrange("(c p) e -> p c e", p=P)),
                (env["w_route"][:, :, E:E + 1], dram["w_shared_gate"].rearrange("(c p) e -> p c e", p=P)),
                (env["ws_gate"][:, :, :], dram["sw_gate"].rearrange("(c p) f -> p c f", p=P)),
                (env["ws_up"][:, :, :], dram["sw_up"].rearrange("(c p) f -> p c f", p=P)),
                (env["ws_down"][:, 0:FT - 1, :], dram["sw_down"][0:(FT - 1) * P].rearrange("(c p) f -> p c f", p=P)),
                (env["ws_down"][0:FS - (FT - 1) * P, FT - 1, :], dram["sw_down"][(FT - 1) * P:]),
            ):
                sp.dma_start(dst, src, allow_slow_non_contiguous=True).then_inc(env["w_in"], 16)
                n += 1
            env["w_loads"] = n
            for dst, src in (
                (env["w_q"][:, :, :], dram["Wq"].rearrange("(c p) f -> p c f", p=P)),
                (env["w_kv"][:, :, :], dram["Wkv"].rearrange("(c p) f -> p c f", p=P)),
                (env["w_out"][:, :, :], dram["Wout"].rearrange("(c p) f -> p c f", p=P)),
            ):
                sp.dma_start(dst, src).then_inc(env["attn_w_in"], 16)

        @block.gpsimd
        def _(pool):
            nc.gpsimd.memset(env["ones_b"], 1.0).then_inc(env["tables_ready"], 1)
            pool.wait_ge(env["w_in"], 16 * 8)
            for dst, src in (("before_b", "before"), ("ident_b", "ident"), ("mask_b", "mask")):
                at, n = CONST[src]
                nc.gpsimd.tensor_copy(env[dst], env["const"][:, at:at + n]).then_inc(env["tables_ready"], 1)


INPUTS = ("attn_x", "attn_Wq", "attn_Wkv", "attn_Wout", "ffn_w_norm", "ffn_w_router", "ffn_w_gate", "ffn_w_up",
          "ffn_w_down", "ffn_sw_gate", "ffn_sw_up", "ffn_sw_down", "ffn_w_shared_gate")


def kernel(**inputs):
    import concourse.bacc as bacc
    from concourse.bass_utils import run_bass_kernel_spmd

    nc = bacc.Bacc("TRN2", target_bir_lowering=False, num_devices=1)
    arrays = {f"in_{n}": np.ascontiguousarray(inputs[f"L0_{n}"]) for n in INPUTS}
    arrays["in_attn_x"] = arrays["in_attn_x"].reshape(BATCH * SEQ, D)
    arrays["in_all_const"] = constants()
    dram = {}
    for name, a in arrays.items():
        dram[name.split("_", 2)[-1]] = nc.dram_tensor(name, a.shape, mybir.dt.from_np(a.dtype), kind="ExternalInput").ap()
    dram["out"] = nc.dram_tensor("out", (BATCH * SEQ, D), F32, kind="ExternalOutput").ap()
    macaron(nc, dram)
    r = run_bass_kernel_spmd(nc, [arrays], core_ids=[0])
    return r.results[0]["out"].reshape(BATCH, SEQ, D)
```

```python
from contextlib import ExitStack

import numpy as np
import concourse.bass as bass
from concourse import mybir

F32 = mybir.dt.float32
F32R = mybir.dt.float32r
F16 = mybir.dt.float16
BF16 = mybir.dt.bfloat16
U32 = mybir.dt.uint32
ALU = mybir.AluOpType
ACT = mybir.ActivationFunctionType
AX = mybir.AxisListType.X

P = 128
BATCH, SEQ, D = 2, 1024, 256
NT = BATCH * SEQ // P
DC = D // P
BLK = 4
NB = NT // BLK
SBT = 256
SB = NT * P // SBT
EARLY = 3
LAG = 8
E, TOPK, FE, CAP = 32, 4, 176, 128
FH = FE // 2
FS = 704
FT = -(-FS // P)
HEADS, DH = 16, 128
HG = 4
SCALE = DH ** -0.5
QT = SEQ // P
UNITS = QT * HEADS // HG
STEPS = (("turn", 0), ("scores", 0), ("project_queries",), ("project",), ("turn", 1), ("scores", 1), ("turn", 2),
         ("values", 0), ("turn", 3), ("scores", 2), ("turn_queries",), ("scores", 3), ("values", 1))
HALVES = 2
HALF = DH // 2
RING = HG + 2
LN_EPS, RMS_EPS = 1e-5, 1e-6
W_LOADS = 4
MASKED = -3e38
EXP_ZERO = -87.3
FAR = 65536.0
MAGIC = 12582912.0
EG, AS, BS = 16, 8, 16

CONST = {}
_at = 0
for _name, _n in (("ident", P), ("mask", P), ("before", P), ("cos", QT * HALF), ("sin", QT * HALF),
                  ("cos_scaled", QT * HALF),
                  ("own", EG), ("expert", E), ("first_slot", E), ("sixteen", BS), ("token", NT)):
    CONST[_name] = (_at, _n)
    _at += _n
CONST_COLS = _at


def constants():
    c = np.zeros((P, CONST_COLS), np.float32)

    def put(name, value):
        at, n = CONST[name]
        c[:, at:at + n] = value

    p = np.arange(P)
    put("ident", np.eye(P))
    put("mask", np.where(p[None, :] > p[:, None], MASKED, 0.0))
    put("before", p[:, None] < p[None, :])
    inv = (1.0 / np.float32(10000.0) ** (np.arange(0, DH, 2, dtype=np.float32) / np.float32(DH))).astype(np.float32)
    pos = (np.arange(SEQ, dtype=np.float32)[:, None] * inv[None, :]).astype(np.float32)
    for name, f, scale in (("cos", np.cos, 1.0), ("sin", np.sin, 1.0), ("cos_scaled", np.cos, SCALE)):
        put(name, (f(pos).astype(np.float32) * np.float32(scale)).reshape(QT, P, HALF).transpose(1, 0, 2).reshape(P, QT * HALF))
    put("own", p[:, None] // AS == np.arange(EG)[None, :])
    put("expert", np.arange(E))
    put("first_slot", np.arange(E) * CAP)
    put("sixteen", np.arange(BS))
    put("token", p[:, None] + P * np.arange(NT)[None, :])
    return c


def one(i):
    return bass.ds(i, 1)


class Chain:

    def __init__(self, eng, sem):
        self.eng, self.sem, self.base, self.n = eng, sem, 0, 0

    def link(self, ins):
        self.n += 1
        ins.then_inc(self.sem, 1)
        self.eng.wait_ge(self.sem, self.base + self.n)

    def enter(self, i, links):
        self.start, self.links = self.base + self.n, links
        self.base, self.n = self.start + i * links, 0

    def leave(self, iterations):
        assert self.n == self.links, (self.n, self.links)
        self.base, self.n = self.start + iterations * self.links, 0


def split_matmul(nc, out, w, x, start, stop):
    (w_hi, w_lo), (x_hi, x_lo) = w, x
    nc.tensor.matmul(out, w_hi, x_hi, start=start, stop=False)
    nc.tensor.matmul(out, w_hi, x_lo, start=False, stop=False)
    return nc.tensor.matmul(out, w_lo, x_hi, start=False, stop=stop)


def ffn(nc, layer, env):
    ctx = ExitStack()

    def sb(name, shape, dt):
        return ctx.enter_context(nc.sbuf_tensor(f"{name}_{layer}", shape, dt))

    semaphores = []

    def sem(name):
        semaphores.append(nc.alloc_semaphore(name=f"{name}_{layer}"))
        return semaphores[-1]

    with ctx:
        x, const, bank = env["x"], env["const"], env["bank"]
        ident, ones_b, before_b = env["ident"], env["ones_b"], env["before_b"]
        w_norm, w_route = env["w_norm"], env["w_route"]
        xr_dram, y_dram = env["xr_dram"], env["y_dram"]
        dram = env["dram"]

        h = sb("h", [P, NT, D], F32)
        xT = [sb(f"xT{k}", [P, DC, NT * P], F32R) for k in range(2)]
        place = env["place"]
        GU, DOWN = 4 * DC * FE, 8 * D
        xTf = place[:, 2 * GU + DOWN:2 * GU + DOWN + DC * BLK * P].rearrange("p (c t) -> p c t", c=DC)
        xr = [sb(f"xr{k}", [P, BLK, D], F32) for k in range(2)]
        stats = env["stats"]
        mv = sb("mv", [P, NT, 2], F32)
        half_p = sb("half_p", [P, NT], F32)
        ve = sb("ve", [P, NT], F32)
        rstd = sb("rstd", [P, NT], F32)
        shift = sb("shift", [P, NT], F32)
        msq = sb("msq", [P, NT], F32)
        rrms = sb("rrms", [P, NT], F32)
        logitsT = [sb(f"logitsT{k}", [E + 1, BLK * P], F32) for k in range(2)]
        logits = sb("logits", [P, NT, E + 1], F32)
        top = sb("top", [P, NT], F32)
        diff = sb("diff", [P, NT, E], F32)
        key = sb("key", [P, NT, E], F32)
        probs = sb("probs", [P, NT, E], F32)
        sig = sb("sig", [P, NT], F32)
        val8 = sb("val8", [P, NT, 8], F32)
        idx8 = sb("idx8", [P, NT, 8], U32)
        idxf = sb("idxf", [P, NT, TOPK], F32)
        onehot = sb("onehot", [P, NT, TOPK, E], BF16)
        chosen2 = sb("chosen2", [P, NT, 2, E], BF16)
        chosen = sb("chosen", [P, NT, E], BF16)
        den = sb("den", [P, NT], F32)
        wk = sb("wk", [P, NT, TOPK], F32)
        late = diff
        slot = sb("slot", [P, NT, E], F32)
        slotk = sb("slotk", [P, NT, TOPK], F32)
        slotu = sb("slotu", [P, NT * TOPK], U32)
        row_a = probs
        row_ah = sb("row_ah", [P, NT, E], F16)
        row_bh = sb("row_bh", [P, NT, E], F16)
        hot_a = sb("hot_a", [P, NT, EG, AS], F16)
        hot_b = sb("hot_b", [P, NT, EG, BS], F16)
        picked = hot_b[:, :, :, :].rearrange("p t e b -> p (t e b)").bitcast(F32)\
            .rearrange("p (t k e) -> p t k e", t=NT, k=TOPK)
        sixteen_h = sb("sixteen_h", [P, BS], F16)
        token_h = sb("token_h", [P, NT], F16)
        table_own = sb("table_own", [P, 2, EG, BS], F32)
        table = sb("table", [P, 2, BS], F32)
        tableT = sb("tableT", [BS, AS, E], U32)
        source = sb("source", [P, E], U32)
        ws_gate = [sb(f"ws_gate{k}", [P, DC, FT * P], F32R) for k in range(2)]
        ws_up = [sb(f"ws_up{k}", [P, DC, FT * P], F32R) for k in range(2)]
        ws_down = [sb(f"ws_down{k}", [P, FT, D], F32R) for k in range(2)]
        s_gate = [sb(f"s_gate{k}", [P, SBT], F32) for k in range(2)]
        s_upc = [sb(f"s_upc{k}", [P, SBT], F32) for k in range(2)]
        s_val = [sb(f"s_val{k}", [P, SBT], F32) for k in range(2)]
        s_hid = [sb(f"s_hid{k}", [P, FT, SBT], F32R) for k in range(2)]
        s_sum = [sb(f"s_sum{k}", [P, D], F32) for k in range(2)]
        we_gu = [place[:, k * GU:(k + 1) * GU].rearrange("p (e c g f) -> p e c g f", e=2, c=DC, g=2) for k in range(2)]
        we_down = place[:, 2 * GU:2 * GU + DOWN].rearrange("p (k e c d) -> p k e c d", k=2, e=2, c=2)
        xe = [sb(f"xe{k}", [P, D], F32) for k in range(4)]
        xeT = [s_upc[k][:, :].rearrange("p (c t) -> p c t", c=DC) for k in range(2)]
        e_gate = [key[:, :, :].rearrange("p t e -> p (t e)")[:, k * FE:(k + 1) * FE] for k in range(2)]
        e_hid = [table_own[:, :, :, :].rearrange("p g e b -> p (g e b)")[:, k * FE:(k + 1) * FE] for k in range(2)]
        e_hidT = [s_sum[k][0:FH, :].rearrange("p (c t) -> p c t", c=2) for k in range(2)]
        ye = [hot_a[:, 4 * k:4 * k + 4, :, :].rearrange("p t e a -> p (t e a)").bitcast(F32) for k in range(4)]
        back = [xr[0][:, :, :], xr[1][:, :, :], xTf[:, :, :].rearrange("p c (a d) -> p (c a) d", d=D),
                onehot[:, :, :, :].rearrange("p t k e -> p (t k e)").bitcast(F32).rearrange("p (k d) -> p k d", k=TOPK)]

        raw_gate = we_gu[0][:, :, :, :, :].rearrange("p e c g f -> p (e c g f)").rearrange("p (c f) -> p c f", c=DC)
        raw_up = we_gu[1][:, :, :, :, :].rearrange("p e c g f -> p (e c g f)").rearrange("p (c f) -> p c f", c=DC)
        raw_down = we_down[:, :, :, :, :].rearrange("p k e c d -> p (k e c) d")[:, 0:FT, :]
        LAST = FS - (FT - 1) * P

        def col(name):
            at, n = CONST[name]
            return const[:, at:at + n]

        names = ("moments mv_ready ve_ready rstd_ready msq_ready rrms_ready pool_own h_ready xr_ready xr_turned xTf_ready "
                 "xT_hi xT_lo xTf_used "
                 "rT_done rT_copied r_done r_copied diff_ready val_ready exps_ready sig_ready chosen_ready pos_done "
                 "hots_ready table_done table_ready tableT_done tableT_ready source_ready slots_ready "
                 "ws_in ws_zero ws_ready sg_done sg_act su_copied s_val_ready s_hi s_lo so_done so_copied so_used row_added back_used out_ready "
                 "xeT_turned xeT_ready gu_done e_act e_hid_ready e_hid_turned e_hidT_ready y_done ye_ready dve_own out_done").split()
        s = {n: sem(n) for n in names}
        xr_saved = [sem(f"xr_saved{k}") for k in range(2)]
        we_in = [sem(f"we_in{k}") for k in range(2)]
        xe_in = [sem(f"xe_in{k}") for k in range(4)]
        ye_out = [sem(f"ye_out{k}") for k in range(4)]
        back_in = [sem(f"back_in{k}") for k in range(4)]

        def load_pair(sp, pair, k):
            g = dram["w_gate"].rearrange("(n e) (c p) f -> n p e c f", e=2, p=P)
            u = dram["w_up"].rearrange("(n e) (c p) f -> n p e c f", e=2, p=P)
            d = dram["w_down"].rearrange("(n e) (c p) f -> n p e c f", e=2, p=FH)
            for q in range(2):
                sp.dma_start(we_gu[k][:, q, :, 0, :], g[one(pair), :, q].rearrange("n p c f -> (n p) c f")).then_inc(we_in[k], 16)
                sp.dma_start(we_gu[k][:, q, :, 1, :], u[one(pair), :, q].rearrange("n p c f -> (n p) c f")).then_inc(we_in[k], 16)
                sp.dma_start(we_down[0:FH, k, q], d[one(pair), :, q].rearrange("n p c f -> (n p) c f")).then_inc(we_in[k], 16)

        block = ctx.enter_context(nc.Block())

        @block.sync
        def _(sp):
            for k in range(4):
                sp.sem_inc(ye_out[k], 16)
            if layer == 0:
                load_all(sp, env)
            sp.dma_start(raw_gate, dram["sw_gate"].rearrange("(c p) f -> p c f", p=P)).then_inc(s["ws_in"], 16)
            sp.dma_start(raw_up, dram["sw_up"].rearrange("(c p) f -> p c f", p=P)).then_inc(s["ws_in"], 16)
            sp.dma_start(raw_down[:, 0:FT - 1, :], dram["sw_down"][0:(FT - 1) * P].rearrange("(c p) f -> p c f", p=P)).then_inc(s["ws_in"], 16)
            sp.dma_start(raw_down[0:LAST, FT - 1, :], dram["sw_down"][(FT - 1) * P:]).then_inc(s["ws_in"], 16)
            xr_rows = xr_dram.rearrange("(n t p) d -> n p t d", p=P, t=BLK)
            for blk in range(NB):
                sp.wait_ge(s["xr_ready"], BLK * (blk + 1))
                sp.dma_start(xr_rows[blk], xr[blk % 2][:, :, :]).then_inc(xr_saved[blk % 2], 16)
            sp.wait_ge(s["ws_ready"], 4)
            for k in range(2):
                load_pair(sp, k, k)
            sp.wait_ge(s["tableT_ready"], 2)
            for a in range(AS):
                sp.dma_start(source[a * BS:(a + 1) * BS, :], tableT[:, a, :]).then_inc(s["source_ready"], 16)

            y_rows = y_dram.rearrange("(e c) d -> e c d", c=CAP)

            def store_y(e, k):
                sp.wait_ge(s["ye_ready"], e + 3)
                sp.dma_start(y_rows[one(e)].rearrange("e c d -> (e c) d"), ye[k]).then_inc(ye_out[k], 16)

            with sp.Fori(0, E // 4 - 1) as it:
                for q in range(4):
                    store_y(it * 4 + q, q)
                    if q % 2:
                        sp.wait_ge(s["y_done"], it * 4 + q + 1)
                        load_pair(sp, it * 2 + q // 2 + 2, q // 2)
            for q in range(4):
                store_y(E - 4 + q, q)
            if layer == 0:
                sp.wait_ge(s["y_done"], E)
                sp.dma_start(env["raw_kv"], dram["Wkv"].rearrange("(c p) f -> p c f", p=P)).then_inc(env["kv_in"], 16)
                sp.dma_start(env["raw_q"], dram["Wq"].rearrange("(c p) f -> p c f", p=P)).then_inc(env["q_in"], 16)
            if layer == 1:
                out_rows = dram["out"].rearrange("(n p) d -> n p d", p=P)
                with sp.Fori(0, NT) as t:
                    sp.wait_ge(s["out_ready"], t + 1)
                    sp.dma_start(out_rows[one(t)].rearrange("n p d -> (n p) d"),
                                 x[:, one(t), :].rearrange("p n d -> p (n d)")).then_inc(s["out_done"], 16)
                sp.wait_ge(s["out_done"], 16 * NT)
            for k in range(4):
                sp.wait_ge(ye_out[k], 16 * E // 4 + 16)

        @block.gpsimd
        def _(pool):
            if layer == 0:
                make_tables(nc, pool, env)
            nc.gpsimd.memset(half_p[:, :], -0.5).then_inc(s["pool_own"], 1)
            for w in (ws_gate, ws_up):
                for k in range(2):
                    nc.gpsimd.memset(w[k][:, :, FS:].bitcast(F32), 0.0).then_inc(s["ws_zero"], 1)
            for k in range(2):
                nc.gpsimd.memset(ws_down[k][:, FT - 1, :].bitcast(F32), 0.0).then_inc(s["ws_zero"], 1)
            pool.wait_ge(s["pool_own"], 1)
            order = [(0, 0), (0, 1), (1, 0), (0, 2), (1, 1), (0, 3), (1, 2), (1, 3)]
            for norm, blk in order:
                b = slice(blk * BLK, (blk + 1) * BLK)
                if norm == 0:
                    pool.wait_ge(s["ve_ready"], blk + 1)
                    nc.gpsimd.tensor_tensor(rstd[:, b], ve[:, b], half_p[:, b], ALU.pow).then_inc(s["rstd_ready"], 1)
                else:
                    pool.wait_ge(s["msq_ready"], blk + 1)
                    nc.gpsimd.tensor_tensor(rrms[:, b], msq[:, b], half_p[:, b], ALU.pow).then_inc(s["rrms_ready"], 1)
            pool.wait_ge(s["ws_in"], 16 * 4)
            parts = ((ws_gate, raw_gate, slice(0, P), slice(0, DC), slice(0, FS)), (ws_up, raw_up, slice(0, P), slice(0, DC), slice(0, FS)),
                     (ws_down, raw_down, slice(0, P), slice(0, FT - 1), slice(0, D)), (ws_down, raw_down, slice(0, LAST), slice(FT - 1, FT), slice(0, D)))
            pool.wait_ge(s["ws_zero"], 6)
            for n, (w, raw, p, c, f) in enumerate(parts):
                if n:
                    pool.wait_ge(s["ws_ready"], n)
                nc.gpsimd.tensor_copy(w[0][p, c, f], raw[p, c, f]).then_inc(s["pool_own"], 1)
                pool.wait_ge(s["pool_own"], n + 2)
                nc.gpsimd.tensor_tensor(w[1][p, c, f], raw[p, c, f], w[0][p, c, f].bitcast(F32), ALU.subtract).then_inc(s["ws_ready"], 1)

            def early_hidden(blk):
                for f in range(FT):
                    n = blk * FT + f
                    pool.wait_ge(s["su_copied"], n + 1)
                    nc.gpsimd.tensor_tensor(s_val[n % 2][:, :], s_gate[n % 2][:, :], s_upc[n % 2][:, :], ALU.mult).then_inc(s["s_val_ready"], 1)
                    pool.wait_ge(s["s_hi"], n + 1)
                    nc.gpsimd.tensor_tensor(s_hid[1][:, f, :], s_val[n % 2][:, :], s_hid[0][:, f, :].bitcast(F32),
                                            ALU.subtract).then_inc(s["s_lo"], 1)

            def early_sum(blk):
                for q in range(SBT // P):
                    t = blk * (SBT // P) + q
                    pool.wait_ge(s["so_copied"], t + 1)
                    nc.gpsimd.tensor_tensor(h[:, t, :], h[:, t, :], s_sum[t % 2][:, :], ALU.add).then_inc(s["so_used"], 1)

            for blk in range(EARLY):
                early_hidden(blk)
                if blk:
                    early_sum(blk - 1)
            early_sum(EARLY - 1)

            for k in range(2):
                pool.wait_ge(xr_saved[k], 16 * NB // 2)
            pool.wait_ge(s["source_ready"], 16 * AS)
            for e in range(E):
                k = e % 4
                if e >= 4:
                    pool.wait_ge(s["xeT_turned"], e - 3)
                nc.gpsimd.indirect_dma_start(xe[k][:, :], None, xr_dram[:, :],
                                             bass.IndirectOffsetOnAxis(source[:, e:e + 1], 0)).then_inc(xe_in[k], 16)
            for k in range(4):
                pool.wait_ge(ye_out[k], 16 * E // 4 + 16)
            pool.wait_ge(s["slots_ready"], 1)
            for t in range(NT):
                k = t % 4
                if t >= 4:
                    pool.wait_ge(s["back_used"], t - 3)
                for j in range(TOPK):
                    n = t * TOPK + j
                    nc.gpsimd.indirect_dma_start(back[k][:, j, :], None, y_dram[:, :],
                                                 bass.IndirectOffsetOnAxis(slotu[:, n:n + 1], 0),
                                                 bounds_check=E * CAP - 1, oob_is_err=False).then_inc(back_in[k], 16)

        @block.scalar
        def _(act):
            act.sem_inc(s["xeT_ready"], 2)
            act.sem_inc(s["e_hidT_ready"], 2)
            def normal_rows(blk):
                act.wait_ge(s["rstd_ready"], blk + 1)
                act.wait_ge(s["msq_ready"], blk + 1)
                for q in range(BLK):
                    t = blk * BLK + q
                    nc.scalar.activation(h[:, t, :], x[:, t, :], ACT.Identity, bias=shift[:, t:t + 1],
                                         scale=rstd[:, t:t + 1]).then_inc(s["h_ready"], 1)

            def turned_rows(blk):
                b = slice(blk * BLK * P, (blk + 1) * BLK * P)
                if blk:
                    act.wait_ge(s["rT_done"], blk)
                    act.wait_ge(s["xT_lo"], DC * blk)
                for c in range(DC):
                    act.wait_ge(s["xr_turned"], DC * blk + c + 1)
                    nc.scalar.copy(xTf[:, c, :], bank(c)).then_inc(s["xTf_ready"], 1)
                for c in range(DC):
                    nc.scalar.copy(xT[0][:, c, b], bank(c)).then_inc(s["xT_hi"], 1)
                act.wait_ge(s["rT_done"], blk + 1)
                nc.scalar.copy(logitsT[blk % 2][:, :], bank(6)[0:E + 1, :]).then_inc(s["rT_copied"], 1)

            normal_rows(0)
            normal_rows(1)
            for blk in range(NB):
                if blk + 2 < NB:
                    normal_rows(blk + 2)
                turned_rows(blk)
            act.wait_ge(s["r_copied"], NB)
            nc.scalar.activation(sig[:, :], logits[:, :, E], ACT.Exp, scale=-1.0).then_inc(s["exps_ready"], 1)
            act.wait_ge(s["diff_ready"], 1)
            nc.scalar.activation(probs[:, :, :], diff[:, :, :], ACT.Exp).then_inc(s["exps_ready"], 1)
            act.wait_ge(s["val_ready"], 1)
            nc.scalar.activation(wk[:, :, :], val8[:, :, 0:TOPK], ACT.Exp).then_inc(s["exps_ready"], 1)

            def shared_gates(blk):
                for f in range(FT):
                    n = blk * FT + f
                    gu = bank(2 + n % 4).rearrange("p (g t) -> p g t", g=2)
                    act.wait_ge(s["sg_done"], n + 1)
                    if n >= 2:
                        act.wait_ge(s["s_val_ready"], n - 1)
                    nc.scalar.activation(s_gate[n % 2][:, :], gu[:, 0, :], ACT.Silu).then_inc(s["sg_act"], 1)
                    if blk < EARLY:
                        nc.scalar.copy(s_upc[n % 2][:, :], gu[:, 1, :]).then_inc(s["su_copied"], 1)
                    act.wait_ge(s["s_val_ready"], n + 1)
                    if f == 0 and blk:
                        act.wait_ge(s["so_done"], blk * (SBT // P))
                    nc.scalar.copy(s_hid[0][:, f, :], s_val[n % 2][:, :]).then_inc(s["s_hi"], 1)

            def early_out(blk):
                for q in range(SBT // P):
                    t = blk * (SBT // P) + q
                    act.wait_ge(s["so_done"], t + 1)
                    act.wait_ge(s["sig_ready"], 1)
                    if t >= 2:
                        act.wait_ge(s["so_used"], t - 1)
                    nc.scalar.activation(s_sum[t % 2][:, :], bank(6 + t % 2)[:, 0:D], ACT.Copy,
                                         scale=sig[:, t:t + 1]).then_inc(s["so_copied"], 1)

            for blk in range(EARLY):
                shared_gates(blk)
                early_out(blk)
            with act.Fori(0, E // 4) as it:
                def turned_expert(q):
                    act.wait_ge(s["xeT_turned"], it * 4 + q + 1)
                    nc.scalar.copy(xeT[q % 2][:, :, :], bank(q % 2)[:, 0:DC * P].rearrange("p (c t) -> p c t", c=DC)).then_inc(s["xeT_ready"], 1)

                turned_expert(0)
                for q in range(4):
                    if q < 3:
                        turned_expert(q + 1)
                    act.wait_ge(s["gu_done"], it * 4 + q + 1)
                    nc.scalar.activation(e_gate[q % 2][:, :], bank(2 + q % 2)[:, 0:FE], ACT.Silu).then_inc(s["e_act"], 1)
                    act.wait_ge(s["e_hid_turned"], it * 4 + q + 1)
                    nc.scalar.copy(e_hidT[q % 2][:, :, :], bank(6 + q % 2)[0:FH, 0:2 * P].rearrange("p (c t) -> p c t", c=2)).then_inc(s["e_hidT_ready"], 1)
            for blk in range(EARLY, SB):
                shared_gates(blk)

        @block.vector
        def _(dve):
            own = Chain(dve, s["dve_own"])
            link = own.link
            dve.sem_inc(s["e_hid_ready"], 2)
            dve.sem_inc(s["ye_ready"], 2)

            def moments(blk):
                b = slice(blk * BLK, (blk + 1) * BLK)
                if layer == 0:
                    dve.wait_ge(env["x_in"][blk], 16)
                    for t in range(blk * BLK, (blk + 1) * BLK):
                        ins = nc.vector.bn_stats(stats[:, t, :], x[:, t, :])
                    link(ins)
                for t in range(blk * BLK, (blk + 1) * BLK):
                    ins = nc.vector.bn_aggr(mv[:, t, :], stats[:, t, :])
                link(ins)
                nc.vector.tensor_scalar(ve[:, b], mv[:, b, 1], LN_EPS, None, ALU.add).then_inc(s["ve_ready"], 1)

            def mean_squares(blk):
                b = slice(blk * BLK, (blk + 1) * BLK)
                dve.wait_ge(s["rstd_ready"], blk + 1)
                link(nc.vector.tensor_tensor(msq[:, b], mv[:, b, 1], rstd[:, b], ALU.mult))
                nc.vector.scalar_tensor_tensor(shift[:, b], mv[:, b, 0], -1.0, rstd[:, b], ALU.mult, ALU.mult)
                link(nc.vector.tensor_tensor(msq[:, b], msq[:, b], rstd[:, b], ALU.mult))
                nc.vector.tensor_scalar(msq[:, b], msq[:, b], RMS_EPS, None, ALU.add).then_inc(s["msq_ready"], 1)

            def rows(blk):
                dve.wait_ge(s["rrms_ready"], blk + 1)
                if layer == 0 and blk == 0:
                    dve.wait_ge(env["w_in"], 16 * W_LOADS)
                if blk >= 2:
                    dve.wait_ge(s["xr_turned"], DC * (blk - 1))
                    dve.wait_ge(xr_saved[blk % 2], 16 * (blk // 2))
                for q in range(BLK):
                    t = blk * BLK + q
                    dve.wait_ge(s["h_ready"], t + 1)
                    nc.vector.scalar_tensor_tensor(xr[blk % 2][:, q, :], h[:, t, :], rrms[:, t:t + 1], w_norm[:, :],
                                                   ALU.mult, ALU.mult).then_inc(s["xr_ready"], 1)

            def turned(blk):
                b = slice(blk * BLK * P, (blk + 1) * BLK * P)
                for c in range(DC):
                    dve.wait_ge(s["xT_hi"], DC * blk + c + 1)
                    nc.vector.tensor_tensor(xT[1][:, c, b], xTf[:, c, :], xT[0][:, c, b].bitcast(F32),
                                            ALU.subtract).then_inc(s["xT_lo"], 1)
                dve.wait_ge(s["r_done"], blk + 1)
                nc.vector.tensor_copy(logits[:, blk * BLK:(blk + 1) * BLK, :],
                                      bank(7)[:, 0:BLK * (E + 1)].rearrange("p (t e) -> p t e", t=BLK)).then_inc(s["r_copied"], 1)

            moments(0)
            moments(1)
            mean_squares(0)
            moments(2)
            mean_squares(1)
            rows(0)
            moments(3)
            mean_squares(2)
            rows(1)
            mean_squares(3)
            turned(0)
            rows(2)
            turned(1)
            rows(3)
            turned(2)
            turned(3)
            dve.wait_ge(s["r_copied"], NB)
            link(nc.vector.reduce_max(top[:, :], logits[:, :, 0:E], axis=AX))
            nc.vector.tensor_tensor(diff[:, :, :], logits[:, :, 0:E], top[:, :].unsqueeze(2).to_broadcast([P, NT, E]),
                                    ALU.subtract).then_inc(s["diff_ready"], 1)
            dve.wait_ge(s["diff_ready"], 1)
            link(nc.vector.tensor_scalar(key[:, :, :], diff[:, :, :], EXP_ZERO, None, ALU.max))
            for t in range(NT):
                ins = nc.vector.max(val8[:, t, :], key[:, t, :])
            ins.then_inc(s["val_ready"], 1)
            dve.wait_ge(s["val_ready"], 1)
            for t in range(NT):
                ins = nc.vector.max_index(idx8[:, t, :], val8[:, t, :], key[:, t, :])
            link(ins)
            link(nc.vector.tensor_copy(idxf[:, :, :], idx8[:, :, 0:TOPK]))
            link(nc.vector.tensor_tensor(onehot[:, :, :, :], col("expert").unsqueeze(1).unsqueeze(1).to_broadcast([P, NT, TOPK, E]),
                                         idxf[:, :, :].unsqueeze(3).to_broadcast([P, NT, TOPK, E]), ALU.is_equal))
            link(nc.vector.tensor_tensor(chosen2[:, :, :, :], onehot[:, :, 0:2, :], onehot[:, :, 2:4, :], ALU.add))
            nc.vector.tensor_tensor(chosen[:, :, :], chosen2[:, :, 0, :], chosen2[:, :, 1, :], ALU.add).then_inc(s["chosen_ready"], 1)
            dve.wait_ge(s["exps_ready"], 3)
            link(nc.vector.tensor_scalar(sig[:, :], sig[:, :], 1.0, None, ALU.add))
            nc.vector.reciprocal(sig[:, :], sig[:, :]).then_inc(s["sig_ready"], 1)
            link(nc.vector.reduce_sum(den[:, :], probs[:, :, :], axis=AX))
            link(nc.vector.reciprocal(den[:, :], den[:, :]))
            link(nc.vector.tensor_tensor(wk[:, :, :], wk[:, :, :], den[:, :].unsqueeze(2).to_broadcast([P, NT, TOPK]), ALU.mult))
            nc.vector.tensor_copy(sixteen_h[:, :], col("sixteen"))
            link(nc.vector.tensor_copy(token_h[:, :], col("token")))
            pos = bank(0).rearrange("p (t e) -> p t e", t=NT)
            dve.wait_ge(s["chosen_ready"], 1)
            dve.wait_ge(s["pos_done"], 1)
            link(nc.vector.tensor_scalar(late[:, :, :], pos, float(CAP), FAR, ALU.is_ge, ALU.mult))
            link(nc.vector.tensor_tensor(late[:, :, :], pos, late[:, :, :], ALU.add))
            link(nc.vector.scalar_tensor_tensor(key[:, :, :], chosen[:, :, :], -FAR, late[:, :, :], ALU.mult, ALU.add))
            link(nc.vector.tensor_scalar(key[:, :, :], key[:, :, :], FAR, 1024.0, ALU.add, ALU.min))
            link(nc.vector.tensor_scalar(row_a[:, :, :], key[:, :, :], 1.0 / BS, -0.46875, ALU.mult, ALU.add))
            link(nc.vector.tensor_scalar(row_a[:, :, :], row_a[:, :, :], MAGIC, -MAGIC, ALU.add, ALU.add))
            link(nc.vector.tensor_copy(row_ah[:, :, :], row_a[:, :, :]))
            link(nc.vector.scalar_tensor_tensor(row_bh[:, :, :], row_a[:, :, :], -float(BS), key[:, :, :], ALU.mult, ALU.add))
            for g in range(2):
                eg = slice(g * EG, (g + 1) * EG)
                if g:
                    dve.wait_ge(s["table_done"], g)
                link(nc.vector.tensor_tensor(hot_a[:, :, :, :], row_ah[:, :, eg].unsqueeze(3).to_broadcast([P, NT, EG, AS]),
                                             sixteen_h[:, 0:AS].unsqueeze(1).unsqueeze(1).to_broadcast([P, NT, EG, AS]), ALU.is_equal))
                link(nc.vector.tensor_tensor(hot_a[:, :, :, :], hot_a[:, :, :, :],
                                             token_h[:, :].unsqueeze(2).unsqueeze(2).to_broadcast([P, NT, EG, AS]), ALU.mult))
                nc.vector.tensor_tensor(hot_b[:, :, :, :], row_bh[:, :, eg].unsqueeze(3).to_broadcast([P, NT, EG, BS]),
                                        sixteen_h[:, :].unsqueeze(1).unsqueeze(1).to_broadcast([P, NT, EG, BS]),
                                        ALU.is_equal).then_inc(s["hots_ready"], 1)
            dve.wait_ge(s["table_done"], 2)
            tab = bank(1).rearrange("p (g e b) -> p g e b", g=2, e=EG)
            link(nc.vector.tensor_tensor(table_own[:, :, :, :], tab,
                                         col("own").unsqueeze(1).unsqueeze(3).to_broadcast([P, 2, EG, BS]), ALU.mult))
            nc.vector.reduce_sum(table[:, :, :], table_own[:, :, :, :].rearrange("p g e b -> p g b e"), axis=AX).then_inc(s["table_ready"], 1)
            dve.wait_ge(s["tableT_done"], 1)
            for g in range(2):
                nc.vector.tensor_copy(tableT[:, :, g * EG:(g + 1) * EG],
                                      bank(1)[0:BS, g * P:(g + 1) * P].rearrange("b (e a) -> b a e", e=EG)).then_inc(s["tableT_ready"], 1)
            link(nc.vector.tensor_tensor(slot[:, :, :], late[:, :, :],
                                         col("first_slot").unsqueeze(1).to_broadcast([P, NT, E]), ALU.add))
            link(nc.vector.tensor_tensor(picked, onehot[:, :, :, :],
                                         slot[:, :, :].unsqueeze(2).to_broadcast([P, NT, TOPK, E]), ALU.mult))
            link(nc.vector.reduce_sum(slotk[:, :, :], picked, axis=AX))
            nc.vector.tensor_copy(slotu[:, :].rearrange("p (t k) -> p t k", k=TOPK), slotk[:, :, :]).then_inc(s["slots_ready"], 1)
            link(nc.vector.scalar_tensor_tensor(wk[:, :, :], slotk[:, :, :], float(E * CAP), wk[:, :, :], ALU.is_lt, ALU.mult))

            with dve.Fori(0, E // 4) as it:
                def rows_out(q):
                    e = it * 4 + q
                    dve.wait_ge(s["y_done"], e + 1)
                    dve.wait_ge(ye_out[q], it * 16 + 16)
                    nc.vector.tensor_copy(ye[q], bank(4 + q % 2)[:, 0:D]).then_inc(s["ye_ready"], 1)

                for q in range(4):
                    e = it * 4 + q
                    dve.wait_ge(s["e_act"], e + 1)
                    nc.vector.tensor_tensor(e_hid[q % 2][:, :], bank(2 + q % 2)[:, FE:2 * FE], e_gate[q % 2][:, :],
                                            ALU.mult).then_inc(s["e_hid_ready"], 1)
                    if q:
                        rows_out(q - 1)
                rows_out(3)

            def late_hidden(blk, f):
                n = blk * FT + f
                dve.wait_ge(s["sg_act"], n + 1)
                nc.vector.tensor_tensor(s_val[n % 2][:, :], bank(2 + n % 4)[:, SBT:2 * SBT], s_gate[n % 2][:, :],
                                        ALU.mult).then_inc(s["s_val_ready"], 1)
                dve.wait_ge(s["s_hi"], n + 1)
                nc.vector.tensor_tensor(s_hid[1][:, f, :], s_val[n % 2][:, :], s_hid[0][:, f, :].bitcast(F32),
                                        ALU.subtract).then_inc(s["s_lo"], 1)

            def combine(n):
                t, j = divmod(n, TOPK)
                if j == 0:
                    dve.wait_ge(back_in[t % 4], 16 * TOPK * (t // 4 + 1))
                else:
                    dve.wait_ge(s["row_added"], n - t)
                ins = nc.vector.scalar_tensor_tensor(h[:, t, :], back[t % 4][:, j, :], wk[:, t, j:j + 1], h[:, t, :], ALU.mult, ALU.add)
                ins.then_inc(s["row_added" if j < TOPK - 1 else "back_used"], 1)

            def close(t):
                nc.vector.scalar_tensor_tensor(x[:, t, :], h[:, t, :], 0.5, x[:, t, :], ALU.mult, ALU.add).then_inc(s["out_ready"], 1)

            def moments_of(t, closed):
                if layer == 0:
                    dve.wait_ge(s["out_ready"], closed)
                    nc.vector.bn_stats(stats[:, t, :], x[:, t, :])

            dve.wait_ge(s["so_used"], EARLY * (SBT // P))
            n, closed, summed = -LAG, 0, EARLY * (SBT // P)

            def step():
                nonlocal n
                if 0 <= n < NT * TOPK:
                    combine(n)
                n += 1

            def close_all():
                nonlocal closed
                first = closed
                while closed < summed and (closed + 1) * TOPK <= n:
                    dve.wait_ge(s["back_used"], closed + 1)
                    close(closed)
                    closed += 1
                for t in range(first, closed):
                    moments_of(t, t + 1)

            for blk in range(EARLY, SB):
                for f in range(FT):
                    m = blk * FT + f
                    dve.wait_ge(s["sg_act"], m + 1)
                    nc.vector.tensor_tensor(s_val[m % 2][:, :], bank(2 + m % 4)[:, SBT:2 * SBT], s_gate[m % 2][:, :],
                                            ALU.mult).then_inc(s["s_val_ready"], 1)
                    step()
                    dve.wait_ge(s["s_hi"], m + 1)
                    nc.vector.tensor_tensor(s_hid[1][:, f, :], s_val[m % 2][:, :], s_hid[0][:, f, :].bitcast(F32),
                                            ALU.subtract).then_inc(s["s_lo"], 1)
                    step()
                if n >= TOPK:
                    dve.wait_ge(s["back_used"], n // TOPK)
                if n > 0:
                    dve.wait_ge(s["row_added"], n - n // TOPK)
                for t in range(summed, summed + SBT // P):
                    dve.wait_ge(s["so_done"], t + 1)
                    nc.vector.scalar_tensor_tensor(h[:, t, :], bank(6 + t % 2)[:, 0:D], sig[:, t:t + 1], h[:, t, :],
                                                   ALU.mult, ALU.add).then_inc(s["so_used"], 1)
                summed += SBT // P
                dve.wait_ge(s["so_used"], summed)
                step()
                step()
                close_all()
            while closed < NT:
                step()
                close_all()

        @block.tensor
        def _(pe):
            if layer == 0:
                pe.wait_ge(env["w_in"], 16 * W_LOADS)
                pe.wait_ge(env["tables_ready"], 4)
            for blk in range(NB):
                pe.wait_ge(s["xr_ready"], BLK * (blk + 1))
                if blk:
                    pe.wait_ge(s["xT_hi"], DC * blk)
                for c in range(DC):
                    for q in range(BLK):
                        ins = nc.tensor.transpose(bank(c)[:, q * P:(q + 1) * P], xr[blk % 2][:, q, c * P:(c + 1) * P], ident)
                    ins.then_inc(s["xr_turned"], 1)
                pe.wait_ge(s["xTf_ready"], DC * (blk + 1))
                if blk:
                    pe.wait_ge(s["rT_copied"], blk)
                for c in range(DC):
                    ins = nc.tensor.matmul(bank(6)[0:E + 1, :], w_route[:, c, :], xTf[:, c, :], start=c == 0, stop=c == DC - 1)
                ins.then_inc(s["rT_done"], 1)
                pe.wait_ge(s["rT_copied"], blk + 1)
                if blk:
                    pe.wait_ge(s["r_copied"], blk)
                for q in range(BLK):
                    ins = nc.tensor.transpose(bank(7)[:, q * (E + 1):(q + 1) * (E + 1)], logitsT[blk % 2][:, q * P:(q + 1) * P],
                                              ident[0:E + 1, 0:E + 1])
                ins.then_inc(s["r_done"], 1)

            def shared_in(blk):
                b = slice(blk * SBT, (blk + 1) * SBT)
                pe.wait_ge(s["xT_lo"], DC * (blk * SBT // (BLK * P) + 1))
                for f in range(FT):
                    n = blk * FT + f
                    ft = slice(f * P, (f + 1) * P)
                    if n >= 4:
                        pe.wait_ge(s["s_val_ready"], n - 3)
                        if blk <= EARLY:
                            pe.wait_ge(s["su_copied"], min(n - 3, EARLY * FT))
                    for g, w in enumerate((ws_gate, ws_up)):
                        for c in range(DC):
                            ins = split_matmul(nc, bank(2 + n % 4)[:, g * SBT:(g + 1) * SBT],
                                               (w[0][:, c, ft], w[1][:, c, ft]), (xT[0][:, c, b], xT[1][:, c, b]), c == 0, c == DC - 1)
                    ins.then_inc(s["sg_done"], 1)

            def shared_down(blk):
                pe.wait_ge(s["s_lo"], FT * (blk + 1))
                for q in range(SBT // P):
                    t = blk * (SBT // P) + q
                    if t >= 2:
                        pe.wait_ge(s["so_used"], t - 1)
                    r = slice(q * P, (q + 1) * P)
                    for f in range(FT):
                        ins = split_matmul(nc, bank(6 + t % 2)[:, 0:D], (s_hid[0][:, f, r], s_hid[1][:, f, r]),
                                           (ws_down[0][:, f, :], ws_down[1][:, f, :]), f == 0, f == FT - 1)
                    ins.then_inc(s["so_done"], 1)

            pe.wait_ge(s["ws_ready"], 4)
            pe.wait_ge(s["ws_zero"], 6)
            pe.wait_ge(s["r_copied"], NB)
            shared_in(0)
            pe.wait_ge(s["chosen_ready"], 1)
            nc.tensor.matmul(bank(0), before_b, chosen[:, :, :], start=True, stop=False)
            for t in range(NT - 1):
                ins = nc.tensor.matmul(bank(0)[:, (t + 1) * E:], ones_b, chosen[:, t:t + 1, :].to_broadcast([P, NT - 1 - t, E]),
                                       start=False, stop=t == NT - 2)
            ins.then_inc(s["pos_done"], 1)
            shared_down(0)
            shared_in(1)
            for g in range(2):
                pe.wait_ge(s["hots_ready"], g + 1)
                for t in range(NT):
                    ins = nc.tensor.matmul(bank(1)[:, g * EG * BS:(g + 1) * EG * BS], hot_a[:, t, :, :], hot_b[:, t, :, :],
                                           start=t == 0, stop=t == NT - 1)
                ins.then_inc(s["table_done"], 1)
                if g == 0:
                    shared_down(1)
            pe.wait_ge(s["table_ready"], 1)
            for g in range(2):
                ins = nc.tensor.transpose(bank(1)[0:BS, g * P:(g + 1) * P], table[:, g, :], ident)
            ins.then_inc(s["tableT_done"], 1)
            for blk in range(2, EARLY):
                shared_in(blk)
                shared_down(blk)
            pe.wait_ge(s["tableT_ready"], 2)
            pe.wait_ge(s["so_used"], EARLY * (SBT // P))

            with pe.Fori(0, E // 4) as it:
                def turn(q):
                    e = it * 4 + q
                    pe.wait_ge(xe_in[q], it * 16 + 16)
                    pe.wait_ge(s["xeT_ready"], e + 1)
                    for c in range(DC):
                        ins = nc.tensor.transpose(bank(q % 2)[:, c * P:(c + 1) * P], xe[q][:, c * P:(c + 1) * P], ident)
                    ins.then_inc(s["xeT_turned"], 1)

                def gate_up(q):
                    e = it * 4 + q
                    if q % 2 == 0:
                        pe.wait_ge(we_in[q // 2], it * 96 + 96)
                    pe.wait_ge(s["xeT_ready"], e + 3)
                    pe.wait_ge(s["e_hid_ready"], e + 1)
                    for c in range(DC):
                        ins = nc.tensor.matmul(bank(2 + q % 2)[:, 0:2 * FE], xeT[q % 2][:, c, :], we_gu[q // 2][:, q % 2, c, :, :],
                                               start=c == 0, stop=c == DC - 1)
                    ins.then_inc(s["gu_done"], 1)

                def turn_hidden(q):
                    e = it * 4 + q
                    pe.wait_ge(s["e_hid_ready"], e + 3)
                    pe.wait_ge(s["e_hidT_ready"], e + 1)
                    for f in range(2):
                        ins = nc.tensor.transpose(bank(6 + q % 2)[0:FH, f * P:(f + 1) * P], e_hid[q % 2][:, f * FH:(f + 1) * FH], ident)
                    ins.then_inc(s["e_hid_turned"], 1)

                def down(q):
                    e = it * 4 + q
                    pe.wait_ge(s["e_hidT_ready"], e + 3)
                    pe.wait_ge(s["ye_ready"], e + 1)
                    for f in range(2):
                        ins = nc.tensor.matmul(bank(4 + q % 2)[:, 0:D], e_hidT[q % 2][:, f, :], we_down[0:FH, q // 2, q % 2, f, :],
                                               start=f == 0, stop=f == 1)
                    ins.then_inc(s["y_done"], 1)

                turn(0)
                turn(1)
                for q in range(4):
                    gate_up(q)
                    if q:
                        down(q - 1)
                    if q < 2:
                        turn(q + 2)
                    turn_hidden(q)
                down(3)
            pe.wait_ge(s["ye_ready"], E + 2)
            pe.wait_ge(s["e_hidT_ready"], E + 2)
            for blk in range(EARLY, SB):
                shared_in(blk)
                shared_down(blk)
    return semaphores



def attention(nc, env):
    ctx = ExitStack()

    def sb(name, shape, dt):
        return ctx.enter_context(nc.sbuf_tensor(f"a_{name}", shape, dt))

    def two(name, shape):
        return [sb(f"{name}_{part}", shape, F32R) for part in ("hi", "lo")]

    with ctx:
        x, const, bank, dram = env["x"], env["const"], env["bank"], env["dram"]
        ident, ident_b, mask_b = env["ident"], env["ident_b"], env["mask_b"]

        def table(name):
            at, n = CONST[name]
            return const[:, at:at + n].rearrange("p (t d) -> p t d", t=QT)

        cos, sin, cos_scaled = table("cos"), table("sin"), table("cos_scaled")
        w_q = two("w_q", [P, DC, HEADS * DH])
        w_kv = two("w_kv", [P, DC, 2 * DH])
        w_out = two("w_out", [P, HEADS, D])
        stats = env["stats"]
        mv = sb("mv", [P, NT, 2], F32)
        half_p = sb("half_p", [P, NT], F32)
        ve = sb("ve", [P, NT], F32)
        rstd = sb("rstd", [P, NT], F32)
        shift = sb("shift", [P, NT], F32)
        xnT = two("xnT", [P, DC, SEQ])
        k_sin = sb("k_sin", [P, DH], F32)
        k_cos = sb("k_cos", [P, DH], F32)
        k_rot = [sb(f"k_rot{k}", [P, DH], F32) for k in range(2)]
        kT = two("kT", [P, SEQ])
        v = two("v", [P, QT, DH])
        q_cos = sb("q_cos", [P, HG, DH], F32)
        q_sin = sb("q_sin", [P, HG, DH], F32)
        q_rot = sb("q_rot", [P, HG, DH], F32)
        xn = [q_rot[:, 2 * k:2 * k + 2, :].rearrange("p h d -> p (h d)") for k in range(2)]
        qT = [two(f"qT{k}", [P, HG, P]) for k in range(2)]
        peak = sb("peak", [P, RING], F32)
        total = sb("total", [P, RING], F32)
        weight = sb("weight", [P, RING], F32)
        probs = env["place"][:, :].rearrange("p (k t) -> p k t", k=RING)
        pT = two("pT", [P, QT, HG, P])
        oT = two("oT", [P, HG, P])
        SLOT_HEADS = 3
        out_slots = [(k, slice(k * SLOT_HEADS, min((k + 1) * SLOT_HEADS, HEADS))) for k in range(-(-HEADS // SLOT_HEADS))]

        def raw_out(k, heads):
            n = heads.stop - heads.start
            return probs[:, k, 2 * P:2 * P + n * D].rearrange("p (h f) -> p h f", h=n)

        names = ("out_in kv_split ve_ready rstd_ready dve_own half_ready w_hi w_lo out_hi out_split xn_ready xn_turned xnT_hi "
                 "xnT_ready kv_done v_hi v_ready kv_read k_rot_ready k_turned kT_hi kT_ready q_done q_parts q_rotated q_turned "
                 "qT_hi qT_ready s_done max_ready exp_done weight_ready probs_ready p_turned pT_hi pT_ready o_done oT_hi oT_ready "
                 "a_done x_ready").split()
        s = {n: ctx.enter_context(nc.semaphore(f"a_{n}")) for n in names}

        def group_count(i):
            return -(-(i + 1) // 4)

        turned = np.cumsum([0] + [group_count(n // (HG * HG)) for n in range(UNITS * HG)]).tolist()
        TURNED = turned[-1]
        NH = UNITS * HG

        def score(n):
            return bank(n % 4) if n // (HG * HG) < 4 else env["bank2"](2 * (n % 2))

        def heads_of(half):
            return slice(half * HG // HALVES, (half + 1) * HG // HALVES)

        def values_bank(half):
            n = HG // HALVES * P
            return bank(7)[:, half * n:(half + 1) * n].rearrange("p (h t) -> p h t", t=P)

        def scores_held(n):
            return 4 if n // (HG * HG) < 4 else 2

        block = ctx.enter_context(nc.Block())

        @block.sync
        def _(sp):
            sp.wait_ge(s["w_lo"], DC)
            sp.wait_ge(s["kv_split"], 1)
            wout = dram["Wout"].rearrange("(c p) f -> p c f", p=P)
            for k, heads in out_slots:
                sp.dma_start(raw_out(k, heads), wout[:, heads, :]).then_inc(s["out_in"], 16)

        @block.gpsimd
        def _(pool):
            pool.sem_inc(s["q_rotated"], 1)
            nc.gpsimd.memset(half_p[:, :], -0.5).then_inc(s["half_ready"], 1)
            pool.wait_ge(s["half_ready"], 1)
            pool.wait_ge(s["ve_ready"], 1)
            nc.gpsimd.tensor_tensor(rstd[:, :], ve[:, :], half_p[:, :], ALU.pow).then_inc(s["rstd_ready"], 1)
            for c in range(DC):
                pool.wait_ge(s["w_hi"], c + 1)
                nc.gpsimd.tensor_tensor(w_q[1][:, c, :], env["raw_q"][:, c, :], w_q[0][:, c, :].bitcast(F32), ALU.subtract).then_inc(s["w_lo"], 1)
            pool.wait_ge(s["out_in"], 16 * len(out_slots))
            for k, heads in out_slots:
                nc.gpsimd.tensor_scalar(w_out[0][:, heads, :], raw_out(k, heads), 1.0, 1.0, ALU.mult, ALU.mult).then_inc(s["out_hi"], 1)
            for k, heads in out_slots:
                pool.wait_ge(s["out_hi"], k + 1)
                nc.gpsimd.tensor_tensor(w_out[1][:, heads, :], raw_out(k, heads), w_out[0][:, heads, :].bitcast(F32),
                                        ALU.subtract).then_inc(s["out_split"], 1)
            for b in range(BATCH):
                def rotate(u):
                    pool.wait_ge(s["q_parts"], b * UNITS + (u + 1))
                    if b or u:
                        pool.wait_ge(s["q_turned"], b * UNITS + u)
                    nc.gpsimd.tensor_tensor(q_rot[:, :, :], q_cos[:, :, :], q_sin[:, :, :], ALU.add).then_inc(s["q_rotated"], 1)

                rotate(0)
                for u in range(UNITS):
                    keys = (u // HG + 1) * P
                    for j in range(HG):
                        n = u * HG + j
                        k = n % RING
                        if j == 0 and u + 1 < UNITS:
                            rotate(u + 1)
                        pool.wait_ge(s["weight_ready"], b * NH + (n + 1))
                        nc.gpsimd.tensor_scalar(probs[:, k, 0:keys], probs[:, k, 0:keys], weight[:, k:k + 1], 1.0,
                                                ALU.mult, ALU.mult).then_inc(s["probs_ready"], 1)

        @block.scalar
        def _(act):
            act.sem_inc(s["pT_hi"], 1)
            for c in range(DC):
                act.wait_ge(env["q_in"], 16)
                nc.scalar.copy(w_q[0][:, c, :], env["raw_q"][:, c, :]).then_inc(s["w_hi"], 1)
            with act.Fori(0, BATCH) as b:
                def turned_keys(i):
                    act.wait_ge(s["k_turned"], b * QT + (i + 1))
                    nc.scalar.copy(kT[0][:, i * P:(i + 1) * P], bank(i % 2)[:, 0:P]).then_inc(s["kT_hi"], 1)

                for i in range(QT):
                    act.wait_ge(s["xn_turned"], b * QT + (i + 1))
                    nc.scalar.copy(xnT[0][:, :, i * P:(i + 1) * P], bank(4 + i % 2)[:, 0:DC * P].rearrange("p (c t) -> p c t", c=DC))\
                        .then_inc(s["xnT_hi"], 1)
                    if i >= 1:
                        act.wait_ge(s["kv_done"], b * QT + i)
                        nc.scalar.copy(v[0][:, i - 1, :], bank(7 - i % 2)[:, DH:2 * DH]).then_inc(s["v_hi"], 1)
                    if i >= 2:
                        turned_keys(i - 2)
                act.wait_ge(s["kv_done"], b * QT + QT)
                nc.scalar.copy(v[0][:, QT - 1, :], bank(7)[:, DH:2 * DH]).then_inc(s["v_hi"], 1)
                turned_keys(QT - 2)
                turned_keys(QT - 1)

                def queries(u):
                    act.wait_ge(s["q_turned"], b * UNITS + (u + 1))
                    nc.scalar.copy(qT[u % 2][0][:, :, :], bank(6).rearrange("p (h t) -> p h t", h=HG)).then_inc(s["qT_hi"], 1)

                def turned_probs(u, j):
                    i, n = u // HG, u * HG + j
                    for g in range(group_count(i)):
                        m = min(4, i + 1 - 4 * g)
                        at = turned[n] + g
                        act.wait_ge(s["p_turned"], b * TURNED + (at + 1))
                        nc.scalar.copy(pT[0][:, 4 * g:4 * g + m, j, :],
                                       bank(4 + at % 2)[:, 0:m * P].rearrange("p (m t) -> p m t", m=m)).then_inc(s["pT_hi"], 1)

                def exponentials(u, j):
                    n = u * HG + j
                    k = n % RING
                    keys = (u // HG + 1) * P
                    act.wait_ge(s["max_ready"], b * NH + (n + 1))
                    if u == 2 * HG and j == 0:
                        act.wait_ge(s["out_split"], len(out_slots))
                    if n >= RING:
                        act.wait_ge(s["p_turned"], b * TURNED + turned[n - RING + 1])
                    nc.scalar.activation(probs[:, k, 0:keys], score(n)[:, 0:keys], ACT.Exp, bias=peak[:, k:k + 1],
                                         accum_out=total[:, k:k + 1]).then_inc(s["exp_done"], 1)

                def half_values(u, half):
                    act.wait_ge(s["o_done"], b * UNITS * HALVES + (u * HALVES + half + 1))
                    nc.scalar.copy(oT[0][:, heads_of(half), :], values_bank(half)).then_inc(s["oT_hi"], 1)

                queries(0)
                for u in range(UNITS + 1):
                    for step in STEPS:
                        if step[0] == "turn" and u:
                            turned_probs(u - 1, step[1])
                        if step[0] == "scores" and u < UNITS:
                            exponentials(u, step[1])
                        if step[0] == "turn_queries" and u + 1 < UNITS:
                            queries(u + 1)
                        if step[0] == "values" and u:
                            half_values(u - 1, step[1])
        @block.vector
        def _(dve):
            own = Chain(dve, s["dve_own"])
            link = own.link
            dve.sem_inc(s["x_ready"], 1)
            dve.sem_inc(s["pT_ready"], 1)
            for t in range(NT):
                ins = nc.vector.bn_aggr(mv[:, t, :], stats[:, t, :])
            link(ins)
            nc.vector.tensor_scalar(ve[:, :], mv[:, :, 1], LN_EPS, None, ALU.add).then_inc(s["ve_ready"], 1)
            dve.wait_ge(env["kv_in"], 16)
            link(nc.vector.tensor_copy(w_kv[0][:, :, :], env["raw_kv"]))
            nc.vector.tensor_tensor(w_kv[1][:, :, :], env["raw_kv"], w_kv[0][:, :, :].bitcast(F32), ALU.subtract).then_inc(s["kv_split"], 1)
            dve.wait_ge(s["rstd_ready"], 1)
            link(nc.vector.scalar_tensor_tensor(shift[:, :], mv[:, :, 0], -1.0, rstd[:, :], ALU.mult, ALU.mult))
            with dve.Fori(0, BATCH) as b:
                def rows(i):
                    return x[:, one(b * QT + i), :].rearrange("p n d -> p (n d)")

                def low(out, src, high):
                    return nc.vector.tensor_tensor(out, src, high.bitcast(F32), ALU.subtract)

                def parts(src, a_cos, a_sin, i, heads, cos, scale):
                    shape = [P, heads, 2, HALF]
                    q = src.rearrange("p (h s d) -> p h s d", h=heads, s=2)
                    c = cos[:, i:i + 1, :].unsqueeze(1).to_broadcast(shape)
                    d = sin[:, i:i + 1, :].to_broadcast([P, heads, HALF])
                    nc.vector.tensor_tensor(a_cos.rearrange("p h (s d) -> p h s d", s=2), q, c, ALU.mult)
                    nc.vector.scalar_tensor_tensor(a_sin[:, :, 0:HALF], q[:, :, 1, :], -scale, d, ALU.mult, ALU.mult)
                    return nc.vector.scalar_tensor_tensor(a_sin[:, :, HALF:DH], q[:, :, 0, :], scale, d, ALU.mult, ALU.mult)

                def turned_input(i):
                    dve.wait_ge(s["xnT_hi"], b * QT + (i + 1))
                    at = slice(i * P, (i + 1) * P)
                    low(xnT[1][:, :, at], bank(4 + i % 2)[:, 0:DC * P].rearrange("p (c t) -> p c t", c=DC),
                        xnT[0][:, :, at]).then_inc(s["xnT_ready"], 1)

                def turned_keys(i):
                    dve.wait_ge(s["kT_hi"], b * QT + (i + 1))
                    at = slice(i * P, (i + 1) * P)
                    low(kT[1][:, at], bank(i % 2)[:, 0:P], kT[0][:, at]).then_inc(s["kT_ready"], 1)

                def key_value(i):
                    dve.wait_ge(s["kv_done"], b * QT + (i + 1))
                    kv = bank(6 + i % 2)
                    dve.wait_ge(s["v_hi"], b * QT + (i + 1))
                    low(v[1][:, i, :], kv[:, DH:2 * DH], v[0][:, i, :])
                    parts(kv[:, 0:DH], k_cos[:, :].unsqueeze(1), k_sin[:, :].unsqueeze(1), i, 1, cos, 1.0).then_inc(s["kv_read"], 1)
                    dve.wait_ge(s["kv_read"], b * QT + (i + 1))
                    if i >= 2:
                        dve.wait_ge(s["k_turned"], b * QT + (i - 1))
                    nc.vector.tensor_tensor(k_rot[i % 2][:, :], k_cos[:, :], k_sin[:, :], ALU.add).then_inc(s["k_rot_ready"], 1)
                    dve.wait_ge(s["k_rot_ready"], b * QT + (i + 1))

                def normal_rows(i):
                    if i >= 2:
                        dve.wait_ge(s["xn_turned"], b * QT + (i - 1))
                    nc.vector.tensor_scalar(xn[i % 2][:, :], rows(i), rstd[:, one(b * QT + i)], shift[:, one(b * QT + i)],
                                            ALU.mult, ALU.add).then_inc(s["xn_ready"], 1)

                normal_rows(0)
                for i in range(QT):
                    if i + 1 < QT:
                        normal_rows(i + 1)
                    turned_input(i)
                    if i >= 1:
                        key_value(i - 1)
                    if i >= 2:
                        turned_keys(i - 2)
                key_value(QT - 1)
                turned_keys(QT - 2)
                turned_keys(QT - 1)

                def query_parts(u):
                    dve.wait_ge(s["q_done"], b * UNITS + (u + 1))
                    dve.wait_ge(s["q_rotated"], b * UNITS + (u + 1))
                    parts(bank(6), q_cos[:, :, :], q_sin[:, :, :], u // HG, HG, cos_scaled, SCALE).then_inc(s["q_parts"], 1)

                def queries(u):
                    dve.wait_ge(s["qT_hi"], b * UNITS + (u + 1))
                    low(qT[u % 2][1][:, :, :], bank(6).rearrange("p (h t) -> p h t", h=HG), qT[u % 2][0][:, :, :]).then_inc(s["qT_ready"], 1)

                def normal(n):
                    k = n % RING
                    dve.wait_ge(s["exp_done"], b * NH + (n + 1))
                    nc.vector.reciprocal(weight[:, k:k + 1], total[:, k:k + 1]).then_inc(s["weight_ready"], 1)

                def turned_probs(u, j):
                    i, n = u // HG, u * HG + j
                    for g in range(group_count(i)):
                        m = min(4, i + 1 - 4 * g)
                        at = turned[n] + g
                        dve.wait_ge(s["pT_hi"], b * TURNED + (at + 2))
                        low(pT[1][:, 4 * g:4 * g + m, j, :], bank(4 + at % 2)[:, 0:m * P].rearrange("p (m t) -> p m t", m=m),
                            pT[0][:, 4 * g:4 * g + m, j, :]).then_inc(s["pT_ready"], 1)

                def maximum(u, j):
                    n = u * HG + j
                    k = n % RING
                    dve.wait_ge(s["s_done"], b * NH + (n + 1))
                    nc.vector.reduce_max(peak[:, k:k + 1], score(n)[:, 0:(u // HG + 1) * P], axis=AX, negate=True).then_inc(s["max_ready"], 1)

                def add_to_x(u):
                    dve.wait_ge(s["a_done"], b * UNITS + (u + 1))
                    nc.vector.tensor_tensor(rows(u // HG), bank(7)[:, 0:D], rows(u // HG), ALU.add).then_inc(s["x_ready"], 1)
                    dve.wait_ge(s["x_ready"], b * UNITS + (u + 2))
                    if u % HG == HG - 1:
                        nc.vector.bn_stats(stats[:, one(b * QT + u // HG), :].rearrange("p n d -> p (n d)"), rows(u // HG))

                def half_values(u, half):
                    dve.wait_ge(s["oT_hi"], b * UNITS * HALVES + (u * HALVES + half + 1))
                    low(oT[1][:, heads_of(half), :], values_bank(half), oT[0][:, heads_of(half), :]).then_inc(s["oT_ready"], 1)

                query_parts(0)
                queries(0)
                for u in range(UNITS + 1):
                    for step in STEPS:
                        if step[0] == "turn" and u:
                            turned_probs(u - 1, step[1])
                        if step[0] == "project" and u >= 2:
                            add_to_x(u - 2)
                        if step[0] == "scores" and u < UNITS:
                            maximum(u, step[1])
                        if step[0] == "scores" and 0 < u * HG + step[1] <= NH:
                            normal(u * HG + step[1] - 1)
                        if step == ("scores", 0) and u + 1 < UNITS:
                            query_parts(u + 1)
                        if step[0] == "turn_queries" and u + 1 < UNITS:
                            queries(u + 1)
                        if step[0] == "values" and u:
                            half_values(u - 1, step[1])
                add_to_x(UNITS - 1)

        @block.tensor
        def _(pe):
            with pe.Fori(0, BATCH) as b:
                pe.wait_ge(s["kv_split"], 1)
                pe.wait_ge(s["pT_ready"], b * TURNED + 1)
                pe.wait_ge(s["x_ready"], b * UNITS + 1)

                def key_value(i):
                    pe.wait_ge(s["xnT_ready"], b * QT + (i + 1))
                    if i >= 2:
                        pe.wait_ge(s["kv_read"], b * QT + (i - 1))
                    at = slice(i * P, (i + 1) * P)
                    for c in range(DC):
                        ins = split_matmul(nc, bank(6 + i % 2)[:, 0:2 * DH], (xnT[0][:, c, at], xnT[1][:, c, at]),
                                           (w_kv[0][:, c, :], w_kv[1][:, c, :]), c == 0, c == DC - 1)
                    ins.then_inc(s["kv_done"], 1)

                def turn_keys(i):
                    pe.wait_ge(s["k_rot_ready"], b * QT + (i + 1))
                    if i >= 2:
                        pe.wait_ge(s["kT_ready"], b * QT + (i - 1))
                    nc.tensor.transpose(bank(i % 2)[:, 0:P], k_rot[i % 2][:, :], ident).then_inc(s["k_turned"], 1)

                for i in range(QT):
                    pe.wait_ge(s["xn_ready"], b * QT + (i + 1))
                    if i >= 2:
                        pe.wait_ge(s["xnT_ready"], b * QT + (i - 1))
                    for c in range(DC):
                        ins = nc.tensor.transpose(bank(4 + i % 2)[:, c * P:(c + 1) * P], xn[i % 2][:, c * P:(c + 1) * P], ident)
                    ins.then_inc(s["xn_turned"], 1)
                    if i >= 1:
                        key_value(i - 1)
                    if i >= 2:
                        turn_keys(i - 2)
                key_value(QT - 1)
                turn_keys(QT - 2)
                turn_keys(QT - 1)

                def project_queries(u):
                    i, g = u // HG, u % HG
                    if u:
                        pe.wait_ge(s["qT_ready"], b * UNITS + u)
                    else:
                        pe.wait_ge(s["kv_read"], b * QT + QT)
                    at, heads = slice(i * P, (i + 1) * P), slice(g * HG * DH, (g + 1) * HG * DH)
                    for c in range(DC):
                        ins = split_matmul(nc, bank(6), (xnT[0][:, c, at], xnT[1][:, c, at]),
                                           (w_q[0][:, c, heads], w_q[1][:, c, heads]), c == 0, c == DC - 1)
                    ins.then_inc(s["q_done"], 1)

                def turn_queries(u):
                    pe.wait_ge(s["q_rotated"], b * UNITS + (u + 2))
                    for j in range(HG):
                        ins = nc.tensor.transpose(bank(6)[:, j * P:(j + 1) * P], q_rot[:, j, :], ident)
                    ins.then_inc(s["q_turned"], 1)

                def scores(u, j):
                    i, n = u // HG, u * HG + j
                    if j == 0:
                        pe.wait_ge(s["qT_ready"], b * UNITS + (u + 1))
                    if n == 0:
                        pe.wait_ge(s["kT_ready"], b * QT + QT)
                    if n >= scores_held(n):
                        pe.wait_ge(s["exp_done"], b * NH + (n - scores_held(n) + 1))
                    keys = (i + 1) * P
                    for at in range(0, keys, 512):
                        end = max(min(keys, at + 512), at + 256)
                        split_matmul(nc, score(n)[:, at:end], (qT[u % 2][0][:, j, :], qT[u % 2][1][:, j, :]),
                                     (kT[0][:, at:end], kT[1][:, at:end]), True, end < keys)
                    nc.tensor.matmul(score(n)[:, i * P:keys], ident_b, mask_b, start=False, stop=True).then_inc(s["s_done"], 1)

                def turn_probs(u, j):
                    i, n = u // HG, u * HG + j
                    pe.wait_ge(s["probs_ready"], b * NH + (n + 1))
                    for g in range(group_count(i)):
                        at = turned[n] + g
                        if at >= 2:
                            pe.wait_ge(s["pT_ready"], b * TURNED + at)
                        for m in range(4 * g, min(4 * g + 4, i + 1)):
                            ins = nc.tensor.transpose(bank(4 + at % 2)[:, (m - 4 * g) * P:(m - 4 * g + 1) * P],
                                                      probs[:, n % RING, m * P:(m + 1) * P], ident)
                        ins.then_inc(s["p_turned"], 1)

                def values(u, half):
                    i = u // HG
                    pe.wait_ge(s["pT_ready"], b * TURNED + (turned[u * HG + heads_of(half).stop] + 1))
                    if half:
                        pe.wait_ge(s["oT_ready"], b * UNITS * HALVES + (u * HALVES + half))
                    elif u:
                        pe.wait_ge(s["x_ready"], b * UNITS + (u + 1))
                    for m in range(i + 1):
                        ins = split_matmul(nc, values_bank(half), (v[0][:, m, :], v[1][:, m, :]),
                                           (pT[0][:, m, heads_of(half), :], pT[1][:, m, heads_of(half), :]), m == 0, m == i)
                    ins.then_inc(s["o_done"], 1)

                def project(u):
                    pe.wait_ge(s["oT_ready"], b * UNITS * HALVES + (u + 1) * HALVES)
                    if u == 0:
                        pe.wait_ge(s["out_split"], len(out_slots))
                    for j in range(HG):
                        hd = u % HG * HG + j
                        ins = split_matmul(nc, bank(7)[:, 0:D], (oT[0][:, j, :], oT[1][:, j, :]),
                                           (w_out[0][:, hd, :], w_out[1][:, hd, :]), j == 0, j == HG - 1)
                    ins.then_inc(s["a_done"], 1)

                pe.wait_ge(s["w_lo"], DC)
                project_queries(0)
                turn_queries(0)
                for u in range(UNITS + 1):
                    for step in STEPS:
                        if step[0] == "turn" and u:
                            turn_probs(u - 1, step[1])
                        if step[0] == "scores" and u < UNITS:
                            scores(u, step[1])
                        if step[0] == "project_queries" and u + 1 < UNITS:
                            project_queries(u + 1)
                        if step[0] == "project" and u >= 2:
                            project(u - 2)
                        if step[0] == "turn_queries" and u + 1 < UNITS:
                            turn_queries(u + 1)
                        if step[0] == "values" and u:
                            values(u - 1, step[1])
                project(UNITS - 1)


def load_all(sp, env):
    dram = env["dram"]
    rows = dram["x"].rearrange("(n t p) d -> n p t d", p=P, t=BLK)
    for blk in range(NB):
        sp.dma_start(env["x"][:, blk * BLK:(blk + 1) * BLK, :], rows[blk]).then_inc(env["x_in"][blk], 16)
    for dst, src in (
        (env["const"][:, :], dram["const"]),
        (env["w_norm"][:, :], dram["w_norm"].rearrange("(o d) -> o d", o=1).to_broadcast([P, D])),
        (env["w_route"][:, :, 0:E], dram["w_router"].rearrange("(c p) e -> p c e", p=P)),
        (env["w_route"][:, :, E:E + 1], dram["w_shared_gate"].rearrange("(c p) e -> p c e", p=P)),
    ):
        sp.dma_start(dst, src, allow_slow_non_contiguous=True).then_inc(env["w_in"], 16)


def make_tables(nc, pool, env):
    nc.gpsimd.memset(env["ones_b"], 1.0).then_inc(env["tables_ready"], 1)
    pool.wait_ge(env["w_in"], 16 * W_LOADS)
    for dst, src in (("before_b", "before"), ("ident_b", "ident"), ("mask_b", "mask")):
        at, n = CONST[src]
        nc.gpsimd.tensor_copy(env[dst], env["const"][:, at:at + n]).then_inc(env["tables_ready"], 1)


def macaron(nc, dram):
    with ExitStack() as ctx:
        def sb(name, shape, dt=F32):
            return ctx.enter_context(nc.sbuf_tensor(name, shape, dt))

        const = sb("const", [P, CONST_COLS])
        ps = ctx.enter_context(nc.psum_tensor("ps", [P, 8 * 512], F32))
        env = {
            "dram": dram,
            "x": sb("x", [P, NT, D]),
            "const": const,
            "bank": lambda k: ps[:, k * 512:(k + 1) * 512],
            "bank2": lambda k: ps[:, k * 512:(k + 2) * 512],
            "ident": const[:, 0:P],
            "stats": sb("stats", [P, NT, 6]),
            "place": sb("place", [P, RING * SEQ]),
            "w_norm": sb("w_norm", [P, D]),
            "w_route": sb("w_route", [P, DC, E + 1]),
            "xr_dram": nc.dram_tensor("xr_rows", [NT * P, D], F32, kind="Internal").ap(),
            "y_dram": nc.dram_tensor("expert_rows", [E * CAP, D], F32, kind="Internal").ap(),
            "x_in": [ctx.enter_context(nc.semaphore(f"x_in{k}")) for k in range(NB)],
        }
        for n in ("w_in", "tables_ready", "kv_in", "q_in"):
            env[n] = ctx.enter_context(nc.semaphore(n))
        env["raw_q"] = env["place"][:, 0:DC * HEADS * DH].rearrange("p (c f) -> p c f", c=DC)
        env["raw_kv"] = env["place"][:, DC * HEADS * DH:DC * (HEADS + 2) * DH].rearrange("p (c f) -> p c f", c=DC)
        for n in ("ones_b", "before_b", "ident_b", "mask_b"):
            env[n] = sb(n, [P, P], BF16)[:, :]
        nc.clear_and_free_semaphores(ffn(nc, 0, env))
        nc.all_engine_barrier()
        attention(nc, env)
        ffn(nc, 1, env)


INPUTS = ("attn_x", "attn_Wq", "attn_Wkv", "attn_Wout", "ffn_w_norm", "ffn_w_router", "ffn_w_gate", "ffn_w_up",
          "ffn_w_down", "ffn_sw_gate", "ffn_sw_up", "ffn_sw_down", "ffn_w_shared_gate")


def kernel(**inputs):
    import concourse.bacc as bacc
    from concourse.bass_utils import run_bass_kernel_spmd

    nc = bacc.Bacc("TRN2", target_bir_lowering=False, num_devices=1)
    arrays = {f"in_{n}": np.ascontiguousarray(inputs[f"L0_{n}"]) for n in INPUTS}
    arrays["in_attn_x"] = arrays["in_attn_x"].reshape(BATCH * SEQ, D)
    arrays["in_all_const"] = constants()
    dram = {}
    for name, a in arrays.items():
        dram[name.split("_", 2)[-1]] = nc.dram_tensor(name, a.shape, mybir.dt.from_np(a.dtype), kind="ExternalInput").ap()
    dram["out"] = nc.dram_tensor("out", (BATCH * SEQ, D), F32, kind="ExternalOutput").ap()
    macaron(nc, dram)
    r = run_bass_kernel_spmd(nc, [arrays], core_ids=[0])
    return r.results[0]["out"].reshape(BATCH, SEQ, D)
```

```python
from contextlib import ExitStack

import numpy as np
import concourse.bass as bass
from concourse import mybir

F32 = mybir.dt.float32
F32R = mybir.dt.float32r
F16 = mybir.dt.float16
BF16 = mybir.dt.bfloat16
U32 = mybir.dt.uint32
ALU = mybir.AluOpType
ACT = mybir.ActivationFunctionType
AX = mybir.AxisListType.X

P = 128
BATCH, SEQ, D = 2, 1024, 256
NT = BATCH * SEQ // P
DC = D // P
BLK = 4
NB = NT // BLK
SBT = 256
SB = NT * P // SBT
EARLY = 2
PLACES_AT, TABLES_AT = 5, (10, 11)
LAG = 12
E, TOPK, FE, CAP = 32, 4, 176, 128
FH = FE // 2
FS = 704
FT = -(-FS // P)
HEADS, DH = 16, 128
HG = 4
SCALE = DH ** -0.5
QT = SEQ // P
UNITS = QT * HEADS // HG
STEPS = (("turn", 0), ("scores", 0), ("project_queries",), ("project",), ("turn", 1), ("scores", 1), ("turn", 2),
         ("values", 0), ("turn_queries",), ("turn", 3), ("scores", 2), ("scores", 3), ("values", 1))
HALVES = 2
HALF = DH // 2
RING = HG + 2
LN_EPS, RMS_EPS = 1e-5, 1e-6
W_LOADS = 4
MASKED = -3e38
EXP_ZERO = -87.3
FAR = 65536.0
MAGIC = 12582912.0
EG, AS, BS = 16, 8, 16

CONST = {}
_at = 0
for _name, _n in (("ident", P), ("mask", P), ("before", P), ("cos", QT * HALF), ("sin", QT * HALF),
                  ("cos_scaled", QT * HALF),
                  ("own", EG), ("expert", E), ("first_slot", E), ("token", NT)):
    CONST[_name] = (_at, _n)
    _at += _n
CONST_COLS = _at


def constants():
    c = np.zeros((P, CONST_COLS), np.float32)

    def put(name, value):
        at, n = CONST[name]
        c[:, at:at + n] = value

    p = np.arange(P)
    put("ident", np.eye(P))
    put("mask", np.where(p[None, :] > p[:, None], MASKED, 0.0))
    put("before", p[:, None] < p[None, :])
    inv = (1.0 / np.float32(10000.0) ** (np.arange(0, DH, 2, dtype=np.float32) / np.float32(DH))).astype(np.float32)
    pos = (np.arange(SEQ, dtype=np.float32)[:, None] * inv[None, :]).astype(np.float32)
    for name, f, scale in (("cos", np.cos, 1.0), ("sin", np.sin, 1.0), ("cos_scaled", np.cos, SCALE)):
        put(name, (f(pos).astype(np.float32) * np.float32(scale)).reshape(QT, P, HALF).transpose(1, 0, 2).reshape(P, QT * HALF))
    put("own", p[:, None] // AS == np.arange(EG)[None, :])
    put("expert", np.arange(E))
    put("first_slot", np.arange(E) * CAP)
    put("token", p[:, None] + P * np.arange(NT)[None, :])
    return c


def one(i):
    return bass.ds(i, 1)


class Chain:

    def __init__(self, eng, sem):
        self.eng, self.sem, self.base, self.n = eng, sem, 0, 0

    def link(self, ins):
        self.n += 1
        ins.then_inc(self.sem, 1)
        self.eng.wait_ge(self.sem, self.base + self.n)

    def enter(self, i, links):
        self.start, self.links = self.base + self.n, links
        self.base, self.n = self.start + i * links, 0

    def leave(self, iterations):
        assert self.n == self.links, (self.n, self.links)
        self.base, self.n = self.start + iterations * self.links, 0


def split_matmul(nc, out, w, x, start, stop):
    (w_hi, w_lo), (x_hi, x_lo) = w, x
    nc.tensor.matmul(out, w_hi, x_hi, start=start, stop=False)
    nc.tensor.matmul(out, w_hi, x_lo, start=False, stop=False)
    return nc.tensor.matmul(out, w_lo, x_hi, start=False, stop=stop)


def ffn(nc, layer, env):
    ctx = ExitStack()

    def sb(name, shape, dt):
        return ctx.enter_context(nc.sbuf_tensor(f"{name}_{layer}", shape, dt))

    semaphores = []

    def sem(name):
        semaphores.append(nc.alloc_semaphore(name=f"{name}_{layer}"))
        return semaphores[-1]

    with ctx:
        x, const, bank = env["x"], env["const"], env["bank"]
        ident, ones_b, before_b = env["ident"], env["ones_b"], env["before_b"]
        w_norm, w_route = env["w_norm"], env["w_route"]
        xr_dram, y_dram = env["xr_dram"], env["y_dram"]
        dram = env["dram"]

        h = sb("h", [P, NT, D], F32)
        xT = [sb(f"xT{k}", [P, DC, NT * P], F32R) for k in range(2)]
        place = env["place"]
        GU, DOWN = 4 * DC * FE, 8 * D
        xTf = place[:, 2 * GU + DOWN:2 * GU + DOWN + DC * BLK * P].rearrange("p (c t) -> p c t", c=DC)
        xr = [sb(f"xr{k}", [P, BLK, D], F32) for k in range(2)]
        stats = env["stats"]
        mv = sb("mv", [P, NT, 2], F32)
        half_p = sb("half_p", [P, NT], F32)
        ve = sb("ve", [P, NT], F32)
        rstd = sb("rstd", [P, NT], F32)
        shift = sb("shift", [P, NT], F32)
        msq = sb("msq", [P, NT], F32)
        rrms = sb("rrms", [P, NT], F32)
        logitsT = [sb(f"logitsT{k}", [E + 1, BLK * P], F32) for k in range(2)]
        logits = sb("logits", [P, NT, E + 1], F32)
        top = sb("top", [P, NT], F32)
        diff = sb("diff", [P, NT, E], F32)
        key = sb("key", [P, NT, E], F32)
        probs = sb("probs", [P, NT, E], F32)
        sig = sb("sig", [P, NT], F32)
        val8 = sb("val8", [P, NT, 8], F32)
        idx8 = sb("idx8", [P, NT, 8], U32)
        idxf = sb("idxf", [P, NT, TOPK], F32)
        onehot = sb("onehot", [P, NT, TOPK, E], BF16)
        chosen2 = sb("chosen2", [P, NT, 2, E], BF16)
        chosen = sb("chosen", [P, NT, E], BF16)
        den = sb("den", [P, NT], F32)
        wk = sb("wk", [P, NT, TOPK], F32)
        late = diff
        slot = sb("slot", [P, NT, E], F32)
        slotk = sb("slotk", [P, NT, TOPK], F32)
        slotu = sb("slotu", [P, NT * TOPK], U32)
        row_a = probs
        row_ah = sb("row_ah", [P, NT, E], F16)
        row_bh = sb("row_bh", [P, NT, E], F16)
        hot_a = sb("hot_a", [P, NT, EG, AS], F16)
        hot_b = sb("hot_b", [P, BS, NT, EG], F16)
        picked = hot_b[:, :, :, :].rearrange("p b t e -> p (b t e)").bitcast(F32)\
            .rearrange("p (t k e) -> p t k e", t=NT, k=TOPK)
        token_h = sb("token_h", [P, NT], F16)
        table_own = sb("table_own", [P, 2, BS, EG], F32)
        table = sb("table", [P, 2, BS], F32)
        tableT = sb("tableT", [BS, AS, E], U32)
        source = sb("source", [P, E], U32)
        ws_gate = [sb(f"ws_gate{k}", [P, DC, FT * P], F32R) for k in range(2)]
        ws_up = [sb(f"ws_up{k}", [P, DC, FT * P], F32R) for k in range(2)]
        ws_down = [sb(f"ws_down{k}", [P, FT, D], F32R) for k in range(2)]
        s_gate = [sb(f"s_gate{k}", [P, SBT], F32) for k in range(2)]
        s_upc = [sb(f"s_upc{k}", [P, SBT], F32) for k in range(2)]
        s_val = [sb(f"s_val{k}", [P, SBT], F32) for k in range(2)]
        s_hid = [sb(f"s_hid{k}", [P, FT, SBT], F32R) for k in range(2)]
        s_sum = [sb(f"s_sum{k}", [P, D], F32) for k in range(2)]
        we_gu = [place[:, k * GU:(k + 1) * GU].rearrange("p (e c g f) -> p e c g f", e=2, c=DC, g=2) for k in range(2)]
        we_down = place[:, 2 * GU:2 * GU + DOWN].rearrange("p (k e c d) -> p k e c d", k=2, e=2, c=2)
        xe = [sb(f"xe{k}", [P, D], F32) for k in range(4)]
        xeT = [s_upc[k][:, :].rearrange("p (c t) -> p c t", c=DC) for k in range(2)]
        e_gate = [key[:, :, :].rearrange("p t e -> p (t e)")[:, k * FE:(k + 1) * FE] for k in range(2)]
        e_hid = [table_own[:, :, :, :].rearrange("p g b e -> p (g b e)")[:, k * FE:(k + 1) * FE] for k in range(2)]
        e_hidT = [s_sum[k][0:FH, :].rearrange("p (c t) -> p c t", c=2) for k in range(2)]
        ye = [hot_a[:, 4 * k:4 * k + 4, :, :].rearrange("p t e a -> p (t e a)").bitcast(F32) for k in range(4)]
        back = [xr[0][:, :, :], xr[1][:, :, :], xTf[:, :, :].rearrange("p c (a d) -> p (c a) d", d=D),
                onehot[:, :, :, :].rearrange("p t k e -> p (t k e)").bitcast(F32).rearrange("p (k d) -> p k d", k=TOPK)]

        raw_gate = we_gu[0][:, :, :, :, :].rearrange("p e c g f -> p (e c g f)").rearrange("p (c f) -> p c f", c=DC)
        raw_up = we_gu[1][:, :, :, :, :].rearrange("p e c g f -> p (e c g f)").rearrange("p (c f) -> p c f", c=DC)
        raw_down = we_down[:, :, :, :, :].rearrange("p k e c d -> p (k e c) d")[:, 0:FT, :]
        LAST = FS - (FT - 1) * P

        def col(name):
            at, n = CONST[name]
            return const[:, at:at + n]

        names = ("ve_ready rstd_ready msq_ready rrms_ready pool_own h_ready xr_ready xr_turned xTf_ready "
                 "xT_hi xT_lo "
                 "rT_done rT_copied r_done r_copied diff_ready val_ready exps_ready sig_ready chosen_ready pos_done "
                 "hots_ready table_done table_ready tableT_done tableT_ready source_ready slots_ready "
                 "ws_in ws_zero ws_ready sg_done sg_act su_copied s_val_ready s_hi s_lo s_hid_used so_done so_copied so_used row_added back_used out_ready "
                 "xeT_turned xeT_ready gu_done e_act e_hid_ready e_hid_turned e_hidT_ready y_done ye_ready dve_own out_done").split()
        s = {n: sem(n) for n in names}
        xr_saved = [sem(f"xr_saved{k}") for k in range(2)]
        we_in = [sem(f"we_in{k}") for k in range(4)]
        xe_in = [sem(f"xe_in{k}") for k in range(4)]
        ye_out = [sem(f"ye_out{k}") for k in range(4)]
        back_in = [sem(f"back_in{k}") for k in range(4)]

        def out_bank(t):
            blk = t // (SBT // P)
            return bank((6 if blk < EARLY or (blk - EARLY) % 2 == 0 else 0) + t % 2)

        def load_expert(sp, e, k):
            place_gu = we_gu[k // 2][:, k % 2]
            for g, name in enumerate(("w_gate", "w_up")):
                rows = dram[name].rearrange("e (c p) f -> e p c f", p=P)
                sp.dma_start(place_gu[:, :, g, :], rows[one(e)].rearrange("e p c f -> (e p) c f")).then_inc(we_in[k], 16)
            rows = dram["w_down"].rearrange("e (c p) d -> e p c d", p=FH)
            sp.dma_start(we_down[0:FH, k // 2, k % 2], rows[one(e)].rearrange("e p c d -> (e p) c d")).then_inc(we_in[k], 16)

        block = ctx.enter_context(nc.Block())

        @block.sync
        def _(sp):
            for k in range(4):
                sp.sem_inc(ye_out[k], 16)
            if layer == 0:
                load_all(sp, env)
            sp.dma_start(raw_gate, dram["sw_gate"].rearrange("(c p) f -> p c f", p=P)).then_inc(s["ws_in"], 16)
            sp.dma_start(raw_up, dram["sw_up"].rearrange("(c p) f -> p c f", p=P)).then_inc(s["ws_in"], 16)
            sp.dma_start(raw_down[:, 0:FT - 1, :], dram["sw_down"][0:(FT - 1) * P].rearrange("(c p) f -> p c f", p=P)).then_inc(s["ws_in"], 16)
            sp.dma_start(raw_down[0:LAST, FT - 1, :], dram["sw_down"][(FT - 1) * P:]).then_inc(s["ws_in"], 16)
            xr_rows = xr_dram.rearrange("(n t p) d -> n p t d", p=P, t=BLK)
            for blk in range(NB):
                sp.wait_ge(s["xr_ready"], BLK * (blk + 1))
                sp.dma_start(xr_rows[blk], xr[blk % 2][:, :, :]).then_inc(xr_saved[blk % 2], 16)
            sp.wait_ge(s["ws_ready"], 4)
            for k in range(4):
                load_expert(sp, k, k)
            sp.wait_ge(s["tableT_ready"], 2)
            for a in range(AS):
                sp.dma_start(source[a * BS:(a + 1) * BS, :], tableT[:, a, :]).then_inc(s["source_ready"], 16)

            y_rows = y_dram.rearrange("(e c) d -> e c d", c=CAP)

            def store_y(e, k):
                sp.wait_ge(s["ye_ready"], e + 3)
                sp.dma_start(y_rows[one(e)].rearrange("e c d -> (e c) d"), ye[k]).then_inc(ye_out[k], 16)

            with sp.Fori(0, E // 4 - 1) as it:
                for q in range(4):
                    sp.wait_ge(s["y_done"], it * 4 + q + 1)
                    load_expert(sp, it * 4 + q + 4, q)
                    store_y(it * 4 + q, q)
            for q in range(4):
                store_y(E - 4 + q, q)
            if layer == 0:
                sp.wait_ge(s["y_done"], E)
                sp.dma_start(env["raw_kv"], dram["Wkv"].rearrange("(c p) f -> p c f", p=P)).then_inc(env["kv_in"], 16)
                sp.dma_start(env["raw_q"], dram["Wq"].rearrange("(c p) f -> p c f", p=P)).then_inc(env["q_in"], 16)
            if layer == 1:
                out_rows = dram["out"].rearrange("(n p) d -> n p d", p=P)
                with sp.Fori(0, NT) as t:
                    sp.wait_ge(s["out_ready"], t + 1)
                    sp.dma_start(out_rows[one(t)].rearrange("n p d -> (n p) d"),
                                 x[:, one(t), :].rearrange("p n d -> p (n d)")).then_inc(s["out_done"], 16)
                sp.wait_ge(s["out_done"], 16 * NT)
            for k in range(4):
                sp.wait_ge(ye_out[k], 16 * E // 4 + 16)

        @block.gpsimd
        def _(pool):
            nc.gpsimd.memset(half_p[:, :], -0.5).then_inc(s["pool_own"], 1)
            for w in (ws_gate, ws_up):
                for k in range(2):
                    nc.gpsimd.memset(w[k][:, :, FS:].bitcast(F32), 0.0).then_inc(s["ws_zero"], 1)
            for k in range(2):
                nc.gpsimd.memset(ws_down[k][:, FT - 1, :].bitcast(F32), 0.0).then_inc(s["ws_zero"], 1)
            pool.wait_ge(s["pool_own"], 1)
            order = [(0, 0), (0, 1), (1, 0), (0, 2), (1, 1), (0, 3), (1, 2), (1, 3)]
            for norm, blk in order:
                b = slice(blk * BLK, (blk + 1) * BLK)
                if norm == 0:
                    pool.wait_ge(s["ve_ready"], blk + 1)
                    nc.gpsimd.tensor_tensor(rstd[:, b], ve[:, b], half_p[:, b], ALU.pow).then_inc(s["rstd_ready"], 1)
                else:
                    pool.wait_ge(s["msq_ready"], blk + 1)
                    nc.gpsimd.tensor_tensor(rrms[:, b], msq[:, b], half_p[:, b], ALU.pow).then_inc(s["rrms_ready"], 1)
            if layer == 0:
                make_tables(nc, pool, env)
            pool.wait_ge(s["ws_in"], 16 * 4)
            parts = ((ws_gate, raw_gate, slice(0, P), slice(0, DC), slice(0, FS)), (ws_up, raw_up, slice(0, P), slice(0, DC), slice(0, FS)),
                     (ws_down, raw_down, slice(0, P), slice(0, FT - 1), slice(0, D)), (ws_down, raw_down, slice(0, LAST), slice(FT - 1, FT), slice(0, D)))
            pool.wait_ge(s["ws_zero"], 6)
            for n, (w, raw, p, c, f) in enumerate(parts):
                if n:
                    pool.wait_ge(s["ws_ready"], n)
                nc.gpsimd.tensor_scalar(w[0][p, c, f], raw[p, c, f], 1.0, 1.0, ALU.mult, ALU.mult).then_inc(s["pool_own"], 1)
                pool.wait_ge(s["pool_own"], n + 2)
                nc.gpsimd.tensor_tensor(w[1][p, c, f], raw[p, c, f], w[0][p, c, f].bitcast(F32), ALU.subtract).then_inc(s["ws_ready"], 1)

            def early_hidden(n):
                pool.wait_ge(s["su_copied"], n + 1)
                nc.gpsimd.tensor_tensor(s_val[n % 2][:, :], s_gate[n % 2][:, :], s_upc[n % 2][:, :], ALU.mult).then_inc(s["s_val_ready"], 1)
                pool.wait_ge(s["s_hi"], n + 1)
                nc.gpsimd.tensor_tensor(s_hid[1][:, n % FT, :], s_val[n % 2][:, :], s_hid[0][:, n % FT, :].bitcast(F32),
                                        ALU.subtract).then_inc(s["s_lo"], 1)

            def early_sum(blk):
                for q in range(SBT // P):
                    t = blk * (SBT // P) + q
                    pool.wait_ge(s["so_copied"], t + 1)
                    nc.gpsimd.tensor_tensor(h[:, t, :], h[:, t, :], s_sum[t % 2][:, :], ALU.add).then_inc(s["so_used"], 1)

            for n in range(EARLY * FT):
                early_hidden(n)
                if n % FT == FT - 1 and n >= FT:
                    early_sum(n // FT - 1)
            early_sum(EARLY - 1)

            for k in range(2):
                pool.wait_ge(xr_saved[k], 16 * NB // 2)
            pool.wait_ge(s["source_ready"], 16 * AS)
            for e in range(E):
                k = e % 4
                if e >= 4:
                    pool.wait_ge(s["xeT_turned"], e - 3)
                nc.gpsimd.indirect_dma_start(xe[k][:, :], None, xr_dram[:, :],
                                             bass.IndirectOffsetOnAxis(source[:, e:e + 1], 0)).then_inc(xe_in[k], 16)
            for k in range(4):
                pool.wait_ge(ye_out[k], 16 * E // 4 + 16)
            pool.wait_ge(s["slots_ready"], 1)
            for t in range(NT):
                k = t % 4
                if t >= 4:
                    pool.wait_ge(s["back_used"], t - 3)
                for j in range(TOPK):
                    n = t * TOPK + j
                    nc.gpsimd.indirect_dma_start(back[k][:, j, :], None, y_dram[:, :],
                                                 bass.IndirectOffsetOnAxis(slotu[:, n:n + 1], 0),
                                                 bounds_check=E * CAP - 1, oob_is_err=False).then_inc(back_in[k], 16)

        @block.scalar
        def _(act):
            act.sem_inc(s["xeT_ready"], 2)
            act.sem_inc(s["e_hidT_ready"], 2)
            def normal_rows(blk):
                act.wait_ge(s["rstd_ready"], blk + 1)
                act.wait_ge(s["msq_ready"], blk + 1)
                for q in range(BLK):
                    t = blk * BLK + q
                    nc.scalar.activation(h[:, t, :], x[:, t, :], ACT.Identity, bias=shift[:, t:t + 1],
                                         scale=rstd[:, t:t + 1]).then_inc(s["h_ready"], 1)

            def turned_rows(blk):
                b = slice(blk * BLK * P, (blk + 1) * BLK * P)
                if blk:
                    act.wait_ge(s["rT_done"], blk)
                    act.wait_ge(s["xT_lo"], DC * blk)
                for c in range(DC):
                    act.wait_ge(s["xr_turned"], DC * blk + c + 1)
                    nc.scalar.copy(xTf[:, c, :], bank(blk % 2 * DC + c)).then_inc(s["xTf_ready"], 1)
                for c in range(DC):
                    nc.scalar.copy(xT[0][:, c, b], bank(blk % 2 * DC + c)).then_inc(s["xT_hi"], 1)

            def routed(blk):
                act.wait_ge(s["rT_done"], blk + 1)
                if blk >= 2:
                    act.wait_ge(s["r_done"], blk - 1)
                nc.scalar.copy(logitsT[blk % 2][:, :], bank(6)[0:E + 1, :]).then_inc(s["rT_copied"], 1)

            normal_rows(0)
            normal_rows(1)
            for blk in range(NB):
                turned_rows(blk)
                if blk + 2 < NB:
                    normal_rows(blk + 2)
                routed(blk)
            act.wait_ge(s["r_copied"], NB)
            nc.scalar.activation(sig[:, :], logits[:, :, E], ACT.Exp, scale=-1.0).then_inc(s["exps_ready"], 1)
            act.wait_ge(s["diff_ready"], 1)
            nc.scalar.activation(probs[:, :, :], diff[:, :, :], ACT.Exp).then_inc(s["exps_ready"], 1)
            act.wait_ge(s["val_ready"], 1)
            nc.scalar.activation(wk[:, :, :], val8[:, :, 0:TOPK], ACT.Exp).then_inc(s["exps_ready"], 1)

            def shared_gate(n):
                gu = bank(2 + n % 4).rearrange("p (g t) -> p g t", g=2)
                act.wait_ge(s["sg_done"], n + 1)
                if n >= 2:
                    act.wait_ge(s["s_val_ready"], n - 1)
                nc.scalar.activation(s_gate[n % 2][:, :], gu[:, 0, :], ACT.Silu).then_inc(s["sg_act"], 1)
                if n < EARLY * FT:
                    nc.scalar.copy(s_upc[n % 2][:, :], gu[:, 1, :]).then_inc(s["su_copied"], 1)

            def shared_high(n):
                blk, f = divmod(n, FT)
                act.wait_ge(s["s_val_ready"], n + 1)
                if blk and f < FT - 1:
                    act.wait_ge(s["s_hid_used"], (blk - 1) * (FT - 1) + f + 1)
                elif blk:
                    act.wait_ge(s["so_done"], blk * (SBT // P))
                nc.scalar.copy(s_hid[0][:, f, :], s_val[n % 2][:, :]).then_inc(s["s_hi"], 1)

            def early_out(blk):
                for q in range(SBT // P):
                    t = blk * (SBT // P) + q
                    act.wait_ge(s["so_done"], t + 1)
                    act.wait_ge(s["sig_ready"], 1)
                    if t >= 2:
                        act.wait_ge(s["so_used"], t - 1)
                    nc.scalar.activation(s_sum[t % 2][:, :], out_bank(t)[:, 0:D], ACT.Copy,
                                         scale=sig[:, t:t + 1]).then_inc(s["so_copied"], 1)

            shared_gate(0)
            for n in range(EARLY * FT):
                if n + 1 < EARLY * FT:
                    shared_gate(n + 1)
                shared_high(n)
                if n % FT == FT - 1 and n >= FT:
                    early_out(n // FT - 1)
            early_out(EARLY - 1)

            def turned_expert(it, q):
                act.wait_ge(s["xeT_turned"], it * 4 + q + 1)
                nc.scalar.copy(xeT[q % 2][:, :, :], bank(q % 2)[:, 0:DC * P].rearrange("p (c t) -> p c t", c=DC)).then_inc(s["xeT_ready"], 1)

            def four_experts(it, last):
                for q in range(4):
                    act.wait_ge(s["gu_done"], it * 4 + q + 1)
                    nc.scalar.activation(e_gate[q % 2][:, :], bank(2 + q % 2)[:, 0:FE], ACT.Silu).then_inc(s["e_act"], 1)
                    if not last or q < 2:
                        turned_expert(it, q + 2)
                    act.wait_ge(s["e_hid_turned"], it * 4 + q + 1)
                    nc.scalar.copy(e_hidT[q % 2][:, :, :], bank(6 + q % 2)[0:FH, 0:2 * P].rearrange("p (c t) -> p c t", c=2)).then_inc(s["e_hidT_ready"], 1)

            turned_expert(0, 0)
            turned_expert(0, 1)
            with act.Fori(0, E // 4 - 1) as it:
                four_experts(it, False)
            four_experts(E // 4 - 1, True)
            shared_gate(EARLY * FT)
            for n in range(EARLY * FT, SB * FT):
                if n + 1 < SB * FT:
                    shared_gate(n + 1)
                shared_high(n)

        @block.vector
        def _(dve):
            own = Chain(dve, s["dve_own"])
            link = own.link
            dve.sem_inc(s["e_hid_ready"], 2)
            dve.sem_inc(s["ye_ready"], 2)

            def moments(blk):
                b = slice(blk * BLK, (blk + 1) * BLK)
                if layer == 0:
                    dve.wait_ge(env["x_in"][blk], 16)
                    for t in range(blk * BLK, (blk + 1) * BLK):
                        ins = nc.vector.bn_stats(stats[:, t, :], x[:, t, :])
                    link(ins)
                for t in range(blk * BLK, (blk + 1) * BLK):
                    ins = nc.vector.bn_aggr(mv[:, t, :], stats[:, t, :])
                link(ins)
                nc.vector.tensor_scalar(ve[:, b], mv[:, b, 1], LN_EPS, None, ALU.add).then_inc(s["ve_ready"], 1)

            def mean_squares(blk):
                b = slice(blk * BLK, (blk + 1) * BLK)
                dve.wait_ge(s["rstd_ready"], blk + 1)
                link(nc.vector.tensor_tensor(msq[:, b], mv[:, b, 1], rstd[:, b], ALU.mult))
                nc.vector.scalar_tensor_tensor(shift[:, b], mv[:, b, 0], -1.0, rstd[:, b], ALU.mult, ALU.mult)
                link(nc.vector.tensor_tensor(msq[:, b], msq[:, b], rstd[:, b], ALU.mult))
                nc.vector.tensor_scalar(msq[:, b], msq[:, b], RMS_EPS, None, ALU.add).then_inc(s["msq_ready"], 1)

            def rows(blk):
                dve.wait_ge(s["rrms_ready"], blk + 1)
                if layer == 0 and blk == 0:
                    dve.wait_ge(env["w_in"], 16 * W_LOADS)
                if blk >= 2:
                    dve.wait_ge(s["xr_turned"], DC * (blk - 1))
                    dve.wait_ge(xr_saved[blk % 2], 16 * (blk // 2))
                for q in range(BLK):
                    t = blk * BLK + q
                    dve.wait_ge(s["h_ready"], t + 1)
                    nc.vector.scalar_tensor_tensor(xr[blk % 2][:, q, :], h[:, t, :], rrms[:, t:t + 1], w_norm[:, :],
                                                   ALU.mult, ALU.mult).then_inc(s["xr_ready"], 1)

            def turned(blk):
                b = slice(blk * BLK * P, (blk + 1) * BLK * P)
                for c in range(DC):
                    dve.wait_ge(s["xT_hi"], DC * blk + c + 1)
                    nc.vector.tensor_tensor(xT[1][:, c, b], xTf[:, c, :], xT[0][:, c, b].bitcast(F32),
                                            ALU.subtract).then_inc(s["xT_lo"], 1)

            def routed(blk):
                dve.wait_ge(s["r_done"], blk + 1)
                nc.vector.tensor_copy(logits[:, blk * BLK:(blk + 1) * BLK, :],
                                      bank(7)[:, 0:BLK * (E + 1)].rearrange("p (t e) -> p t e", t=BLK)).then_inc(s["r_copied"], 1)

            moments(0)
            moments(1)
            mean_squares(0)
            moments(2)
            mean_squares(1)
            rows(0)
            moments(3)
            mean_squares(2)
            rows(1)
            mean_squares(3)
            turned(0)
            rows(2)
            turned(1)
            routed(0)
            rows(3)
            turned(2)
            routed(1)
            turned(3)
            routed(2)
            routed(3)
            dve.wait_ge(s["r_copied"], NB)
            link(nc.vector.reduce_max(top[:, :], logits[:, :, 0:E], axis=AX))
            nc.vector.tensor_tensor(diff[:, :, :], logits[:, :, 0:E], top[:, :].unsqueeze(2).to_broadcast([P, NT, E]),
                                    ALU.subtract).then_inc(s["diff_ready"], 1)
            dve.wait_ge(s["diff_ready"], 1)
            link(nc.vector.tensor_scalar(key[:, :, :], diff[:, :, :], EXP_ZERO, None, ALU.max))
            for t in range(NT):
                ins = nc.vector.max(val8[:, t, :], key[:, t, :])
            ins.then_inc(s["val_ready"], 1)
            dve.wait_ge(s["val_ready"], 1)
            for t in range(NT):
                ins = nc.vector.max_index(idx8[:, t, :], val8[:, t, :], key[:, t, :])
            link(ins)
            link(nc.vector.tensor_copy(idxf[:, :, :], idx8[:, :, 0:TOPK]))
            link(nc.vector.tensor_tensor(onehot[:, :, :, :], col("expert").unsqueeze(1).unsqueeze(1).to_broadcast([P, NT, TOPK, E]),
                                         idxf[:, :, :].unsqueeze(3).to_broadcast([P, NT, TOPK, E]), ALU.is_equal))
            link(nc.vector.tensor_tensor(chosen2[:, :, :, :], onehot[:, :, 0:2, :], onehot[:, :, 2:4, :], ALU.add))
            nc.vector.tensor_tensor(chosen[:, :, :], chosen2[:, :, 0, :], chosen2[:, :, 1, :], ALU.add).then_inc(s["chosen_ready"], 1)
            dve.wait_ge(s["exps_ready"], 3)
            link(nc.vector.tensor_scalar(sig[:, :], sig[:, :], 1.0, None, ALU.add))
            nc.vector.reciprocal(sig[:, :], sig[:, :]).then_inc(s["sig_ready"], 1)
            link(nc.vector.reduce_sum(den[:, :], probs[:, :, :], axis=AX))
            link(nc.vector.reciprocal(den[:, :], den[:, :]))
            link(nc.vector.tensor_tensor(wk[:, :, :], wk[:, :, :], den[:, :].unsqueeze(2).to_broadcast([P, NT, TOPK]), ALU.mult))
            link(nc.vector.tensor_copy(token_h[:, :], col("token")))
            pos = bank(0).rearrange("p (t e) -> p t e", t=NT)
            dve.wait_ge(s["chosen_ready"], 1)
            dve.wait_ge(s["pos_done"], 1)
            link(nc.vector.tensor_scalar(late[:, :, :], pos, float(CAP), FAR, ALU.is_ge, ALU.mult))
            link(nc.vector.tensor_tensor(late[:, :, :], pos, late[:, :, :], ALU.add))
            link(nc.vector.scalar_tensor_tensor(key[:, :, :], chosen[:, :, :], -FAR, late[:, :, :], ALU.mult, ALU.add))
            link(nc.vector.tensor_scalar(key[:, :, :], key[:, :, :], FAR, 1024.0, ALU.add, ALU.min))
            link(nc.vector.tensor_scalar(row_a[:, :, :], key[:, :, :], 1.0 / BS, -0.46875, ALU.mult, ALU.add))
            link(nc.vector.tensor_scalar(row_a[:, :, :], row_a[:, :, :], MAGIC, -MAGIC, ALU.add, ALU.add))
            link(nc.vector.tensor_copy(row_ah[:, :, :], row_a[:, :, :]))
            link(nc.vector.scalar_tensor_tensor(row_bh[:, :, :], row_a[:, :, :], -float(BS), key[:, :, :], ALU.mult, ALU.add))
            for g in range(2):
                eg = slice(g * EG, (g + 1) * EG)
                if g:
                    dve.wait_ge(s["table_done"], g)
                for a in range(AS):
                    nc.vector.scalar_tensor_tensor(hot_a[:, :, :, a], row_ah[:, :, eg], float(a),
                                                   token_h[:, :].unsqueeze(2).to_broadcast([P, NT, EG]), ALU.is_equal, ALU.mult)
                for b in range(BS):
                    ins = nc.vector.tensor_scalar(hot_b[:, b, :, :], row_bh[:, :, eg], float(b), None, ALU.is_equal)
                ins.then_inc(s["hots_ready"], 1)
            dve.wait_ge(s["table_done"], 2)
            tab = bank(1).rearrange("p (g b e) -> p g b e", g=2, e=EG)
            link(nc.vector.tensor_tensor(table_own[:, :, :, :], tab,
                                         col("own").unsqueeze(1).unsqueeze(1).to_broadcast([P, 2, BS, EG]), ALU.mult))
            nc.vector.reduce_sum(table[:, :, :], table_own[:, :, :, :], axis=AX).then_inc(s["table_ready"], 1)
            dve.wait_ge(s["tableT_done"], 1)
            for g in range(2):
                nc.vector.tensor_copy(tableT[:, :, g * EG:(g + 1) * EG],
                                      bank(1)[0:BS, g * P:(g + 1) * P].rearrange("b (e a) -> b a e", e=EG)).then_inc(s["tableT_ready"], 1)
            link(nc.vector.tensor_tensor(slot[:, :, :], late[:, :, :],
                                         col("first_slot").unsqueeze(1).to_broadcast([P, NT, E]), ALU.add))
            link(nc.vector.tensor_tensor(picked, onehot[:, :, :, :],
                                         slot[:, :, :].unsqueeze(2).to_broadcast([P, NT, TOPK, E]), ALU.mult))
            link(nc.vector.reduce_sum(slotk[:, :, :], picked, axis=AX))
            nc.vector.tensor_copy(slotu[:, :].rearrange("p (t k) -> p t k", k=TOPK), slotk[:, :, :]).then_inc(s["slots_ready"], 1)
            link(nc.vector.scalar_tensor_tensor(wk[:, :, :], slotk[:, :, :], float(E * CAP), wk[:, :, :], ALU.is_lt, ALU.mult))


            def rows_out(e, q):
                dve.wait_ge(s["y_done"], e + 1)
                dve.wait_ge(ye_out[q], (e - q) // 4 * 16 + 16)
                nc.vector.tensor_copy(ye[q], bank(4 + q % 2)[:, 0:D]).then_inc(s["ye_ready"], 1)

            def four_experts(it, first):
                for q in range(4):
                    e = it * 4 + q
                    dve.wait_ge(s["e_act"], e + 1)
                    nc.vector.tensor_tensor(e_hid[q % 2][:, :], bank(2 + q % 2)[:, FE:2 * FE], e_gate[q % 2][:, :],
                                            ALU.mult).then_inc(s["e_hid_ready"], 1)
                    if not first or q:
                        rows_out(e - 1, (q - 1) % 4)

            four_experts(0, True)
            with dve.Fori(1, E // 4) as it:
                four_experts(it, False)
            rows_out(E - 1, 3)

            def combine(n):
                t, j = divmod(n, TOPK)
                if j == 0:
                    dve.wait_ge(back_in[t % 4], 16 * TOPK * (t // 4 + 1))
                else:
                    dve.wait_ge(s["row_added"], n - t)
                ins = nc.vector.scalar_tensor_tensor(h[:, t, :], back[t % 4][:, j, :], wk[:, t, j:j + 1], h[:, t, :], ALU.mult, ALU.add)
                ins.then_inc(s["row_added" if j < TOPK - 1 else "back_used"], 1)

            def close(t):
                nc.vector.scalar_tensor_tensor(x[:, t, :], h[:, t, :], 0.5, x[:, t, :], ALU.mult, ALU.add).then_inc(s["out_ready"], 1)

            def moments_of(t, closed):
                if layer == 0:
                    dve.wait_ge(s["out_ready"], closed)
                    nc.vector.bn_stats(stats[:, t, :], x[:, t, :])

            dve.wait_ge(s["so_used"], EARLY * (SBT // P))
            n, closed, summed = -LAG, 0, EARLY * (SBT // P)

            def step():
                nonlocal n
                if 0 <= n < NT * TOPK:
                    combine(n)
                n += 1

            def close_all():
                nonlocal closed
                first = closed
                while closed < summed and (closed + 1) * TOPK <= n:
                    dve.wait_ge(s["back_used"], closed + 1)
                    close(closed)
                    closed += 1
                for t in range(first, closed):
                    moments_of(t, t + 1)

            def shared_out():
                nonlocal summed
                added = min(n, NT * TOPK)
                if added >= TOPK:
                    dve.wait_ge(s["back_used"], added // TOPK)
                if added > 0:
                    dve.wait_ge(s["row_added"], added - added // TOPK)
                for t in range(summed, summed + SBT // P):
                    dve.wait_ge(s["so_done"], t + 1)
                    nc.vector.scalar_tensor_tensor(h[:, t, :], out_bank(t)[:, 0:D], sig[:, t:t + 1], h[:, t, :],
                                                   ALU.mult, ALU.add).then_inc(s["so_used"], 1)
                summed += SBT // P
                dve.wait_ge(s["so_used"], summed)
                close_all()

            for m in range(EARLY * FT, SB * FT):
                dve.wait_ge(s["sg_act"], m + 1)
                nc.vector.tensor_tensor(s_val[m % 2][:, :], bank(2 + m % 4)[:, SBT:2 * SBT], s_gate[m % 2][:, :],
                                        ALU.mult).then_inc(s["s_val_ready"], 1)
                step()
                if m % FT == FT - 1 and m >= (EARLY + 1) * FT:
                    shared_out()
                dve.wait_ge(s["s_hi"], m + 1)
                nc.vector.tensor_tensor(s_hid[1][:, m % FT, :], s_val[m % 2][:, :], s_hid[0][:, m % FT, :].bitcast(F32),
                                        ALU.subtract).then_inc(s["s_lo"], 1)
                step()
            step()
            step()
            shared_out()
            while closed < NT:
                step()
                close_all()

        @block.tensor
        def _(pe):
            if layer == 0:
                pe.wait_ge(env["w_in"], 16 * W_LOADS)

            def turn_rows(blk):
                pe.wait_ge(s["xr_ready"], BLK * (blk + 1))
                if blk >= 2:
                    pe.wait_ge(s["xT_hi"], DC * (blk - 1))
                for c in range(DC):
                    for q in range(BLK):
                        ins = nc.tensor.transpose(bank(blk % 2 * DC + c)[:, q * P:(q + 1) * P], xr[blk % 2][:, q, c * P:(c + 1) * P], ident)
                    ins.then_inc(s["xr_turned"], 1)

            def route(blk):
                pe.wait_ge(s["xTf_ready"], DC * (blk + 1))
                if blk:
                    pe.wait_ge(s["rT_copied"], blk)
                for c in range(DC):
                    ins = nc.tensor.matmul(bank(6)[0:E + 1, :], w_route[:, c, :], xTf[:, c, :], start=c == 0, stop=c == DC - 1)
                ins.then_inc(s["rT_done"], 1)

            def turn_logits(blk):
                pe.wait_ge(s["rT_copied"], blk + 1)
                if blk:
                    pe.wait_ge(s["r_copied"], blk)
                for q in range(BLK):
                    ins = nc.tensor.transpose(bank(7)[:, q * (E + 1):(q + 1) * (E + 1)], logitsT[blk % 2][:, q * P:(q + 1) * P],
                                              ident[0:E + 1, 0:E + 1])
                ins.then_inc(s["r_done"], 1)

            turn_rows(0)
            for blk in range(NB):
                if blk + 1 < NB:
                    turn_rows(blk + 1)
                route(blk)
                if blk:
                    turn_logits(blk - 1)
            turn_logits(NB - 1)

            def shared_in(n):
                blk, f = divmod(n, FT)
                b = slice(blk * SBT, (blk + 1) * SBT)
                ft = slice(f * P, (f + 1) * P)
                if n >= 4:
                    pe.wait_ge(s["s_val_ready"], n - 3)
                    if n < (EARLY + 1) * FT:
                        pe.wait_ge(s["su_copied"], min(n - 3, EARLY * FT))
                for g, w in enumerate((ws_gate, ws_up)):
                    for c in range(DC):
                        ins = split_matmul(nc, bank(2 + n % 4)[:, g * SBT:(g + 1) * SBT],
                                           (w[0][:, c, ft], w[1][:, c, ft]), (xT[0][:, c, b], xT[1][:, c, b]), c == 0, c == DC - 1)
                ins.then_inc(s["sg_done"], 1)

            def shared_down(n):
                blk, f = divmod(n, FT)
                pe.wait_ge(s["s_lo"], n + 1)
                for q in range(SBT // P):
                    t = blk * (SBT // P) + q
                    if f == 0 and 0 < blk < EARLY:
                        pe.wait_ge(s["so_used"], t - 1)
                    if f == 0 and blk >= EARLY + 2:
                        pe.wait_ge(s["so_used"], t - 3)
                    r = slice(q * P, (q + 1) * P)
                    ins = split_matmul(nc, out_bank(t)[:, 0:D], (s_hid[0][:, f, r], s_hid[1][:, f, r]),
                                       (ws_down[0][:, f, :], ws_down[1][:, f, :]), f == 0, f == FT - 1)
                    if f == FT - 1:
                        ins.then_inc(s["so_done"], 1)
                if f < FT - 1:
                    ins.then_inc(s["s_hid_used"], 1)

            def places():
                if layer == 0:
                    pe.wait_ge(env["tables_ready"], 4)
                pe.wait_ge(s["chosen_ready"], 1)
                nc.tensor.matmul(bank(0), before_b, chosen[:, :, :], start=True, stop=False)
                for t in range(NT - 1):
                    ins = nc.tensor.matmul(bank(0)[:, (t + 1) * E:], ones_b, chosen[:, t:t + 1, :].to_broadcast([P, NT - 1 - t, E]),
                                           start=False, stop=t == NT - 2)
                ins.then_inc(s["pos_done"], 1)

            def token_table(g):
                pe.wait_ge(s["hots_ready"], g + 1)
                for t in range(NT):
                    ins = nc.tensor.matmul(bank(1)[:, g * EG * BS:(g + 1) * EG * BS], hot_a[:, t, :, :], hot_b[:, :, t, :],
                                           start=t == 0, stop=t == NT - 1)
                ins.then_inc(s["table_done"], 1)

            def turn_table():
                pe.wait_ge(s["table_ready"], 1)
                for g in range(2):
                    ins = nc.tensor.transpose(bank(1)[0:BS, g * P:(g + 1) * P], table[:, g, :], ident)
                ins.then_inc(s["tableT_done"], 1)

            pe.wait_ge(s["ws_ready"], 4)
            pe.wait_ge(s["ws_zero"], 6)
            pe.wait_ge(s["r_copied"], NB)
            for n in range(EARLY * FT):
                shared_in(n)
                if n >= FT:
                    shared_down(n - FT)
                if n == PLACES_AT:
                    places()
                if n in TABLES_AT:
                    token_table(TABLES_AT.index(n))
            turn_table()
            for n in range((EARLY - 1) * FT, EARLY * FT):
                shared_down(n)
            pe.wait_ge(s["tableT_ready"], 2)
            pe.wait_ge(s["so_used"], EARLY * (SBT // P))

            def turn(it, q):
                e = it * 4 + q
                pe.wait_ge(xe_in[q % 4], it * 16 + 16 * (q // 4 + 1))
                pe.wait_ge(s["xeT_ready"], e + 1)
                for c in range(DC):
                    ins = nc.tensor.transpose(bank(q % 2)[:, c * P:(c + 1) * P], xe[q % 4][:, c * P:(c + 1) * P], ident)
                ins.then_inc(s["xeT_turned"], 1)

            def gate_up(it, q):
                e = it * 4 + q
                pe.wait_ge(we_in[q], it * 48 + 48)
                pe.wait_ge(s["xeT_ready"], e + 3)
                pe.wait_ge(s["e_hid_ready"], e + 1)
                for c in range(DC):
                    ins = nc.tensor.matmul(bank(2 + q % 2)[:, 0:2 * FE], xeT[q % 2][:, c, :], we_gu[q // 2][:, q % 2, c, :, :],
                                           start=c == 0, stop=c == DC - 1)
                ins.then_inc(s["gu_done"], 1)

            def turn_hidden(it, q):
                e = it * 4 + q
                pe.wait_ge(s["e_hid_ready"], e + 3)
                pe.wait_ge(s["e_hidT_ready"], e + 1)
                for f in range(2):
                    ins = nc.tensor.transpose(bank(6 + q % 2)[0:FH, f * P:(f + 1) * P], e_hid[q % 2][:, f * FH:(f + 1) * FH], ident)
                ins.then_inc(s["e_hid_turned"], 1)

            def down(e, q):
                pe.wait_ge(s["e_hidT_ready"], e + 3)
                pe.wait_ge(s["ye_ready"], e + 1)
                for f in range(2):
                    ins = nc.tensor.matmul(bank(4 + q % 2)[:, 0:D], e_hidT[q % 2][:, f, :], we_down[0:FH, q // 2, q % 2, f, :],
                                           start=f == 0, stop=f == 1)
                ins.then_inc(s["y_done"], 1)

            def four_experts(it, first=False, last=False):
                for q in range(4):
                    gate_up(it, q)
                    if not first or q:
                        down(it * 4 + q - 1, (q - 1) % 4)
                    if not last or q < 2:
                        turn(it, q + 2)
                    turn_hidden(it, q)

            turn(0, 0)
            turn(0, 1)
            four_experts(0, first=True)
            with pe.Fori(1, E // 4 - 1) as it:
                four_experts(it)
            four_experts(E // 4 - 1, last=True)
            down(E - 1, 3)
            pe.wait_ge(s["ye_ready"], E + 2)
            pe.wait_ge(s["e_hidT_ready"], E + 2)
            for n in range(EARLY * FT, (SB + 1) * FT):
                if n < SB * FT:
                    shared_in(n)
                if n >= (EARLY + 1) * FT:
                    shared_down(n - FT)
    return semaphores



def attention(nc, env):
    ctx = ExitStack()

    def sb(name, shape, dt):
        return ctx.enter_context(nc.sbuf_tensor(f"a_{name}", shape, dt))

    def two(name, shape):
        return [sb(f"{name}_{part}", shape, F32R) for part in ("hi", "lo")]

    with ctx:
        x, const, bank, dram = env["x"], env["const"], env["bank"], env["dram"]
        ident, ident_b, mask_b = env["ident"], env["ident_b"], env["mask_b"]

        def table(name):
            at, n = CONST[name]
            return const[:, at:at + n].rearrange("p (t d) -> p t d", t=QT)

        cos, sin, cos_scaled = table("cos"), table("sin"), table("cos_scaled")
        w_q = two("w_q", [P, DC, HEADS * DH])
        w_kv = two("w_kv", [P, DC, 2 * DH])
        w_out = two("w_out", [P, HEADS, D])
        stats = env["stats"]
        mv = sb("mv", [P, NT, 2], F32)
        half_p = sb("half_p", [P, NT], F32)
        ve = sb("ve", [P, NT], F32)
        rstd = sb("rstd", [P, NT], F32)
        shift = sb("shift", [P, NT], F32)
        xnT = two("xnT", [P, DC, SEQ])
        k_sin = sb("k_sin", [P, DH], F32)
        k_cos = sb("k_cos", [P, DH], F32)
        k_rot = [sb(f"k_rot{k}", [P, DH], F32) for k in range(2)]
        kT = two("kT", [P, SEQ])
        v = two("v", [P, QT, DH])
        q_cos = sb("q_cos", [P, HG, DH], F32)
        q_sin = sb("q_sin", [P, HG, DH], F32)
        q_rot = sb("q_rot", [P, HG, DH], F32)
        xn = [q_rot[:, 2 * k:2 * k + 2, :].rearrange("p h d -> p (h d)") for k in range(2)]
        qT = [two(f"qT{k}", [P, HG, P]) for k in range(2)]
        peak = sb("peak", [P, RING], F32)
        total = sb("total", [P, RING], F32)
        weight = sb("weight", [P, RING], F32)
        probs = env["place"][:, :].rearrange("p (k t) -> p k t", k=RING)
        pT = two("pT", [P, QT, HG, P])
        oT = two("oT", [P, HG, P])
        SLOT_HEADS = 3
        out_slots = [(k, slice(k * SLOT_HEADS, min((k + 1) * SLOT_HEADS, HEADS))) for k in range(-(-HEADS // SLOT_HEADS))]

        def raw_out(k, heads):
            n = heads.stop - heads.start
            return probs[:, k, 2 * P:2 * P + n * D].rearrange("p (h f) -> p h f", h=n)

        names = ("out_in kv_split ve_ready rstd_ready shift_ready dve_own half_ready w_hi w_lo out_hi out_split xn_ready xn_turned xnT_hi "
                 "xnT_ready kv_done v_hi kv_read k_rot_ready k_turned kT_hi kT_ready q_done q_parts q_rotated q_turned "
                 "qT_hi qT_ready s_done max_ready exp_done weight_ready probs_ready p_turned pT_hi pT_ready o_done oT_hi oT_ready "
                 "a_done x_ready").split()
        s = {n: ctx.enter_context(nc.semaphore(f"a_{n}")) for n in names}

        def group_count(i):
            return -(-(i + 1) // 4)

        turned = np.cumsum([0] + [group_count(n // (HG * HG)) for n in range(UNITS * HG)]).tolist()
        TURNED = turned[-1]
        NH = UNITS * HG

        def score(n):
            return bank(n % 4) if n // (HG * HG) < 4 else env["bank2"](2 * (n % 2))

        def heads_of(half):
            return slice(half * HG // HALVES, (half + 1) * HG // HALVES)

        def values_bank(half):
            n = HG // HALVES * P
            return bank(7)[:, half * n:(half + 1) * n].rearrange("p (h t) -> p h t", t=P)

        def scores_held(n):
            return 4 if n // (HG * HG) < 4 else 2

        block = ctx.enter_context(nc.Block())

        @block.sync
        def _(sp):
            sp.wait_ge(s["w_lo"], DC)
            sp.wait_ge(s["kv_split"], 1)
            wout = dram["Wout"].rearrange("(c p) f -> p c f", p=P)
            for k, heads in out_slots:
                sp.dma_start(raw_out(k, heads), wout[:, heads, :]).then_inc(s["out_in"], 16)

        @block.gpsimd
        def _(pool):
            pool.sem_inc(s["q_rotated"], 1)
            nc.gpsimd.memset(half_p[:, :], -0.5).then_inc(s["half_ready"], 1)
            pool.wait_ge(s["half_ready"], 1)
            pool.wait_ge(s["ve_ready"], 1)
            nc.gpsimd.tensor_tensor(rstd[:, :], ve[:, :], half_p[:, :], ALU.pow).then_inc(s["rstd_ready"], 1)
            for c in range(DC):
                pool.wait_ge(s["w_hi"], c + 1)
                nc.gpsimd.tensor_tensor(w_q[1][:, c, :], env["raw_q"][:, c, :], w_q[0][:, c, :].bitcast(F32), ALU.subtract).then_inc(s["w_lo"], 1)

            def split_out(n):
                k, heads = out_slots[n]
                if n == 0:
                    pool.wait_ge(s["out_in"], 16 * len(out_slots))
                nc.gpsimd.tensor_scalar(w_out[0][:, heads, :], raw_out(k, heads), 1.0, 1.0, ALU.mult, ALU.mult).then_inc(s["out_hi"], 1)
                pool.wait_ge(s["out_hi"], n + 1)
                nc.gpsimd.tensor_tensor(w_out[1][:, heads, :], raw_out(k, heads), w_out[0][:, heads, :].bitcast(F32),
                                        ALU.subtract).then_inc(s["out_split"], 1)

            for b in range(BATCH):
                def rotate(u):
                    pool.wait_ge(s["q_parts"], b * UNITS + (u + 1))
                    if b or u:
                        pool.wait_ge(s["q_turned"], b * UNITS + u)
                    nc.gpsimd.tensor_tensor(q_rot[:, :, :], q_cos[:, :, :], q_sin[:, :, :], ALU.add).then_inc(s["q_rotated"], 1)

                rotate(0)
                for u in range(UNITS):
                    keys = (u // HG + 1) * P
                    for j in range(HG):
                        n = u * HG + j
                        k = n % RING
                        if j == 0 and u + 1 < UNITS:
                            rotate(u + 1)
                        pool.wait_ge(s["weight_ready"], b * NH + (n + 1))
                        nc.gpsimd.tensor_scalar(probs[:, k, 0:keys], probs[:, k, 0:keys], weight[:, k:k + 1], 1.0,
                                                ALU.mult, ALU.mult).then_inc(s["probs_ready"], 1)
                        if b == 0 and n < len(out_slots):
                            split_out(n)

        @block.scalar
        def _(act):
            act.sem_inc(s["pT_hi"], 1)
            for c in range(DC):
                act.wait_ge(env["q_in"], 16)
                nc.scalar.copy(w_q[0][:, c, :], env["raw_q"][:, c, :]).then_inc(s["w_hi"], 1)
            act.wait_ge(s["shift_ready"], 1)
            with act.Fori(0, BATCH) as b:
                def turned_keys(i):
                    act.wait_ge(s["k_turned"], b * QT + (i + 1))
                    nc.scalar.copy(kT[0][:, i * P:(i + 1) * P], bank(i % 2)[:, 0:P]).then_inc(s["kT_hi"], 1)

                def normal_rows(i):
                    if i >= 2:
                        act.wait_ge(s["xn_turned"], b * QT + (i - 1))
                    nc.scalar.activation(xn[i % 2], x[:, one(b * QT + i), :].rearrange("p n d -> p (n d)"), ACT.Identity,
                                         bias=shift[:, one(b * QT + i)], scale=rstd[:, one(b * QT + i)]).then_inc(s["xn_ready"], 1)

                normal_rows(0)
                normal_rows(1)
                for i in range(QT):
                    act.wait_ge(s["xn_turned"], b * QT + (i + 1))
                    nc.scalar.copy(xnT[0][:, :, i * P:(i + 1) * P], bank(4 + i % 2)[:, 0:DC * P].rearrange("p (c t) -> p c t", c=DC))\
                        .then_inc(s["xnT_hi"], 1)
                    if i + 2 < QT:
                        normal_rows(i + 2)
                    if i >= 1:
                        act.wait_ge(s["kv_done"], b * QT + i)
                        nc.scalar.copy(v[0][:, i - 1, :], bank(7 - i % 2)[:, DH:2 * DH]).then_inc(s["v_hi"], 1)
                    if i >= 2:
                        turned_keys(i - 2)
                act.wait_ge(s["kv_done"], b * QT + QT)
                nc.scalar.copy(v[0][:, QT - 1, :], bank(7)[:, DH:2 * DH]).then_inc(s["v_hi"], 1)
                turned_keys(QT - 2)
                turned_keys(QT - 1)

                def queries(u):
                    act.wait_ge(s["q_turned"], b * UNITS + (u + 1))
                    nc.scalar.copy(qT[u % 2][0][:, :, :], bank(6).rearrange("p (h t) -> p h t", h=HG)).then_inc(s["qT_hi"], 1)

                def turned_probs(u, j):
                    i, n = u // HG, u * HG + j
                    for g in range(group_count(i)):
                        m = min(4, i + 1 - 4 * g)
                        at = turned[n] + g
                        act.wait_ge(s["p_turned"], b * TURNED + (at + 1))
                        nc.scalar.copy(pT[0][:, 4 * g:4 * g + m, j, :],
                                       bank(4 + at % 2)[:, 0:m * P].rearrange("p (m t) -> p m t", m=m)).then_inc(s["pT_hi"], 1)

                def exponentials(u, j):
                    n = u * HG + j
                    k = n % RING
                    keys = (u // HG + 1) * P
                    act.wait_ge(s["max_ready"], b * NH + (n + 1))
                    if u == 2 * HG and j == 0:
                        act.wait_ge(s["out_split"], len(out_slots))
                    if n >= RING:
                        act.wait_ge(s["p_turned"], b * TURNED + turned[n - RING + 1])
                    nc.scalar.activation(probs[:, k, 0:keys], score(n)[:, 0:keys], ACT.Exp, bias=peak[:, k:k + 1],
                                         accum_out=total[:, k:k + 1]).then_inc(s["exp_done"], 1)

                def half_values(u, half):
                    act.wait_ge(s["o_done"], b * UNITS * HALVES + (u * HALVES + half + 1))
                    nc.scalar.copy(oT[0][:, heads_of(half), :], values_bank(half)).then_inc(s["oT_hi"], 1)

                queries(0)
                for u in range(UNITS + 1):
                    for step in STEPS:
                        if step[0] == "turn" and u:
                            turned_probs(u - 1, step[1])
                        if step[0] == "scores" and u < UNITS:
                            exponentials(u, step[1])
                        if step[0] == "turn_queries" and u + 1 < UNITS:
                            queries(u + 1)
                        if step[0] == "values" and u:
                            half_values(u - 1, step[1])
        @block.vector
        def _(dve):
            own = Chain(dve, s["dve_own"])
            link = own.link
            dve.sem_inc(s["x_ready"], 1)
            dve.sem_inc(s["pT_ready"], 1)
            for t in range(NT):
                ins = nc.vector.bn_aggr(mv[:, t, :], stats[:, t, :])
            link(ins)
            nc.vector.tensor_scalar(ve[:, :], mv[:, :, 1], LN_EPS, None, ALU.add).then_inc(s["ve_ready"], 1)
            dve.wait_ge(env["kv_in"], 16)
            link(nc.vector.tensor_copy(w_kv[0][:, :, :], env["raw_kv"]))
            nc.vector.tensor_tensor(w_kv[1][:, :, :], env["raw_kv"], w_kv[0][:, :, :].bitcast(F32), ALU.subtract).then_inc(s["kv_split"], 1)
            dve.wait_ge(s["rstd_ready"], 1)
            nc.vector.scalar_tensor_tensor(shift[:, :], mv[:, :, 0], -1.0, rstd[:, :], ALU.mult, ALU.mult).then_inc(s["shift_ready"], 1)
            with dve.Fori(0, BATCH) as b:
                def rows(i):
                    return x[:, one(b * QT + i), :].rearrange("p n d -> p (n d)")

                def low(out, src, high):
                    return nc.vector.tensor_tensor(out, src, high.bitcast(F32), ALU.subtract)

                def parts(src, a_cos, a_sin, i, heads, cos, scale):
                    shape = [P, heads, 2, HALF]
                    q = src.rearrange("p (h s d) -> p h s d", h=heads, s=2)
                    c = cos[:, i:i + 1, :].unsqueeze(1).to_broadcast(shape)
                    d = sin[:, i:i + 1, :].to_broadcast([P, heads, HALF])
                    nc.vector.tensor_tensor(a_cos.rearrange("p h (s d) -> p h s d", s=2), q, c, ALU.mult)
                    nc.vector.scalar_tensor_tensor(a_sin[:, :, 0:HALF], q[:, :, 1, :], -scale, d, ALU.mult, ALU.mult)
                    return nc.vector.scalar_tensor_tensor(a_sin[:, :, HALF:DH], q[:, :, 0, :], scale, d, ALU.mult, ALU.mult)

                def turned_input(i):
                    dve.wait_ge(s["xnT_hi"], b * QT + (i + 1))
                    at = slice(i * P, (i + 1) * P)
                    low(xnT[1][:, :, at], bank(4 + i % 2)[:, 0:DC * P].rearrange("p (c t) -> p c t", c=DC),
                        xnT[0][:, :, at]).then_inc(s["xnT_ready"], 1)

                def turned_keys(i):
                    dve.wait_ge(s["kT_hi"], b * QT + (i + 1))
                    at = slice(i * P, (i + 1) * P)
                    low(kT[1][:, at], bank(i % 2)[:, 0:P], kT[0][:, at]).then_inc(s["kT_ready"], 1)

                def key_value(i):
                    dve.wait_ge(s["kv_done"], b * QT + (i + 1))
                    kv = bank(6 + i % 2)
                    dve.wait_ge(s["v_hi"], b * QT + (i + 1))
                    low(v[1][:, i, :], kv[:, DH:2 * DH], v[0][:, i, :])
                    parts(kv[:, 0:DH], k_cos[:, :].unsqueeze(1), k_sin[:, :].unsqueeze(1), i, 1, cos, 1.0).then_inc(s["kv_read"], 1)
                    dve.wait_ge(s["kv_read"], b * QT + (i + 1))
                    if i >= 2:
                        dve.wait_ge(s["k_turned"], b * QT + (i - 1))
                    nc.vector.tensor_tensor(k_rot[i % 2][:, :], k_cos[:, :], k_sin[:, :], ALU.add).then_inc(s["k_rot_ready"], 1)
                    dve.wait_ge(s["k_rot_ready"], b * QT + (i + 1))

                for i in range(QT):
                    turned_input(i)
                    if i >= 1:
                        key_value(i - 1)
                    if i >= 2:
                        turned_keys(i - 2)
                key_value(QT - 1)
                turned_keys(QT - 2)
                turned_keys(QT - 1)

                def query_parts(u):
                    dve.wait_ge(s["q_done"], b * UNITS + (u + 1))
                    dve.wait_ge(s["q_rotated"], b * UNITS + (u + 1))
                    parts(bank(6), q_cos[:, :, :], q_sin[:, :, :], u // HG, HG, cos_scaled, SCALE).then_inc(s["q_parts"], 1)

                def queries(u):
                    dve.wait_ge(s["qT_hi"], b * UNITS + (u + 1))
                    low(qT[u % 2][1][:, :, :], bank(6).rearrange("p (h t) -> p h t", h=HG), qT[u % 2][0][:, :, :]).then_inc(s["qT_ready"], 1)

                def normal(n):
                    k = n % RING
                    dve.wait_ge(s["exp_done"], b * NH + (n + 1))
                    nc.vector.reciprocal(weight[:, k:k + 1], total[:, k:k + 1]).then_inc(s["weight_ready"], 1)

                def turned_probs(u, j):
                    i, n = u // HG, u * HG + j
                    for g in range(group_count(i)):
                        m = min(4, i + 1 - 4 * g)
                        at = turned[n] + g
                        dve.wait_ge(s["pT_hi"], b * TURNED + (at + 2))
                        low(pT[1][:, 4 * g:4 * g + m, j, :], bank(4 + at % 2)[:, 0:m * P].rearrange("p (m t) -> p m t", m=m),
                            pT[0][:, 4 * g:4 * g + m, j, :]).then_inc(s["pT_ready"], 1)

                def maximum(u, j):
                    n = u * HG + j
                    k = n % RING
                    dve.wait_ge(s["s_done"], b * NH + (n + 1))
                    nc.vector.reduce_max(peak[:, k:k + 1], score(n)[:, 0:(u // HG + 1) * P], axis=AX, negate=True).then_inc(s["max_ready"], 1)

                def add_to_x(u):
                    dve.wait_ge(s["a_done"], b * UNITS + (u + 1))
                    nc.vector.tensor_tensor(rows(u // HG), bank(7)[:, 0:D], rows(u // HG), ALU.add).then_inc(s["x_ready"], 1)
                    dve.wait_ge(s["x_ready"], b * UNITS + (u + 2))
                    if u % HG == HG - 1:
                        nc.vector.bn_stats(stats[:, one(b * QT + u // HG), :].rearrange("p n d -> p (n d)"), rows(u // HG))

                def half_values(u, half):
                    dve.wait_ge(s["oT_hi"], b * UNITS * HALVES + (u * HALVES + half + 1))
                    low(oT[1][:, heads_of(half), :], values_bank(half), oT[0][:, heads_of(half), :]).then_inc(s["oT_ready"], 1)

                query_parts(0)
                queries(0)
                for u in range(UNITS + 1):
                    for step in STEPS:
                        if step[0] == "turn" and u:
                            turned_probs(u - 1, step[1])
                        if step[0] == "project" and u >= 2:
                            add_to_x(u - 2)
                        if step[0] == "scores" and u < UNITS:
                            maximum(u, step[1])
                        if step[0] == "scores" and 0 < u * HG + step[1] <= NH:
                            normal(u * HG + step[1] - 1)
                        if step == ("scores", 0) and u + 1 < UNITS:
                            query_parts(u + 1)
                        if step[0] == "turn_queries" and u + 1 < UNITS:
                            queries(u + 1)
                        if step[0] == "values" and u:
                            half_values(u - 1, step[1])
                add_to_x(UNITS - 1)

        @block.tensor
        def _(pe):
            with pe.Fori(0, BATCH) as b:
                pe.wait_ge(s["kv_split"], 1)
                pe.wait_ge(s["pT_ready"], b * TURNED + 1)
                pe.wait_ge(s["x_ready"], b * UNITS + 1)

                def key_value(i):
                    pe.wait_ge(s["xnT_ready"], b * QT + (i + 1))
                    if i >= 2:
                        pe.wait_ge(s["kv_read"], b * QT + (i - 1))
                    at = slice(i * P, (i + 1) * P)
                    for c in range(DC):
                        ins = split_matmul(nc, bank(6 + i % 2)[:, 0:2 * DH], (xnT[0][:, c, at], xnT[1][:, c, at]),
                                           (w_kv[0][:, c, :], w_kv[1][:, c, :]), c == 0, c == DC - 1)
                    ins.then_inc(s["kv_done"], 1)

                def turn_keys(i):
                    pe.wait_ge(s["k_rot_ready"], b * QT + (i + 1))
                    if i >= 2:
                        pe.wait_ge(s["kT_ready"], b * QT + (i - 1))
                    nc.tensor.transpose(bank(i % 2)[:, 0:P], k_rot[i % 2][:, :], ident).then_inc(s["k_turned"], 1)

                for i in range(QT):
                    pe.wait_ge(s["xn_ready"], b * QT + (i + 1))
                    if i >= 2:
                        pe.wait_ge(s["xnT_ready"], b * QT + (i - 1))
                    for c in range(DC):
                        ins = nc.tensor.transpose(bank(4 + i % 2)[:, c * P:(c + 1) * P], xn[i % 2][:, c * P:(c + 1) * P], ident)
                    ins.then_inc(s["xn_turned"], 1)
                    if i >= 1:
                        key_value(i - 1)
                    if i >= 2:
                        turn_keys(i - 2)
                key_value(QT - 1)
                turn_keys(QT - 2)
                turn_keys(QT - 1)

                def project_queries(u):
                    i, g = u // HG, u % HG
                    if u:
                        pe.wait_ge(s["qT_ready"], b * UNITS + u)
                    else:
                        pe.wait_ge(s["kv_read"], b * QT + QT)
                    at, heads = slice(i * P, (i + 1) * P), slice(g * HG * DH, (g + 1) * HG * DH)
                    for c in range(DC):
                        ins = split_matmul(nc, bank(6), (xnT[0][:, c, at], xnT[1][:, c, at]),
                                           (w_q[0][:, c, heads], w_q[1][:, c, heads]), c == 0, c == DC - 1)
                    ins.then_inc(s["q_done"], 1)

                def turn_queries(u):
                    pe.wait_ge(s["q_rotated"], b * UNITS + (u + 2))
                    for j in range(HG):
                        ins = nc.tensor.transpose(bank(6)[:, j * P:(j + 1) * P], q_rot[:, j, :], ident)
                    ins.then_inc(s["q_turned"], 1)

                def scores(u, j):
                    i, n = u // HG, u * HG + j
                    if j == 0:
                        pe.wait_ge(s["qT_ready"], b * UNITS + (u + 1))
                    if n == 0:
                        pe.wait_ge(s["kT_ready"], b * QT + QT)
                    if n >= scores_held(n):
                        pe.wait_ge(s["exp_done"], b * NH + (n - scores_held(n) + 1))
                    keys = (i + 1) * P
                    for at in range(0, keys, 512):
                        end = max(min(keys, at + 512), at + 256)
                        split_matmul(nc, score(n)[:, at:end], (qT[u % 2][0][:, j, :], qT[u % 2][1][:, j, :]),
                                     (kT[0][:, at:end], kT[1][:, at:end]), True, end < keys)
                    nc.tensor.matmul(score(n)[:, i * P:keys], ident_b, mask_b, start=False, stop=True).then_inc(s["s_done"], 1)

                def turn_probs(u, j):
                    i, n = u // HG, u * HG + j
                    pe.wait_ge(s["probs_ready"], b * NH + (n + 1))
                    for g in range(group_count(i)):
                        at = turned[n] + g
                        if at >= 2:
                            pe.wait_ge(s["pT_ready"], b * TURNED + at)
                        for m in range(4 * g, min(4 * g + 4, i + 1)):
                            ins = nc.tensor.transpose(bank(4 + at % 2)[:, (m - 4 * g) * P:(m - 4 * g + 1) * P],
                                                      probs[:, n % RING, m * P:(m + 1) * P], ident)
                        ins.then_inc(s["p_turned"], 1)

                def values(u, half):
                    i = u // HG
                    pe.wait_ge(s["pT_ready"], b * TURNED + (turned[u * HG + heads_of(half).stop] + 1))
                    if half:
                        pe.wait_ge(s["oT_ready"], b * UNITS * HALVES + (u * HALVES + half))
                    elif u:
                        pe.wait_ge(s["x_ready"], b * UNITS + (u + 1))
                    for m in range(i + 1):
                        ins = split_matmul(nc, values_bank(half), (v[0][:, m, :], v[1][:, m, :]),
                                           (pT[0][:, m, heads_of(half), :], pT[1][:, m, heads_of(half), :]), m == 0, m == i)
                    ins.then_inc(s["o_done"], 1)

                def project(u):
                    pe.wait_ge(s["oT_ready"], b * UNITS * HALVES + (u + 1) * HALVES)
                    if u == 0:
                        pe.wait_ge(s["out_split"], len(out_slots))
                    for j in range(HG):
                        hd = u % HG * HG + j
                        ins = split_matmul(nc, bank(7)[:, 0:D], (oT[0][:, j, :], oT[1][:, j, :]),
                                           (w_out[0][:, hd, :], w_out[1][:, hd, :]), j == 0, j == HG - 1)
                    ins.then_inc(s["a_done"], 1)

                pe.wait_ge(s["w_lo"], DC)
                project_queries(0)
                turn_queries(0)
                for u in range(UNITS + 1):
                    for step in STEPS:
                        if step[0] == "turn" and u:
                            turn_probs(u - 1, step[1])
                        if step[0] == "scores" and u < UNITS:
                            scores(u, step[1])
                        if step[0] == "project_queries" and u + 1 < UNITS:
                            project_queries(u + 1)
                        if step[0] == "project" and u >= 2:
                            project(u - 2)
                        if step[0] == "turn_queries" and u + 1 < UNITS:
                            turn_queries(u + 1)
                        if step[0] == "values" and u:
                            values(u - 1, step[1])
                project(UNITS - 1)


def load_all(sp, env):
    dram = env["dram"]
    rows = dram["x"].rearrange("(n t p) d -> n p t d", p=P, t=BLK)
    for blk in range(NB):
        sp.dma_start(env["x"][:, blk * BLK:(blk + 1) * BLK, :], rows[blk]).then_inc(env["x_in"][blk], 16)
    for dst, src in (
        (env["const"][:, :], dram["const"]),
        (env["w_norm"][:, :], dram["w_norm"].rearrange("(o d) -> o d", o=1).to_broadcast([P, D])),
        (env["w_route"][:, :, 0:E], dram["w_router"].rearrange("(c p) e -> p c e", p=P)),
        (env["w_route"][:, :, E:E + 1], dram["w_shared_gate"].rearrange("(c p) e -> p c e", p=P)),
    ):
        sp.dma_start(dst, src, allow_slow_non_contiguous=True).then_inc(env["w_in"], 16)


def make_tables(nc, pool, env):
    nc.gpsimd.memset(env["ones_b"], 1.0).then_inc(env["tables_ready"], 1)
    pool.wait_ge(env["w_in"], 16 * W_LOADS)
    for dst, src in (("before_b", "before"), ("ident_b", "ident"), ("mask_b", "mask")):
        at, n = CONST[src]
        nc.gpsimd.tensor_copy(env[dst], env["const"][:, at:at + n]).then_inc(env["tables_ready"], 1)


def macaron(nc, dram):
    with ExitStack() as ctx:
        def sb(name, shape, dt=F32):
            return ctx.enter_context(nc.sbuf_tensor(name, shape, dt))

        const = sb("const", [P, CONST_COLS])
        ps = ctx.enter_context(nc.psum_tensor("ps", [P, 8 * 512], F32))
        env = {
            "dram": dram,
            "x": sb("x", [P, NT, D]),
            "const": const,
            "bank": lambda k: ps[:, k * 512:(k + 1) * 512],
            "bank2": lambda k: ps[:, k * 512:(k + 2) * 512],
            "ident": const[:, 0:P],
            "stats": sb("stats", [P, NT, 6]),
            "place": sb("place", [P, RING * SEQ]),
            "w_norm": sb("w_norm", [P, D]),
            "w_route": sb("w_route", [P, DC, E + 1]),
            "xr_dram": nc.dram_tensor("xr_rows", [NT * P, D], F32, kind="Internal").ap(),
            "y_dram": nc.dram_tensor("expert_rows", [E * CAP, D], F32, kind="Internal").ap(),
            "x_in": [ctx.enter_context(nc.semaphore(f"x_in{k}")) for k in range(NB)],
        }
        for n in ("w_in", "tables_ready", "kv_in", "q_in"):
            env[n] = ctx.enter_context(nc.semaphore(n))
        env["raw_q"] = env["place"][:, 0:DC * HEADS * DH].rearrange("p (c f) -> p c f", c=DC)
        env["raw_kv"] = env["place"][:, DC * HEADS * DH:DC * (HEADS + 2) * DH].rearrange("p (c f) -> p c f", c=DC)
        for n in ("ones_b", "before_b", "ident_b", "mask_b"):
            env[n] = sb(n, [P, P], BF16)[:, :]
        nc.clear_and_free_semaphores(ffn(nc, 0, env))
        nc.all_engine_barrier()
        attention(nc, env)
        ffn(nc, 1, env)


INPUTS = ("attn_x", "attn_Wq", "attn_Wkv", "attn_Wout", "ffn_w_norm", "ffn_w_router", "ffn_w_gate", "ffn_w_up",
          "ffn_w_down", "ffn_sw_gate", "ffn_sw_up", "ffn_sw_down", "ffn_w_shared_gate")


def kernel(**inputs):
    import concourse.bacc as bacc
    from concourse.bass_utils import run_bass_kernel_spmd

    nc = bacc.Bacc("TRN2", target_bir_lowering=False, num_devices=1)
    arrays = {f"in_{n}": np.ascontiguousarray(inputs[f"L0_{n}"]) for n in INPUTS}
    arrays["in_attn_x"] = arrays["in_attn_x"].reshape(BATCH * SEQ, D)
    arrays["in_all_const"] = constants()
    dram = {}
    for name, a in arrays.items():
        dram[name.split("_", 2)[-1]] = nc.dram_tensor(name, a.shape, mybir.dt.from_np(a.dtype), kind="ExternalInput").ap()
    dram["out"] = nc.dram_tensor("out", (BATCH * SEQ, D), F32, kind="ExternalOutput").ap()
    macaron(nc, dram)
    r = run_bass_kernel_spmd(nc, [arrays], core_ids=[0])
    return r.results[0]["out"].reshape(BATCH, SEQ, D)
```
